# Optimizing a Trainium2 kernel written in Bass

```python
import numpy as np
import jax
import jax.numpy as jnp

def _softmax(x, axis=-1):
    return jax.nn.softmax(x, axis=axis)

def _gelu(x):
    return jax.nn.gelu(x, approximate=True)

def _silu(x):
    return jax.nn.silu(x)

def _sigmoid(x):
    return jax.nn.sigmoid(x)

def _layernorm(x, axis=-1, eps=1e-05):
    m = jnp.mean(x, axis=axis, keepdims=True)
    v = jnp.var(x, axis=axis, keepdims=True)
    return (x - m) / jnp.sqrt(v + eps)

def _scatter_add(tgt, idx, src, axis=0):
    return tgt.at[idx].add(src)

def _segment_sum(src, seg, n):
    return jax.ops.segment_sum(src, seg, n)
kernel_name = 'mk_perceiver_d2_seqx_r4_350da2'

def setup_inputs(seed: int=0):
    np.random.seed(seed)
    _w = jnp.asarray

    def _rec_inputs():
        import jax
        import jax.numpy as jnp
        _rk = jax.random.key(seed)
        x = 7.22e-05 + 1 * jax.random.normal(jax.random.fold_in(_rk, 1), (16, 64, 256), jnp.float32)
        _lenS = 64 - jax.random.randint(jax.random.fold_in(_rk, 7), (16,), 0, max(1, 64 // 4) + 1, jnp.int32)
        _lenS2 = 1601 - jax.random.randint(jax.random.fold_in(_rk, 8), (16,), 0, max(1, 1601 // 4) + 1, jnp.int32)
        _ctx_1024P = jax.random.normal(jax.random.fold_in(_rk, 11), (16, 16, 256), jnp.float32)
        _ctx_1024c = jax.random.dirichlet(jax.random.fold_in(_rk, 511), 0.3 * jnp.ones((16,), jnp.float32), (16, 1601))
        _ctx_1024t = jnp.einsum('bsk,bkd->bsd', _ctx_1024c, _ctx_1024P)
        _ctx_1024t = _ctx_1024t * jax.lax.rsqrt(jnp.mean(jnp.square(_ctx_1024t)) + 1e-12) * 0.953939
        ctx_1024 = 4.13588e-05 + 0.999923 * (_ctx_1024t + 0.3 * jax.random.normal(jax.random.fold_in(_rk, 611), (16, 1601, 256), jnp.float32))
        return (x, ctx_1024)
    x, ctx_1024 = _rec_inputs()

    def _L0_xattn_setup():
        import jax, jax.numpy as jnp
        import numpy as np
        B, S, H, NH = (4, 512, 256, 16)
        D = H // NH
        SCALE = float(D) ** 0.5
        key = jax.random.key(seed)
        ks = jax.random.split(key, 11)
        std = 1.0 / np.sqrt(H)
        return {'q': jax.random.normal(ks[0], (B, S, H), jnp.float32), 'k': jax.random.normal(ks[1], (B, S, H), jnp.float32), 'v': jax.random.normal(ks[2], (B, S, H), jnp.float32), 'wq': jax.random.normal(ks[3], (H, H), jnp.float32) * std, 'bq': jax.random.normal(ks[4], (H,), jnp.float32) * std, 'wk': jax.random.normal(ks[5], (H, H), jnp.float32) * std, 'bk': jax.random.normal(ks[6], (H,), jnp.float32) * std, 'wv': jax.random.normal(ks[7], (H, H), jnp.float32) * std, 'bv': jax.random.normal(ks[8], (H,), jnp.float32) * std, 'wo': jax.random.normal(ks[9], (H, H), jnp.float32) * std, 'bo': jax.random.normal(ks[10], (H,), jnp.float32) * std}
    _L0_xattn_all = _L0_xattn_setup()
    _L0_xattn_in = {k: v for k, v in _L0_xattn_all.items() if k in ('wq', 'bq', 'wk', 'bk', 'wv', 'bv', 'wo', 'bo')}
    del _L0_xattn_all

    def _L0_attn_setup():
        import jax, jax.numpy as jnp
        import numpy as np
        HEADS = 8
        DIM_HEAD = 128
        ATTN_MATRIX_SCALE = 1.5
        SCALE = DIM_HEAD ** (-0.5)

        def _split_heads(t):
            b, n, _ = t.shape
            t = t.reshape(b, n, HEADS, DIM_HEAD)
            return t.transpose(2, 0, 1, 3).reshape(HEADS, b * n, DIM_HEAD)
        key = jax.random.key(seed)
        ks = jax.random.split(key, 7)
        b, n, m = (2, 512, 512)
        qd, cd, inner = (256, 192, HEADS * DIM_HEAD)
        x = jax.random.normal(ks[0], (b, n, qd), dtype=jnp.float32)
        context = jax.random.normal(ks[1], (b, m, cd), dtype=jnp.float32)
        Wq = jax.random.normal(ks[2], (qd, inner), dtype=jnp.float32) * qd ** (-0.5)
        Wk = jax.random.normal(ks[3], (cd, inner), dtype=jnp.float32) * cd ** (-0.5)
        Wv = jax.random.normal(ks[4], (cd, inner), dtype=jnp.float32) * cd ** (-0.5)
        Wout = jax.random.normal(ks[5], (inner, qd), dtype=jnp.float32) * inner ** (-0.5)
        bout = jnp.zeros((qd,), dtype=jnp.float32)
        return {'x': x, 'context': context, 'Wq': Wq, 'Wk': Wk, 'Wv': Wv, 'Wout': Wout, 'bout': bout}
    _L0_attn_all = _L0_attn_setup()
    _L0_attn_in = {k: v for k, v in _L0_attn_all.items() if k in ('context', 'Wq', 'Wk', 'Wv', 'Wout', 'bout')}
    del _L0_attn_all

    def _L0_ffn_setup():
        import jax, jax.numpy as jnp
        import numpy as np
        B, S, H, F, E = (8, 512, 256, 1024, 8)
        INIT_LAMBDA = 0.2
        key = jax.random.key(seed)
        ks = jax.random.split(key, 12)
        std = 0.02
        return {'hidden_states': jax.random.normal(ks[0], (B, S, H), jnp.float32), 'gate_w1': jax.random.normal(ks[1], (H, H), jnp.float32) * 0.01, 'gate_b1': jnp.zeros((H,), jnp.float32), 'gate_w2': jax.random.normal(ks[2], (E, H), jnp.float32) * 0.01, 'gate_b2': jnp.full((E,), INIT_LAMBDA, jnp.float32), 'W1': jax.random.normal(ks[3], (F, H), jnp.float32) * std, 'b1': jax.random.normal(ks[4], (F,), jnp.float32) * std, 'W2': jax.random.normal(ks[5], (H, F), jnp.float32) * std, 'b2': jax.random.normal(ks[6], (H,), jnp.float32) * std, 'TW1': jax.random.normal(ks[7], (E, F, H), jnp.float32) * std, 'Tb1': jax.random.normal(ks[8], (E, F), jnp.float32) * std, 'TW2': jax.random.normal(ks[9], (E, H, F), jnp.float32) * std, 'Tb2': jax.random.normal(ks[10], (E, H), jnp.float32) * std}
    _L0_ffn_all = _L0_ffn_setup()
    _L0_ffn_in = {k: v for k, v in _L0_ffn_all.items() if k in ('gate_w1', 'gate_b1', 'gate_w2', 'gate_b2', 'W1', 'b1', 'W2', 'b2', 'TW1', 'Tb1', 'TW2', 'Tb2')}
    del _L0_ffn_all

    def _L1_xattn_setup():
        import jax, jax.numpy as jnp
        import numpy as np
        N_HEADS = 16
        key = jax.random.key(seed)
        ks = jax.random.split(key, 8)
        B, S, D = (2, 512, 256)
        dk = D // N_HEADS
        s = lambda fan_in: 1.0 / np.sqrt(fan_in)
        return {'q': jax.random.normal(ks[0], (B, S, D), jnp.float32), 'k': jax.random.normal(ks[1], (B, S, D), jnp.float32), 'v': jax.random.normal(ks[2], (B, S, D), jnp.float32), 'Wq': jax.random.normal(ks[3], (D, D), jnp.float32) * s(D), 'bq': jnp.zeros((D,), jnp.float32), 'Wk': jax.random.normal(ks[4], (dk, D), jnp.float32) * s(D), 'bk': jnp.zeros((dk,), jnp.float32), 'Wv': jax.random.normal(ks[5], (dk, D), jnp.float32) * s(D), 'bv': jnp.zeros((dk,), jnp.float32), 'Wo': jax.random.normal(ks[6], (D, D), jnp.float32) * s(D), 'bo': jnp.zeros((D,), jnp.float32)}
    _L1_xattn_all = _L1_xattn_setup()
    _L1_xattn_in = {k: v for k, v in _L1_xattn_all.items() if k in ('Wq', 'bq', 'Wk', 'bk', 'Wv', 'bv', 'Wo', 'bo')}
    del _L1_xattn_all

    def _L1_attn_setup():
        import jax, jax.numpy as jnp
        import numpy as np
        import math
        B, S, HID, H = (2, 512, 256, 16)
        D = HID // H

        def _get_slopes(n):
            start = 2 ** (-2 ** (-(math.log2(n) - 3)))
            return np.array([start * 2 ** (-i) for i in range(n)], dtype=np.float32)
        key = jax.random.key(seed)
        ks = jax.random.split(key, 9)
        sc = 1.0 / math.sqrt(HID)
        return {'x': jax.random.normal(ks[0], (B, S, HID), dtype=jnp.float32), 'Wq': jax.random.normal(ks[1], (HID, HID), dtype=jnp.float32) * sc, 'bq': jnp.zeros((HID,), dtype=jnp.float32), 'Wk': jax.random.normal(ks[2], (HID, HID), dtype=jnp.float32) * sc, 'bk': jnp.zeros((HID,), dtype=jnp.float32), 'Wv': jax.random.normal(ks[3], (HID, HID), dtype=jnp.float32) * sc, 'bv': jnp.zeros((HID,), dtype=jnp.float32), 'Wo': jax.random.normal(ks[4], (HID, HID), dtype=jnp.float32) * sc, 'bo': jnp.zeros((HID,), dtype=jnp.float32), 'slopes': jnp.asarray(_get_slopes(H))}
    _L1_attn_all = _L1_attn_setup()
    _L1_attn_in = {k: v for k, v in _L1_attn_all.items() if k in ('Wq', 'bq', 'Wk', 'bk', 'Wv', 'bv', 'Wo', 'bo', 'slopes')}
    del _L1_attn_all

    def _L1_ffn_setup():
        import jax, jax.numpy as jnp
        import numpy as np
        B, S, D = (2, 512, 256)
        H, HKV = (16, 4)
        HD = D // H
        F, E, K = (512, 8, 2)
        THETA = 10000.0
        EPS = 1e-05

        def _rmsnorm(x, w):
            return x * jax.lax.rsqrt(jnp.mean(x * x, axis=-1, keepdims=True) + EPS) * w

        def _rope_cos_sin(seq_len, head_dim, theta):
            inv_freq = 1.0 / theta ** (jnp.arange(0, head_dim, 2, dtype=jnp.float32) / head_dim)
            freqs = jnp.arange(seq_len, dtype=jnp.float32)[:, None] * inv_freq
            return (jnp.cos(freqs), jnp.sin(freqs))

        def _apply_rope(x, cos, sin):
            x1, x2 = jnp.split(x, 2, axis=-1)
            c = cos[None, :, None, :]
            s = sin[None, :, None, :]
            return jnp.concatenate([x1 * c - x2 * s, x2 * c + x1 * s], axis=-1)
        key = jax.random.key(seed)
        ks = jax.random.split(key, 12)
        s = 0.02
        return {'hidden_states': jax.random.normal(ks[0], (B, S, D), jnp.float32), 'ln1_w': 1.0 + 0.1 * jax.random.normal(ks[1], (D,), jnp.float32), 'ln2_w': 1.0 + 0.1 * jax.random.normal(ks[2], (D,), jnp.float32), 'Wq': s * jax.random.normal(ks[3], (D, H * HD), jnp.float32), 'Wk': s * jax.random.normal(ks[4], (D, HKV * HD), jnp.float32), 'Wv': s * jax.random.normal(ks[5], (D, HKV * HD), jnp.float32), 'Wo': s * jax.random.normal(ks[6], (H * HD, D), jnp.float32), 'Wr': s * jax.random.normal(ks[7], (D, E), jnp.float32), 'Wg': s * jax.random.normal(ks[8], (E, D, F), jnp.float32), 'Wu': s * jax.random.normal(ks[9], (E, D, F), jnp.float32), 'Wd': s * jax.random.normal(ks[10], (E, F, D), jnp.float32)}
    _L1_ffn_all = _L1_ffn_setup()
    _L1_ffn_in = {k: v for k, v in _L1_ffn_all.items() if k in ('ln1_w', 'ln2_w', 'Wq', 'Wk', 'Wv', 'Wo', 'Wr', 'Wg', 'Wu', 'Wd')}
    del _L1_ffn_all
    return {'x': x, 'ctx_1024': ctx_1024, 'L0_xattn_wq': _L0_xattn_in['wq'], 'L0_xattn_bq': _L0_xattn_in['bq'], 'L0_xattn_wk': _L0_xattn_in['wk'], 'L0_xattn_bk': _L0_xattn_in['bk'], 'L0_xattn_wv': _L0_xattn_in['wv'], 'L0_xattn_bv': _L0_xattn_in['bv'], 'L0_xattn_wo': _L0_xattn_in['wo'], 'L0_xattn_bo': _L0_xattn_in['bo'], 'L0_attn_context': _L0_attn_in['context'], 'L0_attn_Wq': _L0_attn_in['Wq'], 'L0_attn_Wk': _L0_attn_in['Wk'], 'L0_attn_Wv': _L0_attn_in['Wv'], 'L0_attn_Wout': _L0_attn_in['Wout'], 'L0_attn_bout': _L0_attn_in['bout'], 'L0_ffn_gate_w1': _L0_ffn_in['gate_w1'], 'L0_ffn_gate_b1': _L0_ffn_in['gate_b1'], 'L0_ffn_gate_w2': _L0_ffn_in['gate_w2'], 'L0_ffn_gate_b2': _L0_ffn_in['gate_b2'], 'L0_ffn_W1': _L0_ffn_in['W1'], 'L0_ffn_b1': _L0_ffn_in['b1'], 'L0_ffn_W2': _L0_ffn_in['W2'], 'L0_ffn_b2': _L0_ffn_in['b2'], 'L0_ffn_TW1': _L0_ffn_in['TW1'], 'L0_ffn_Tb1': _L0_ffn_in['Tb1'], 'L0_ffn_TW2': _L0_ffn_in['TW2'], 'L0_ffn_Tb2': _L0_ffn_in['Tb2'], 'L1_xattn_Wq': _L1_xattn_in['Wq'], 'L1_xattn_bq': _L1_xattn_in['bq'], 'L1_xattn_Wk': _L1_xattn_in['Wk'], 'L1_xattn_bk': _L1_xattn_in['bk'], 'L1_xattn_Wv': _L1_xattn_in['Wv'], 'L1_xattn_bv': _L1_xattn_in['bv'], 'L1_xattn_Wo': _L1_xattn_in['Wo'], 'L1_xattn_bo': _L1_xattn_in['bo'], 'L1_attn_Wq': _L1_attn_in['Wq'], 'L1_attn_bq': _L1_attn_in['bq'], 'L1_attn_Wk': _L1_attn_in['Wk'], 'L1_attn_bk': _L1_attn_in['bk'], 'L1_attn_Wv': _L1_attn_in['Wv'], 'L1_attn_bv': _L1_attn_in['bv'], 'L1_attn_Wo': _L1_attn_in['Wo'], 'L1_attn_bo': _L1_attn_in['bo'], 'L1_attn_slopes': _L1_attn_in['slopes'], 'L1_ffn_ln1_w': _L1_ffn_in['ln1_w'], 'L1_ffn_ln2_w': _L1_ffn_in['ln2_w'], 'L1_ffn_Wq': _L1_ffn_in['Wq'], 'L1_ffn_Wk': _L1_ffn_in['Wk'], 'L1_ffn_Wv': _L1_ffn_in['Wv'], 'L1_ffn_Wo': _L1_ffn_in['Wo'], 'L1_ffn_Wr': _L1_ffn_in['Wr'], 'L1_ffn_Wg': _L1_ffn_in['Wg'], 'L1_ffn_Wu': _L1_ffn_in['Wu'], 'L1_ffn_Wd': _L1_ffn_in['Wd']}

def reference(x, ctx_1024, L0_xattn_wq, L0_xattn_bq, L0_xattn_wk, L0_xattn_bk, L0_xattn_wv, L0_xattn_bv, L0_xattn_wo, L0_xattn_bo, L0_attn_context, L0_attn_Wq, L0_attn_Wk, L0_attn_Wv, L0_attn_Wout, L0_attn_bout, L0_ffn_gate_w1, L0_ffn_gate_b1, L0_ffn_gate_w2, L0_ffn_gate_b2, L0_ffn_W1, L0_ffn_b1, L0_ffn_W2, L0_ffn_b2, L0_ffn_TW1, L0_ffn_Tb1, L0_ffn_TW2, L0_ffn_Tb2, L1_xattn_Wq, L1_xattn_bq, L1_xattn_Wk, L1_xattn_bk, L1_xattn_Wv, L1_xattn_bv, L1_xattn_Wo, L1_xattn_bo, L1_attn_Wq, L1_attn_bq, L1_attn_Wk, L1_attn_bk, L1_attn_Wv, L1_attn_bv, L1_attn_Wo, L1_attn_bo, L1_attn_slopes, L1_ffn_ln1_w, L1_ffn_ln2_w, L1_ffn_Wq, L1_ffn_Wk, L1_ffn_Wv, L1_ffn_Wo, L1_ffn_Wr, L1_ffn_Wg, L1_ffn_Wu, L1_ffn_Wd):
    import jax
    import jax.numpy as jnp

    def _L0_xattn_ref(q, k, v, wq, bq, wk, bk, wv, bv, wo, bo):
        import jax, jax.numpy as jnp
        import numpy as np
        B, S, H, NH = (4, 512, 256, 16)
        D = H // NH
        SCALE = float(D) ** 0.5
        b = q.shape[0]
        qh = (q @ wq + bq).reshape(b, -1, NH, D).transpose(0, 2, 1, 3)
        kh = (k @ wk + bk).reshape(b, -1, NH, D).transpose(0, 2, 1, 3)
        vh = (v @ wv + bv).reshape(b, -1, NH, D).transpose(0, 2, 1, 3)
        attn = jnp.einsum('bhqd,bhkd->bhqk', qh, kh) / SCALE
        score = jax.nn.softmax(attn, axis=-1)
        out = jnp.einsum('bhqk,bhkd->bhqd', score, vh)
        out = out.transpose(0, 2, 1, 3).reshape(b, -1, NH * D)
        return out @ wo + bo

    def _L0_attn_ref(x, context, Wq, Wk, Wv, Wout, bout):
        import jax, jax.numpy as jnp
        import numpy as np
        HEADS = 8
        DIM_HEAD = 128
        ATTN_MATRIX_SCALE = 1.5
        SCALE = DIM_HEAD ** (-0.5)

        def _split_heads(t):
            b, n, _ = t.shape
            t = t.reshape(b, n, HEADS, DIM_HEAD)
            return t.transpose(2, 0, 1, 3).reshape(HEADS, b * n, DIM_HEAD)
        b, n, _ = x.shape
        qh = _split_heads(jnp.einsum('bnq,qi->bni', x, Wq))
        kh = _split_heads(jnp.einsum('bmc,ci->bmi', context, Wk))
        vh = _split_heads(jnp.einsum('bmc,ci->bmi', context, Wv))
        sim = jnp.einsum('hid,hjd->hij', qh, kh) * SCALE
        mean = jnp.mean(sim, axis=-1, keepdims=True)
        sim = (sim - mean) * ATTN_MATRIX_SCALE + mean
        attn = jax.nn.softmax(sim, axis=-1)
        out = jnp.einsum('hij,hjd->hid', attn, vh)
        out = out.reshape(HEADS, b, n, DIM_HEAD).transpose(1, 2, 0, 3)
        out = out.reshape(b, n, HEADS * DIM_HEAD)
        return jnp.einsum('bni,iq->bnq', out, Wout) + bout

    def _L0_ffn_ref(hidden_states, gate_w1, gate_b1, gate_w2, gate_b2, W1, b1, W2, b2, TW1, Tb1, TW2, Tb2):
        import jax, jax.numpy as jnp
        import numpy as np
        B, S, H, F, E = (8, 512, 256, 1024, 8)
        INIT_LAMBDA = 0.2
        x = hidden_states
        h = jax.nn.relu(jnp.einsum('bsh,oh->bso', x, gate_w1) + gate_b1)
        g = jnp.einsum('bso,eo->bse', h, gate_w2) + gate_b2
        g = g.mean(axis=1)
        mW1 = W1 + jnp.einsum('be,efh->bfh', g, TW1)
        mb1 = b1 + g @ Tb1
        mW2 = W2 + jnp.einsum('be,ehf->bhf', g, TW2)
        mb2 = b2 + g @ Tb2
        u = jax.nn.gelu(jnp.einsum('bsh,bfh->bsf', x, mW1) + mb1[:, None, :])
        out = jnp.einsum('bsf,bhf->bsh', u, mW2) + mb2[:, None, :]
        return out

    def _L1_xattn_ref(q, k, v, Wq, bq, Wk, bk, Wv, bv, Wo, bo):
        import jax, jax.numpy as jnp
        import numpy as np
        N_HEADS = 16
        B, S, D = q.shape
        H = N_HEADS
        dk = D // H
        scale = dk ** (-0.5)
        qh = (q @ Wq.T + bq).reshape(B, S, H, dk).transpose(0, 2, 1, 3)
        kh = k @ Wk.T + bk
        vh = v @ Wv.T + bv
        scores = jnp.einsum('bhqd,bkd->bhqk', qh, kh) * scale
        weights = jax.nn.softmax(scores, axis=-1)
        ctx = jnp.einsum('bhqk,bkd->bhqd', weights, vh)
        ctx = ctx.transpose(0, 2, 1, 3).reshape(B, S, D)
        return ctx @ Wo.T + bo

    def _L1_attn_ref(x, Wq, bq, Wk, bk, Wv, bv, Wo, bo, slopes):
        import jax, jax.numpy as jnp
        import numpy as np
        import math
        B, S, HID, H = (2, 512, 256, 16)
        D = HID // H

        def _get_slopes(n):
            start = 2 ** (-2 ** (-(math.log2(n) - 3)))
            return np.array([start * 2 ** (-i) for i in range(n)], dtype=np.float32)
        b, s, hid = x.shape
        h = slopes.shape[0]
        d = hid // h
        q = (x @ Wq.T + bq).reshape(b, s, h, d).transpose(0, 2, 1, 3)
        k = (x @ Wk.T + bk).reshape(b, s, h, d).transpose(0, 2, 1, 3)
        v = (x @ Wv.T + bv).reshape(b, s, h, d).transpose(0, 2, 1, 3)
        scores = jnp.einsum('bhqd,bhkd->bhqk', q, k) / jnp.sqrt(jnp.float32(d))
        pos = jnp.arange(s)
        dist = (pos[None, :] - pos[:, None]).astype(x.dtype)
        scores = scores + slopes[None, :, None, None] * dist[None, None]
        attn = jax.nn.softmax(scores, axis=-1)
        ctx = jnp.einsum('bhqk,bhkd->bhqd', attn, v)
        ctx = ctx.transpose(0, 2, 1, 3).reshape(b, s, hid)
        return ctx @ Wo.T + bo

    def _L1_ffn_ref(hidden_states, ln1_w, ln2_w, Wq, Wk, Wv, Wo, Wr, Wg, Wu, Wd):
        import jax, jax.numpy as jnp
        import numpy as np
        B, S, D = (2, 512, 256)
        H, HKV = (16, 4)
        HD = D // H
        F, E, K = (512, 8, 2)
        THETA = 10000.0
        EPS = 1e-05

        def _rmsnorm(x, w):
            return x * jax.lax.rsqrt(jnp.mean(x * x, axis=-1, keepdims=True) + EPS) * w

        def _rope_cos_sin(seq_len, head_dim, theta):
            inv_freq = 1.0 / theta ** (jnp.arange(0, head_dim, 2, dtype=jnp.float32) / head_dim)
            freqs = jnp.arange(seq_len, dtype=jnp.float32)[:, None] * inv_freq
            return (jnp.cos(freqs), jnp.sin(freqs))

        def _apply_rope(x, cos, sin):
            x1, x2 = jnp.split(x, 2, axis=-1)
            c = cos[None, :, None, :]
            s = sin[None, :, None, :]
            return jnp.concatenate([x1 * c - x2 * s, x2 * c + x1 * s], axis=-1)
        b, s, d = hidden_states.shape
        residual = hidden_states
        h = _rmsnorm(hidden_states, ln1_w)
        q = (h @ Wq).reshape(b, s, H, HD)
        k = (h @ Wk).reshape(b, s, HKV, HD)
        v = (h @ Wv).reshape(b, s, HKV, HD)
        cos, sin = _rope_cos_sin(s, HD, THETA)
        q = _apply_rope(q, cos, sin)
        k = _apply_rope(k, cos, sin)
        rep = H // HKV
        k = jnp.repeat(k, rep, axis=2)
        v = jnp.repeat(v, rep, axis=2)
        scores = jnp.einsum('bqhd,bkhd->bhqk', q, k) / np.sqrt(HD).astype(np.float32)
        causal = jnp.tril(jnp.ones((s, s), dtype=bool))
        scores = jnp.where(causal[None, None], scores, jnp.finfo(scores.dtype).min)
        attn = jax.nn.softmax(scores, axis=-1)
        ctx = jnp.einsum('bhqk,bkhd->bqhd', attn, v).reshape(b, s, H * HD)
        attn_out = ctx @ Wo
        h = jnp.clip(residual + attn_out, -100.0, 100.0)
        residual = h
        hn = _rmsnorm(h, ln2_w)
        flat = hn.reshape(b * s, d)
        logits = flat @ Wr
        probs = jax.nn.softmax(logits, axis=-1)
        topv, topi = jax.lax.top_k(probs, K)
        topv = topv / jnp.sum(topv, axis=-1, keepdims=True)
        w = jnp.sum(jax.nn.one_hot(topi, E, dtype=flat.dtype) * topv[..., None], axis=1)
        g = jnp.einsum('td,edf->etf', flat, Wg)
        u = jnp.einsum('td,edf->etf', flat, Wu)
        a = jax.nn.silu(g) * u
        o = jnp.einsum('etf,efd->etd', a, Wd)
        moe_out = jnp.einsum('te,etd->td', w, o).reshape(b, s, d)
        out = jnp.clip(residual + moe_out, -100.0, 100.0)
        return out
    x = x + _L0_xattn_ref(_layernorm(x, axis=-1), ctx_1024, ctx_1024, L0_xattn_wq, L0_xattn_bq, L0_xattn_wk, L0_xattn_bk, L0_xattn_wv, L0_xattn_bv, L0_xattn_wo, L0_xattn_bo)
    x = x + _L0_attn_ref(_layernorm(x, axis=-1), L0_attn_context, L0_attn_Wq, L0_attn_Wk, L0_attn_Wv, L0_attn_Wout, L0_attn_bout)
    x = x + _L0_ffn_ref(_layernorm(x, axis=-1), L0_ffn_gate_w1, L0_ffn_gate_b1, L0_ffn_gate_w2, L0_ffn_gate_b2, L0_ffn_W1, L0_ffn_b1, L0_ffn_W2, L0_ffn_b2, L0_ffn_TW1, L0_ffn_Tb1, L0_ffn_TW2, L0_ffn_Tb2)
    x = x + _L1_xattn_ref(_layernorm(x, axis=-1), ctx_1024, ctx_1024, L1_xattn_Wq, L1_xattn_bq, L1_xattn_Wk, L1_xattn_bk, L1_xattn_Wv, L1_xattn_bv, L1_xattn_Wo, L1_xattn_bo)
    x = x + _L1_attn_ref(_layernorm(x, axis=-1), L1_attn_Wq, L1_attn_bq, L1_attn_Wk, L1_attn_bk, L1_attn_Wv, L1_attn_bv, L1_attn_Wo, L1_attn_bo, L1_attn_slopes)
    x = x + _L1_ffn_ref(_layernorm(x, axis=-1), L1_ffn_ln1_w, L1_ffn_ln2_w, L1_ffn_Wq, L1_ffn_Wk, L1_ffn_Wv, L1_ffn_Wo, L1_ffn_Wr, L1_ffn_Wg, L1_ffn_Wu, L1_ffn_Wd)
    return x

_drawn_inputs = setup_inputs


def setup_inputs(seed=0):
    import zlib

    import numpy as np

    out = dict(_drawn_inputs(seed))
    spreads = {'L0_attn_bout': (0.0, 0.1),
     'L0_ffn_gate_b1': (0.0, 0.8),
     'L0_ffn_gate_b2': (0.20000000298023224, 0.6),
     'L1_xattn_bq': (0.0, 0.445),
     'L1_xattn_bk': (0.0, 0.8),
     'L1_xattn_bv': (0.0, 0.1),
     'L1_xattn_bo': (0.0, 0.1),
     'L1_attn_bq': (0.0, 0.666),
     'L1_attn_bk': (0.0, 0.8),
     'L1_attn_bv': (0.0, 0.1),
     'L1_attn_bo': (0.0, 0.1)}
    factors = {'L0_xattn_bq': 5.027,
     'L0_xattn_bk': 8.0,
     'L0_ffn_gate_w1': 8.0,
     'L0_ffn_gate_w2': 8.0,
     'L0_ffn_b1': 8.0,
     'L0_ffn_b2': 3.071,
     'L0_ffn_Tb1': 8.0,
     'L0_ffn_Tb2': 5.118,
     'L1_ffn_ln1_w': 8.0,
     'L1_ffn_ln2_w': 8.0,
     'L1_ffn_Wq': 8.0,
     'L1_ffn_Wk': 8.0,
     'L1_ffn_Wr': 8.0,
     'L1_ffn_Wg': 8.0,
     'L1_ffn_Wu': 8.0,
     'L1_ffn_Wd': 8.0}
    for name, (base, spread) in spreads.items():
        noise = np.random.default_rng([zlib.crc32(name.encode()), seed]).standard_normal(out[name].shape)
        drawn = base * np.exp(spread * noise) if base else spread * noise
        out[name] = jnp.asarray(drawn.astype(out[name].dtype))
    for name, factor in factors.items():
        out[name] = (out[name] * factor).astype(out[name].dtype)
    return out
```

```python
from contextlib import ExitStack, contextmanager

import numpy as np
import concourse.bass as bass
from concourse import mybir

F32 = mybir.dt.float32
ALU = mybir.AluOpType
ACT = mybir.ActivationFunctionType
AX = mybir.AxisListType.X

P = 128
BATCH, SEQ, DIM = 16, 64, 256
TOKENS = BATCH * SEQ
TILES = TOKENS // P
CHUNKS = DIM // P
BANK = 512
HALVES = TOKENS // BANK
HEADS, HEAD_DIM = 16, 16
PAIRS = HEADS // 2
GROUP_PAIRS = 4
GROUPS = 2
GROUP_HEADS = 8
KEYS = 1601
KEY_TILES = -(-KEYS // P)
KEYS_PADDED = KEY_TILES * P
LAST_KEYS = KEYS - (KEY_TILES - 1) * P
LN_EPS = 1e-5
ds = bass.ds


class Core:

    def __init__(self, nc, dram):
        self.nc, self.dram = nc, dram
        self.counted = []

    @contextmanager
    def block(self):
        with self.nc.Block() as block:
            yield block
        numbers, self.counted = sorted(self.counted), []
        while numbers:
            n = 1
            while n < len(numbers) and numbers[n] == numbers[0] + n:
                n += 1
            self.nc.gpsimd.sem_clear(range(numbers[0], numbers[0] + n))
            numbers = numbers[n:]

    def sbuf(self, stack, name, shape, dtype=F32):
        return stack.enter_context(self.nc.sbuf_tensor(name, shape, dtype))

    def banks(self, stack, name, n):
        return stack.enter_context(self.nc.psum_tensor(name, [P, n, BANK], F32))

    def sem(self, stack, name):
        semaphore = stack.enter_context(self.nc.semaphore(name))
        self.counted.append(semaphore.num)
        return semaphore


def load_block(core, name, pairs):
    nc = core.nc
    with ExitStack() as stack:
        loaded = core.sem(stack, f"{name}_loaded")
        with core.block() as block:
            @block.sync
            def _(sp):
                for tile, view in pairs:
                    sp.dma_start(tile, view).then_inc(loaded, 16)
                sp.wait_ge(loaded, 16 * len(pairs))


def norm_block(core, name, src, dst, dst_t, centered, feature_scale=None):
    nc = core.nc
    with ExitStack() as stack:
        stats = core.sbuf(stack, f"{name}_stats", [P, TILES, 6])
        moments = core.sbuf(stack, f"{name}_moments", [P, TILES, 2])
        spread = core.sbuf(stack, f"{name}_spread", [P, 3, TILES])
        rstd = core.sbuf(stack, f"{name}_rstd", [P, TILES])
        turned = core.banks(stack, f"{name}_turned", 4)
        sums_done = core.sem(stack, f"{name}_sums_done")
        moments_ready = core.sem(stack, f"{name}_moments_ready")
        own_step = core.sem(stack, f"{name}_own_step")
        spread_ready = core.sem(stack, f"{name}_spread_ready")
        root_ready = core.sem(stack, f"{name}_root_ready")
        rows_ready = core.sem(stack, f"{name}_rows_ready")
        turned_ready = core.sem(stack, f"{name}_turned_ready")

        with core.block() as block:
            @block.vector
            def _(dve):
                steps = [0]

                def step(ins):
                    steps[0] += 1
                    ins.then_inc(own_step, 1)
                    dve.wait_ge(own_step, steps[0])

                for t in range(TILES):
                    nc.vector.bn_stats(stats[:, t, :], src[:, t, :]).then_inc(sums_done, 1)
                for t in range(TILES):
                    dve.wait_ge(sums_done, t + 1)
                    nc.vector.bn_aggr(moments[:, t, :], stats[:, t, :]).then_inc(moments_ready, 1)
                dve.wait_ge(moments_ready, TILES)
                step(nc.vector.tensor_scalar(spread[:, 0], moments[:, :, 1], LN_EPS, None, ALU.add))
                if not centered:
                    step(nc.vector.tensor_tensor(spread[:, 1], moments[:, :, 0], moments[:, :, 0], ALU.mult))
                    step(nc.vector.tensor_tensor(spread[:, 0], spread[:, 0], spread[:, 1], ALU.add))
                dve.sem_inc(spread_ready, 1)
                dve.wait_ge(root_ready, 1)
                step(nc.vector.reciprocal(spread[:, 2], spread[:, 1]))
                step(nc.vector.tensor_tensor(spread[:, 2], spread[:, 2], spread[:, 0], ALU.mult))
                step(nc.vector.tensor_tensor(spread[:, 2], spread[:, 2], spread[:, 1], ALU.add))
                step(nc.vector.tensor_scalar(spread[:, 2], spread[:, 2], 0.5, None, ALU.mult))
                step(nc.vector.reciprocal(rstd[:], spread[:, 2]))
                for t in range(TILES):
                    if centered:
                        ins = nc.vector.tensor_scalar(dst[:, t, :], src[:, t, :], moments[:, t, 0:1],
                                                      rstd[:, t:t + 1], ALU.subtract, ALU.mult)
                    else:
                        ins = nc.vector.tensor_scalar(dst[:, t, :], src[:, t, :], rstd[:, t:t + 1],
                                                      None, ALU.mult)
                    ins.then_inc(rows_ready, 1)

            @block.tensor
            def _(pe):
                for t in range(TILES if dst_t is not None else 0):
                    pe.wait_ge(rows_ready, t + 1)
                    for c in range(CHUNKS):
                        last = nc.tensor.transpose(
                            turned[:, HALVES * c + t // 4, (t % 4) * P:(t % 4 + 1) * P],
                            dst[:, t, c * P:(c + 1) * P], core.ident[:])
                    if t % 4 == 3:
                        last.then_inc(turned_ready, 1)

            @block.scalar
            def _(act):
                act.wait_ge(spread_ready, 1)
                nc.scalar.activation(spread[:, 1], spread[:, 0], ACT.Sqrt).then_inc(root_ready, 1)
                for half in range(HALVES if dst_t is not None else 0):
                    act.wait_ge(turned_ready, half + 1)
                    for c in range(CHUNKS):
                        scale = 1.0 if feature_scale is None else feature_scale[:, c:c + 1]
                        nc.scalar.activation(dst_t[:, c, half * BANK:(half + 1) * BANK],
                                             turned[:, HALVES * c + half, :], ACT.Copy if feature_scale is None else ACT.Identity,
                                             scale=scale)


def dense_block(core, name, tasks):
    nc = core.nc
    units = 4
    with ExitStack() as stack:
        psum = core.banks(stack, f"{name}_psum", 2 * units)
        products_ready = core.sem(stack, f"{name}_products_ready")
        moved = {on: core.sem(stack, f"{name}_moved_{on}") for on in ("dve", "act")}
        own_step = core.sem(stack, f"{name}_own_step")

        def moved_count(i):
            return sum(tasks[k][2] == tasks[i][2] for k in range(i + 1))

        with core.block() as block:
            @block.tensor
            def _(pe):
                for i, (products, _, on) in enumerate(tasks):
                    if i >= units:
                        pe.wait_ge(moved[tasks[i - units][2]], moved_count(i - units))
                    u = 2 * (i % units)
                    for part, lhs_t, rhs, start, stop in products:
                        last = nc.tensor.matmul(part(psum[:, u:u + 2, :]), lhs_t, rhs, start=start, stop=stop)
                    last.then_inc(products_ready, 1)

            @block.vector
            def _(dve):
                steps = [0]

                def step(ins):
                    steps[0] += 1
                    ins.then_inc(own_step, 1)
                    dve.wait_ge(own_step, steps[0])

                for i, (_, move, on) in enumerate(tasks):
                    if on == "dve":
                        dve.wait_ge(products_ready, i + 1)
                        move(psum[:, 2 * (i % units):2 * (i % units) + 2, :], step).then_inc(moved["dve"], 1)

            @block.scalar
            def _(act):
                for i, (_, move, on) in enumerate(tasks):
                    if on == "act":
                        act.wait_ge(products_ready, i + 1)
                        move(psum[:, 2 * (i % units):2 * (i % units) + 2, :], None).then_inc(moved["act"], 1)


def feature_products(weights, m, src_t, chunks=CHUNKS, rows=P, cols=P):
    return [(lambda u, h=h: u[0:cols, h, :], weights[:, k, m * cols:(m + 1) * cols],
             src_t[:, k, h * BANK:(h + 1) * BANK], k == 0, k == chunks - 1)
            for h in range(HALVES) for k in range(chunks)]


def project_feature_major(core, name, jobs):
    nc = core.nc
    tasks = []
    for weights, m_tiles, src_t, dst, bias, relu in jobs:
        for m in range(m_tiles):
            def move_dve(unit, step, m=m, dst=dst, bias=bias, relu=relu):
                out = dst[:, m, :].rearrange("p (h n) -> p h n", h=HALVES)
                if bias is None:
                    return nc.vector.tensor_copy(out, unit)
                if relu:
                    return nc.vector.tensor_scalar(out, unit, bias[:, m:m + 1], 0.0, ALU.add, ALU.max)
                return nc.vector.tensor_scalar(out, unit, bias[:, m:m + 1], None, ALU.add)

            def move_act(unit, step, m=m, dst=dst, bias=bias, relu=relu):
                out = dst[:, m, :].rearrange("p (h n) -> p h n", h=HALVES)
                func = ACT.Relu if relu else (ACT.Copy if bias is None else ACT.Identity)
                return nc.scalar.activation(out, unit, func, bias=0.0 if bias is None else bias[:, m:m + 1])

            on = ("dve", "act")[len(tasks) % 2]
            tasks.append((feature_products(weights, m, src_t), move_dve if on == "dve" else move_act, on))
    dense_block(core, name, tasks)


def add_projection(core, name, heads_t, chunks, weights, x):
    nc = core.nc
    tasks = []
    for t in range(TILES):
        products = [(lambda u: u[:, 0, 0:DIM], heads_t[:, k, t * P:(t + 1) * P], weights[:, k, :],
                     k == 0, k == chunks - 1) for k in range(chunks)]

        def move(unit, step, t=t):
            return nc.vector.tensor_tensor(x[:, t, :], unit[:, 0, 0:DIM], x[:, t, :], ALU.add)

        tasks.append((products, move, "dve"))
    dense_block(core, name, tasks)



A_COLS = 2 * BANK
B_COLS = KEYS - A_COLS
K_STARTS = list(range(0, KEYS, BANK))


def cross_attention(core, layer, key_groups, value_cols):
    nc, dram, x = core.nc, core.dram, core.x
    v_rows_cols = value_cols
    with ExitStack() as outer:
        def sb(name, shape):
            return core.sbuf(outer, f"{layer}_{name}", shape)

        wq, wo = sb("wq", [P, CHUNKS, DIM]), sb("wo", [P, CHUNKS, DIM])
        wk, wv = sb("wk", [P, CHUNKS, key_groups * P]), sb("wv", [P, CHUNKS, value_cols])
        bq, bk, bv = sb("bq", [P, GROUPS]), sb("bk", [P, key_groups]), sb("bv", [P, GROUPS])
        bo = sb("bo", [P, DIM])
        q_t, heads_t = sb("q_t", [P, GROUPS, TOKENS]), sb("heads_t", [P, GROUPS, TOKENS])
        load_block(core, f"{layer}_weights", [
            (wq[:], dram[f"{layer}_wq"]), (wo[:], dram[f"{layer}_wo"]), (wk[:], dram[f"{layer}_wk"]),
            (wv[:], dram[f"{layer}_wv"]), (bq[:], dram[f"{layer}_bq"]), (bk[:], dram[f"{layer}_bk"]),
            (bv[:], dram[f"{layer}_bv"]), (bo[:], dram[f"{layer}_bo"].partition_broadcast(P))])
        with ExitStack() as inner:
            xn = core.sbuf(inner, f"{layer}_xn", [P, TILES, DIM])
            xn_t = core.sbuf(inner, f"{layer}_xn_t", [P, CHUNKS, TOKENS])
            norm_block(core, f"{layer}_norm", x, xn, xn_t, True)
            project_feature_major(core, f"{layer}_q", [(wq, GROUPS, xn_t, q_t, bq, False)])
        cross_attention_block(core, layer, key_groups, value_cols, wk, bk, wv, bv, bo, q_t, heads_t)
        add_projection(core, f"{layer}_out", heads_t, CHUNKS, wo, x)


def cross_attention_block(core, layer, key_groups, value_cols, wk, bk, wv, bv, bo, q_t, heads_t):
    nc, dram, x = core.nc, core.dram, core.x
    SCALE = float(HEAD_DIM) ** -0.5
    v_per_unit = min(KEY_TILES, BANK // value_cols)
    k_units = [(g, s) for s in K_STARTS for g in range(key_groups)]
    v_units = [list(range(t, min(t + v_per_unit, KEY_TILES))) for t in range(0, KEY_TILES, v_per_unit)]
    units = k_units + v_units
    U = len(units)
    slots = [[] for _ in range(2 * PAIRS)]
    if key_groups == 2:
        for i in range(U):
            slots[i].append(i)
    else:
        for i in range(len(k_units)):
            slots[2 * i].append(i)
        slots[8].append(len(k_units))
    assert all(u < len(k_units) for s in slots[:4] for u in s)
    units_before = [sum(len(s) for s in slots[:i]) for i in range(2 * PAIRS)]

    with ExitStack() as stack:
        def sb(name, shape):
            return core.sbuf(stack, f"{layer}_{name}", shape)

        def sem(name):
            return core.sem(stack, f"{layer}_{name}")

        ctx = [sb(f"ctx{i}", [P, CHUNKS, KEYS]) for i in range(2)]
        k_t = [sb(f"k_t{i}", [P, key_groups, KEYS]) for i in range(2)]
        v = [sb(f"v{i}", [P, KEY_TILES, value_cols]) for i in range(2)]
        q_blocks = [sb(f"q_blocks{i}", [P, GROUPS, GROUP_HEADS, SEQ]) for i in range(2)]
        probs = [sb(f"probs{i}", [P, KEYS_PADDED]) for i in range(2)]
        probs_t = sb("probs_t", [P, KEY_TILES, GROUP_PAIRS * P])
        maxima = [sb(f"maxima{i}", [P, 4]) for i in range(2)]
        sums = [sb(f"sums{i}", [P, 4]) for i in range(2)]
        mixed = sb("mixed", [P, SEQ])
        scores = core.banks(stack, f"{layer}_scores", 4)
        turned = core.banks(stack, f"{layer}_turned", 2)
        projected = core.banks(stack, f"{layer}_projected", 1)
        weighed = core.banks(stack, f"{layer}_weighed", 1)
        scores_flat = scores[:].rearrange("p b n -> p (b n)")
        turned_tiles = turned[:].rearrange("p b (t n) -> p (b t) n", n=P)

        ctx_loaded = [sem(f"ctx_loaded{i}") for i in range(2)]
        pads_zeroed = sem("pads_zeroed")
        blocks_ready = sem("blocks_ready")
        projection_done = sem("projection_done")
        projection_moved = sem("projection_moved")
        scored = sem("scored")
        halves_maxed = sem("halves_maxed")
        bias_ready = sem("bias_ready")
        exps_done = sem("exps_done")
        sum_steps = sem("sum_steps")
        probs_ready = sem("probs_ready")
        turned_ready = sem("turned_ready")
        turned_moved = sem("turned_moved")
        weighed_ready = sem("weighed_ready")
        mixed_ready = sem("mixed_ready")
        heads_ready = sem("heads_ready")

        def over_batches(eng, body):
            body(0, 0, True, False)
            body(1, 1, False, False)
            with eng.Fori(1, BATCH // 2 - 1) as j:
                body(2 * j, 0, False, False)
                body(2 * j + 1, 1, False, False)
            body(BATCH - 2, 0, False, False)
            body(BATCH - 1, 1, False, True)

        with core.block() as block:
            @block.sync
            def _(sp):
                sp.dma_start(ctx[0][:], dram["ctx_t"][0]).then_inc(ctx_loaded[0], 16)
                sp.dma_start(ctx[1][:], dram["ctx_t"][1]).then_inc(ctx_loaded[1], 16)
                with sp.Fori(0, BATCH // 2 - 1) as j:
                    for parity in range(2):
                        used = sp.snap(U * (2 * j + parity + 1))
                        sp.wait_ge(projection_done, used)
                        sp.dma_start(ctx[parity][:], dram["ctx_t"][ds(2 * j + parity + 2, 1)].rearrange("o p c n -> (o p) c n")).then_inc(ctx_loaded[parity], 16)

            @block.gpsimd
            def _(pool):
                for i in range(2):
                    nc.gpsimd.memset(probs[i][:, KEYS:KEYS_PADDED], 0.0).then_inc(pads_zeroed, 1)
                nc.gpsimd.tensor_tensor(x[:], x[:], bo[:].unsqueeze(1).to_broadcast([P, TILES, DIM]), ALU.add)

                def blocks(b, parity, wait):
                    if wait:
                        pool.wait_ge(scored, 2 * PAIRS * (b - 1))
                    for g in range(GROUPS):
                        last = nc.gpsimd.tensor_tensor(
                            q_blocks[parity][:, g],
                            q_t[:, g, ds(b * SEQ, SEQ)].unsqueeze(1).to_broadcast([P, GROUP_HEADS, SEQ]),
                            core.head_mask[:].unsqueeze(2).to_broadcast([P, GROUP_HEADS, SEQ]), ALU.mult)
                    last.then_inc(blocks_ready, 1)

                blocks(0, 0, False)
                blocks(1, 1, False)
                with pool.Fori(1, BATCH // 2) as j:
                    blocks(2 * j, 0, True)
                    blocks(2 * j + 1, 1, True)

            @block.tensor
            def _(pe):
                def project(b, parity, u):
                    n = U * b + u
                    if u == 0:
                        pe.wait_ge(ctx_loaded[parity], 8 * (b - parity) + 16)
                    if not (isinstance(b, int) and n == 0):
                        pe.wait_ge(projection_moved, n)
                    if u < len(k_units):
                        g, s = k_units[u]
                        w = min(BANK, KEYS - s)
                        for k in range(CHUNKS):
                            last = nc.tensor.matmul(projected[:, 0, 0:w], wk[:, k, g * P:(g + 1) * P],
                                                    ctx[parity][:, k, s:s + w], start=k == 0, stop=k == CHUNKS - 1)
                    else:
                        for i, t in enumerate(v_units[u - len(k_units)]):
                            rows = P if t < KEY_TILES - 1 else LAST_KEYS
                            for k in range(CHUNKS):
                                last = nc.tensor.matmul(
                                    projected[0:rows, 0, i * value_cols:(i + 1) * value_cols],
                                    ctx[parity][:, k, t * P:t * P + rows], wv[:, k, :],
                                    start=k == 0, stop=k == CHUNKS - 1)
                    last.then_inc(projection_done, 1)

                def score(b, parity, n, half):
                    pair = PAIRS * b + n
                    g = n // GROUP_PAIRS
                    if not (isinstance(b, int) and pair == 0):
                        pe.wait_ge(exps_done, 2 * pair - 1 + half)
                    heads = q_blocks[parity][:, g, 2 * (n % GROUP_PAIRS):2 * (n % GROUP_PAIRS) + 2, :]
                    for s in K_STARTS[2 * half:2 * half + 2]:
                        w = min(BANK, KEYS - s)
                        last = nc.tensor.matmul(scores[:, s // BANK, 0:w], heads.rearrange("p h q -> p (h q)"),
                                                k_t[parity][:, g % key_groups, s:s + w], start=True, stop=True)
                    last.then_inc(scored, 1)

                def turn(b, n, part):
                    pair = PAIRS * b + n
                    if part == 0:
                        pe.wait_ge(probs_ready, pair + 1)
                    if not (isinstance(b, int) and pair == 0 and part == 0):
                        pe.wait_ge(turned_moved, 2 * pair + part)
                    tiles = range(0, 8) if part == 0 else range(8, KEY_TILES)
                    for i, t in enumerate(tiles):
                        last = nc.tensor.transpose(turned_tiles[:, i, :], probs[n % 2][:, t * P:(t + 1) * P], core.ident[:])
                    last.then_inc(turned_ready, 1)

                def weigh(b, parity, g):
                    group = GROUPS * b + g
                    pe.wait_ge(turned_moved, 2 * GROUP_PAIRS * (group + 1))
                    if not (isinstance(b, int) and group == 0):
                        pe.wait_ge(heads_ready, group)
                    for t in range(KEY_TILES):
                        rows = P if t < KEY_TILES - 1 else LAST_KEYS
                        for p in range(GROUP_PAIRS):
                            c = (2 * HEAD_DIM * (GROUP_PAIRS * g + p)) % value_cols
                            last = nc.tensor.matmul(
                                weighed[32 * p:32 * (p + 1), 0, 0:P], v[parity][0:rows, t, c:c + 32],
                                probs_t[0:rows, t, p * P:(p + 1) * P],
                                start=t == 0, stop=t == KEY_TILES - 1, skip_group_check=True)
                    last.then_inc(weighed_ready, 1)

                def batch(b, parity, first, last):
                    for n in range(PAIRS):
                        if n == 0:
                            pe.wait_ge(blocks_ready, b + 1)
                            pe.wait_ge(projection_moved, U * b + U)
                        score(b, parity, n, 0)
                        if n == 1 and not first:
                            weigh(b - 1, 1 - parity, 1)
                        if n == GROUP_PAIRS + 1:
                            weigh(b, parity, 0)
                        if not last:
                            for u in slots[2 * n]:
                                project(b + 1, 1 - parity, u)
                        if n > 0:
                            turn(b, n - 1, 0)
                        elif not first:
                            turn(b - 1, PAIRS - 1, 0)
                        score(b, parity, n, 1)
                        if not last:
                            for u in slots[2 * n + 1]:
                                project(b + 1, 1 - parity, u)
                        if n > 0:
                            turn(b, n - 1, 1)
                        elif not first:
                            turn(b - 1, PAIRS - 1, 1)

                for u in range(U):
                    project(0, 0, u)
                over_batches(pe, batch)
                turn(BATCH - 1, PAIRS - 1, 0)
                turn(BATCH - 1, PAIRS - 1, 1)
                weigh(BATCH - 1, 1, 1)

            @block.vector
            def _(dve):
                def move_projection(b, parity, u):
                    dve.wait_ge(projection_done, U * b + u + 1)
                    if u < len(k_units):
                        g, s = k_units[u]
                        w = min(BANK, KEYS - s)
                        ins = nc.vector.tensor_scalar(k_t[parity][:, g, s:s + w], projected[:, 0, 0:w],
                                                      bk[:, g:g + 1], None, ALU.add)
                    else:
                        tiles = v_units[u - len(k_units)]
                        full = [t for t in tiles if t < KEY_TILES - 1]
                        if full:
                            n = len(full)
                            ins = nc.vector.tensor_copy(
                                v[parity][:, full[0]:full[0] + n, :],
                                projected[:, 0, 0:n * value_cols].rearrange("p (t c) -> p t c", c=value_cols))
                        if tiles[-1] == KEY_TILES - 1:
                            n = len(full)
                            ins = nc.vector.tensor_copy(v[parity][0:LAST_KEYS, KEY_TILES - 1, :],
                                                        projected[0:LAST_KEYS, 0, n * value_cols:(n + 1) * value_cols])
                    ins.then_inc(projection_moved, 1)

                def maximum(b, n, half):
                    pair = PAIRS * b + n
                    dve.wait_ge(scored, 2 * pair + half + 1)
                    cols = scores_flat[:, 0:A_COLS] if half == 0 else scores_flat[:, A_COLS:KEYS]
                    if half == 0 and not (isinstance(b, int) and pair < 2):
                        dve.wait_ge(exps_done, 2 * (pair - 1))
                    nc.vector.reduce_max(maxima[n % 2][:, half:half + 1], cols, axis=AX).then_inc(halves_maxed, 1)
                    if half == 1:
                        dve.wait_ge(halves_maxed, 2 * pair + 2)
                        nc.vector.tensor_scalar(maxima[n % 2][:, 2:3], maxima[n % 2][:, 0:1], maxima[n % 2][:, 1:2],
                                                -SCALE, ALU.max, ALU.mult).then_inc(bias_ready, 1)

                def normalise(b, n):
                    pair = PAIRS * b + n
                    s = sums[n % 2]
                    dve.wait_ge(exps_done, 2 * pair + 2)
                    nc.vector.tensor_tensor(s[:, 2:3], s[:, 0:1], s[:, 1:2], ALU.add).then_inc(sum_steps, 1)
                    dve.wait_ge(sum_steps, 2 * pair + 1)
                    nc.vector.reciprocal(s[:, 3:4], s[:, 2:3]).then_inc(sum_steps, 1)
                    dve.wait_ge(sum_steps, 2 * pair + 2)
                    nc.vector.tensor_scalar(probs[n % 2][:, 0:KEYS], probs[n % 2][:, 0:KEYS], s[:, 3:4], None,
                                            ALU.mult).then_inc(probs_ready, 1)

                def keep_heads(b, g):
                    group = GROUPS * b + g
                    dve.wait_ge(weighed_ready, group + 1)
                    nc.vector.tensor_scalar(mixed[:], weighed[:, 0, 0:SEQ], core.even_head[:], bv[:, g:g + 1],
                                            ALU.mult, ALU.add).then_inc(mixed_ready, 1)
                    dve.wait_ge(mixed_ready, group + 1)
                    nc.vector.scalar_tensor_tensor(heads_t[:, g, ds(b * SEQ, SEQ)], weighed[:, 0, SEQ:2 * SEQ],
                                                   core.odd_head[:], mixed[:], ALU.mult, ALU.add).then_inc(heads_ready, 1)

                def batch(b, parity, first, last):
                    for n in range(PAIRS):
                        maximum(b, n, 0)
                        if n == 1 and not first:
                            keep_heads(b - 1, 1)
                        if n == GROUP_PAIRS + 1:
                            keep_heads(b, 0)
                        if not last:
                            for u in slots[2 * n]:
                                move_projection(b + 1, 1 - parity, u)
                        maximum(b, n, 1)
                        if not last:
                            for u in slots[2 * n + 1]:
                                move_projection(b + 1, 1 - parity, u)
                        normalise(b, n)

                for u in range(U):
                    move_projection(0, 0, u)
                over_batches(dve, batch)
                keep_heads(BATCH - 1, 1)

            @block.scalar
            def _(act):
                def move_turned(b, n, part):
                    pair = PAIRS * b + n
                    act.wait_ge(turned_ready, 2 * pair + part + 1)
                    if n % GROUP_PAIRS == 0 and part == 0 and not (isinstance(b, int) and pair == 0):
                        act.wait_ge(weighed_ready, pair // GROUP_PAIRS if isinstance(pair, int) else GROUPS * b + n // GROUP_PAIRS)
                    t, m = (0, 8) if part == 0 else (8, KEY_TILES - 8)
                    p = n % GROUP_PAIRS
                    nc.scalar.activation(probs_t[:, t:t + m, p * P:(p + 1) * P], turned_tiles[:, 0:m, :],
                                         ACT.Copy).then_inc(turned_moved, 1)

                def exps(b, n, half):
                    pair = PAIRS * b + n
                    if half == 0:
                        act.wait_ge(bias_ready, pair + 1)
                        if not (isinstance(b, int) and pair < 2):
                            act.wait_ge(turned_ready, 2 * pair - 2)
                    lo, hi = (0, A_COLS) if half == 0 else (A_COLS, KEYS)
                    nc.scalar.activation(probs[n % 2][:, lo:hi], scores_flat[:, lo:hi], ACT.Exp,
                                         bias=maxima[n % 2][:, 2:3], scale=SCALE,
                                         accum_out=sums[n % 2][:, half:half + 1]).then_inc(exps_done, 1)

                def batch(b, parity, first, last):
                    for n in range(PAIRS):
                        if n > 0:
                            move_turned(b, n - 1, 0)
                        elif not first:
                            move_turned(b - 1, PAIRS - 1, 0)
                        exps(b, n, 0)
                        exps(b, n, 1)
                        if n > 0:
                            move_turned(b, n - 1, 1)
                        elif not first:
                            move_turned(b - 1, PAIRS - 1, 1)

                act.wait_ge(pads_zeroed, 2)
                over_batches(act, batch)
                move_turned(BATCH - 1, PAIRS - 1, 0)
                move_turned(BATCH - 1, PAIRS - 1, 1)



WIDE_HEADS, WIDE_DIM = 8, 128
WIDE_KEYS = 1024
CTX_ROWS = 96
WIDE_KEY_TILES = WIDE_KEYS // P
QUERY_TILES = 4


def wide_attention(core):
    nc, dram, x = core.nc, core.dram, core.x
    with ExitStack() as outer:
        heads_t = core.sbuf(outer, "wide_heads_t", [P, WIDE_HEADS, TOKENS])
        with ExitStack() as inner:
            xn_t = core.sbuf(inner, "wide_xn_t", [P, CHUNKS, TOKENS])
            with ExitStack() as norm:
                xn = core.sbuf(norm, "wide_xn", [P, TILES, DIM])
                norm_block(core, "wide_norm", x, xn, xn_t, True)
            wide_attention_block(core, xn_t, heads_t)
        wout = core.sbuf(outer, "wide_wout", [P, WIDE_HEADS, DIM])
        bout = core.sbuf(outer, "wide_bout", [P, DIM])
        load_block(core, "wide_out_weights", [(wout[:], dram["L0_attn_wout"]),
                                              (bout[:], dram["L0_attn_bout"].partition_broadcast(P))])
        add_bias_block(core, "wide_bias", bout)
        add_projection(core, "wide_out", heads_t, WIDE_HEADS, wout, x)


def add_bias_block(core, name, bias):
    nc, x = core.nc, core.x
    with core.block() as block:
        @block.gpsimd
        def _(pool):
            nc.gpsimd.tensor_tensor(x[:, 0:3], x[:, 0:3], bias[:].unsqueeze(1).to_broadcast([P, 3, DIM]), ALU.add)

        @block.vector
        def _(dve):
            nc.vector.tensor_tensor(x[:, 3:TILES], x[:, 3:TILES],
                                    bias[:].unsqueeze(1).to_broadcast([P, TILES - 3, DIM]), ALU.add)


def wide_attention_block(core, xn_t, heads_t):
    nc, dram = core.nc, core.dram
    SCALE = 1.5 * float(WIDE_DIM) ** -0.5
    U = 6
    WIDE_GROUPS = TILES // QUERY_TILES
    with ExitStack() as stack:
        def sb(name, shape):
            return core.sbuf(stack, f"wide_{name}", shape)

        def sem(name):
            return core.sem(stack, f"wide_{name}")

        ctx = sb("ctx", [CTX_ROWS, CHUNKS, WIDE_KEYS])
        w_q = [sb(f"w_q{i}", [P, CHUNKS, WIDE_DIM]) for i in range(2)]
        w_k = [sb(f"w_k{i}", [CTX_ROWS, CHUNKS, WIDE_DIM]) for i in range(2)]
        w_v = [sb(f"w_v{i}", [CTX_ROWS, CHUNKS, WIDE_DIM]) for i in range(2)]
        q_t = [sb(f"q_t{i}", [P, TOKENS]) for i in range(2)]
        k_t = [sb(f"k_t{i}", [P, WIDE_KEYS]) for i in range(2)]
        v = [sb(f"v{i}", [P, WIDE_KEY_TILES, WIDE_DIM]) for i in range(2)]
        probs = [sb(f"probs{i}", [P, WIDE_KEYS]) for i in range(2)]
        probs_t = [sb(f"probs_t{i}", [P, WIDE_KEY_TILES, BANK]) for i in range(2)]
        stats = [sb(f"stats{i}", [P, 4]) for i in range(2)]
        scores = [core.banks(stack, f"wide_scores{i}", 2) for i in range(2)]
        turned = core.banks(stack, "wide_turned", 2)
        projected = core.banks(stack, "wide_projected", 1)
        weighed = core.banks(stack, "wide_weighed", 1)

        ctx_loaded = sem("ctx_loaded")
        weights_loaded = [sem(f"weights_loaded{i}") for i in range(2)]
        projection_done = sem("projection_done")
        projection_moved = sem("projection_moved")
        scored = sem("scored")
        maximum_ready = sem("maximum_ready")
        bias_ready = sem("bias_ready")
        exp_done = sem("exp_done")
        inverse_ready = sem("inverse_ready")
        probs_ready = sem("probs_ready")
        turned_ready = sem("turned_ready")
        turned_moved = sem("turned_moved")
        weighed_ready = sem("weighed_ready")
        heads_ready = sem("heads_ready")

        def over_heads(eng, body):
            body(0, 0, True, False)
            body(1, 1, False, False)
            with eng.Fori(1, WIDE_HEADS // 2 - 1) as j:
                body(2 * j, 0, False, False)
                body(2 * j + 1, 1, False, False)
            body(WIDE_HEADS - 2, 0, False, False)
            body(WIDE_HEADS - 1, 1, False, True)

        with core.block() as block:
            @block.sync
            def _(sp):
                def load(h, parity):
                    for tile, name in ((w_q, "L0_attn_wq"), (w_k, "L0_attn_wk"), (w_v, "L0_attn_wv")):
                        sp.dma_start(tile[parity][:], dram[name][ds(h, 1)].rearrange("o p c n -> (o p) c n")).then_inc(weights_loaded[parity], 16)

                load(0, 0)
                sp.dma_start(ctx[:], dram["L0_attn_ctx_t"]).then_inc(ctx_loaded, 16)
                load(1, 1)
                with sp.Fori(0, WIDE_HEADS // 2 - 1) as j:
                    for parity in range(2):
                        used = sp.snap(U * (2 * j + parity + 1))
                        sp.wait_ge(projection_done, used)
                        load(2 * j + parity + 2, parity)

            @block.tensor
            def _(pe):
                def project(h, parity, u):
                    if u == 0:
                        pe.wait_ge(weights_loaded[parity], 24 * (h - parity) + 48)
                    if not (isinstance(h, int) and U * h + u == 0):
                        pe.wait_ge(projection_moved, U * h + u)
                    for k in range(CHUNKS):
                        if u < 2:
                            last = nc.tensor.matmul(projected[:, 0, :], w_q[parity][:, k, :],
                                                    xn_t[:, k, u * BANK:(u + 1) * BANK], start=k == 0, stop=k == 1)
                        elif u < 4:
                            last = nc.tensor.matmul(projected[:, 0, :], w_k[parity][:, k, :],
                                                    ctx[:, k, (u - 2) * BANK:(u - 1) * BANK], start=k == 0, stop=k == 1)
                    if u >= 4:
                        for i in range(4):
                            t = 4 * (u - 4) + i
                            for k in range(CHUNKS):
                                last = nc.tensor.matmul(projected[:, 0, i * P:(i + 1) * P], ctx[:, k, t * P:(t + 1) * P],
                                                        w_v[parity][:, k, :], start=k == 0, stop=k == 1)
                    last.then_inc(projection_done, 1)

                def score(h, parity, t):
                    n = TILES * h + t
                    if not (isinstance(h, int) and n < 2):
                        pe.wait_ge(exp_done, n - 1)
                    for s in range(HALVES):
                        last = nc.tensor.matmul(scores[t % 2][:, s, :], q_t[parity][:, t * P:(t + 1) * P],
                                                k_t[parity][:, s * BANK:(s + 1) * BANK], start=True, stop=True)
                    last.then_inc(scored, 1)

                def turn(h, t):
                    n = TILES * h + t
                    pe.wait_ge(probs_ready, n + 1)
                    if not (isinstance(h, int) and n == 0):
                        pe.wait_ge(turned_moved, n)
                    for i in range(WIDE_KEY_TILES):
                        last = nc.tensor.transpose(turned[:, i // 4, (i % 4) * P:(i % 4 + 1) * P],
                                                   probs[t % 2][:, i * P:(i + 1) * P], core.ident[:])
                    last.then_inc(turned_ready, 1)

                def weigh(h, parity, g):
                    group = WIDE_GROUPS * h + g
                    pe.wait_ge(turned_moved, QUERY_TILES * (group + 1))
                    if not (isinstance(h, int) and group == 0):
                        pe.wait_ge(heads_ready, group)
                    for i in range(WIDE_KEY_TILES):
                        last = nc.tensor.matmul(weighed[:, 0, :], v[parity][:, i, :], probs_t[g][:, i, :],
                                                start=i == 0, stop=i == WIDE_KEY_TILES - 1)
                    last.then_inc(weighed_ready, 1)

                def head(h, parity, first, last):
                    pe.wait_ge(projection_moved, U * h + U)
                    for t in range(TILES):
                        score(h, parity, t)
                        if t == 1 and not first:
                            weigh(h - 1, 1 - parity, 1)
                        if t == QUERY_TILES + 1:
                            weigh(h, parity, 0)
                        if not last and 2 <= t:
                            project(h + 1, 1 - parity, t - 2)
                        if t > 0:
                            turn(h, t - 1)
                        elif not first:
                            turn(h - 1, TILES - 1)

                pe.wait_ge(ctx_loaded, 16)
                for u in range(U):
                    project(0, 0, u)
                over_heads(pe, head)
                turn(WIDE_HEADS - 1, TILES - 1)
                weigh(WIDE_HEADS - 1, 1, 1)

            @block.vector
            def _(dve):
                def move_projection(h, parity, u):
                    dve.wait_ge(projection_done, U * h + u + 1)
                    if u < 2:
                        out = q_t[parity][:, u * BANK:(u + 1) * BANK]
                    elif u < 4:
                        out = k_t[parity][:, (u - 2) * BANK:(u - 1) * BANK]
                    else:
                        out = v[parity][:, 4 * (u - 4):4 * (u - 3), :].rearrange("p t d -> p (t d)")
                    nc.vector.tensor_copy(out, projected[:, 0, :]).then_inc(projection_moved, 1)

                def maximum(h, t):
                    n = TILES * h + t
                    dve.wait_ge(scored, n + 1)
                    nc.vector.reduce_max(stats[t % 2][:, 0:1], scores[t % 2][:].rearrange("p b n -> p (b n)"),
                                         axis=AX).then_inc(maximum_ready, 1)
                    if not (isinstance(h, int) and n < 2):
                        dve.wait_ge(exp_done, n - 1)
                    dve.wait_ge(maximum_ready, n + 1)
                    nc.vector.tensor_scalar(stats[t % 2][:, 1:2], stats[t % 2][:, 0:1], -SCALE, None,
                                            ALU.mult).then_inc(bias_ready, 1)

                def normalise(h, t):
                    n = TILES * h + t
                    dve.wait_ge(exp_done, n + 1)
                    nc.vector.reciprocal(stats[t % 2][:, 3:4], stats[t % 2][:, 2:3]).then_inc(inverse_ready, 1)
                    dve.wait_ge(inverse_ready, n + 1)
                    nc.vector.tensor_scalar(probs[t % 2][:], probs[t % 2][:], stats[t % 2][:, 3:4], None,
                                            ALU.mult).then_inc(probs_ready, 1)

                def keep_heads(h, g):
                    dve.wait_ge(weighed_ready, WIDE_GROUPS * h + g + 1)
                    nc.vector.tensor_copy(heads_t[:, ds(h, 1), g * BANK:(g + 1) * BANK].rearrange("p o n -> p (o n)"),
                                          weighed[:, 0, :]).then_inc(heads_ready, 1)

                def head(h, parity, first, last):
                    for t in range(TILES):
                        maximum(h, t)
                        if t == 1 and not first:
                            keep_heads(h - 1, 1)
                        if t == QUERY_TILES + 1:
                            keep_heads(h, 0)
                        normalise(h, t)
                        if not last and 2 <= t:
                            move_projection(h + 1, 1 - parity, t - 2)

                for u in range(U):
                    move_projection(0, 0, u)
                over_heads(dve, head)
                keep_heads(WIDE_HEADS - 1, 1)

            @block.scalar
            def _(act):
                def move_turned(h, t):
                    n = TILES * h + t
                    act.wait_ge(turned_ready, n + 1)
                    group = WIDE_GROUPS * h + t // QUERY_TILES
                    if t % QUERY_TILES == 0 and not (isinstance(h, int) and group < 2):
                        act.wait_ge(weighed_ready, group - 1)
                    q = t % QUERY_TILES
                    nc.scalar.activation(probs_t[t // QUERY_TILES][:, :, q * P:(q + 1) * P],
                                         turned[:].rearrange("p b (t n) -> p (b t) n", n=P), ACT.Copy).then_inc(turned_moved, 1)

                def head(h, parity, first, last):
                    for t in range(TILES):
                        n = TILES * h + t
                        act.wait_ge(bias_ready, n + 1)
                        if not (isinstance(h, int) and n < 2):
                            act.wait_ge(turned_ready, n - 1)
                        nc.scalar.activation(probs[t % 2][:], scores[t % 2][:].rearrange("p b n -> p (b n)"), ACT.Exp,
                                             bias=stats[t % 2][:, 1:2], scale=SCALE,
                                             accum_out=stats[t % 2][:, 2:3]).then_inc(exp_done, 1)
                        if t > 0:
                            move_turned(h, t - 1)
                        elif not first:
                            move_turned(h - 1, TILES - 1)

                over_heads(act, head)
                move_turned(WIDE_HEADS - 1, TILES - 1)



TASKS = 8
PARTS = TASKS + 1
HIDDEN = 1024
HIDDEN_TILES = HIDDEN // P


def merged_ffn(core):
    nc, dram, x = core.nc, core.dram, core.x
    with ExitStack() as outer:
        def sb(stack, name, shape):
            return core.sbuf(stack, f"ffn_{name}", shape)

        gates_by_token = sb(outer, "gates_by_token", [P, TILES, PARTS])
        gates_by_task = sb(outer, "gates_by_task", [TASKS, TOKENS])
        hidden_t = sb(outer, "hidden_t", [P, HIDDEN_TILES, TOKENS])
        with ExitStack() as inner:
            xn_t = sb(inner, "xn_t", [P, CHUNKS, TOKENS])
            scaled_t = sb(inner, "scaled_t", [P, TASKS, CHUNKS, TOKENS])
            with ExitStack() as norm:
                xn = sb(norm, "xn", [P, TILES, DIM])
                gw1, gb1 = sb(norm, "gw1", [P, CHUNKS, DIM]), sb(norm, "gb1", [P, CHUNKS])
                gw2, gw2_wide = sb(norm, "gw2", [P, CHUNKS, TASKS]), sb(norm, "gw2_wide", [P, CHUNKS, TASKS, P])
                gb2, gb2_column = sb(norm, "gb2", [P, TASKS]), sb(norm, "gb2_column", [TASKS, 1])
                b2 = sb(norm, "b2", [P, DIM])
                gate_t = sb(norm, "gate_t", [P, CHUNKS, TOKENS])
                load_block(core, "ffn_gate_weights", [
                    (gw1[:], dram["gate_w1"]), (gb1[:], dram["gate_b1"]), (gw2[:], dram["gate_w2"]),
                    (gw2_wide[:], dram["gate_w2_wide"]), (gb2[:], dram["gate_b2"].partition_broadcast(P)),
                    (gb2_column[:], dram["gate_b2"].unsqueeze(1)), (b2[:], dram["ffn_b2"].partition_broadcast(P))])
                norm_block(core, "ffn_norm", x, xn, xn_t, True)
                add_bias_block(core, "ffn_bias", b2)
                project_feature_major(core, "ffn_gate", [(gw1, CHUNKS, xn_t, gate_t, gb1, True)])
                gates_block(core, gate_t, gw2, gw2_wide, gb2, gb2_column, xn_t, gates_by_token, gates_by_task, scaled_t)
            merged_up_block(core, xn_t, scaled_t, gates_by_task, hidden_t)
        merged_down_block(core, hidden_t, gates_by_token, gates_by_task)


def gates_block(core, gate_t, gw2, gw2_wide, gb2, gb2_column, xn_t, gates_by_token, gates_by_task, scaled_t):
    nc = core.nc
    with ExitStack() as stack:
        mean = core.sbuf(stack, "gates_mean", [P, CHUNKS, BATCH])
        mean_tokens = core.sbuf(stack, "gates_mean_tokens", [P, CHUNKS, TOKENS])
        gates_wide = core.sbuf(stack, "gates_wide", [P, TASKS, BATCH])
        by_token = core.banks(stack, "gates_by_token_psum", 1)
        by_task = core.banks(stack, "gates_by_task_psum", 2)
        wide = core.banks(stack, "gates_wide_psum", 1)
        own_step = core.sem(stack, "gates_own_step")
        mean_ready = core.sem(stack, "gates_mean_ready")
        products_ready = core.sem(stack, "gates_products_ready")
        wide_ready = core.sem(stack, "gates_wide_ready")
        DVE_TASKS = 5
        with core.block() as block:
            def scale_rows(eng, e):
                return eng.tensor_tensor(
                    scaled_t[:, e].rearrange("p c (b s) -> p c b s", s=SEQ),
                    xn_t[:].rearrange("p c (b s) -> p c b s", s=SEQ),
                    gates_wide[:, e].unsqueeze(1).unsqueeze(3).to_broadcast([P, CHUNKS, BATCH, SEQ]), ALU.mult)

            @block.vector
            def _(dve):
                nc.vector.reduce_sum(mean[:].rearrange("p c b -> p (c b)"),
                                     gate_t[:].rearrange("p c (b s) -> p (c b) s", s=SEQ), axis=AX).then_inc(own_step, 1)
                dve.wait_ge(own_step, 1)
                nc.vector.tensor_scalar(mean[:], mean[:], 1.0 / SEQ, None, ALU.mult).then_inc(own_step, 1)
                dve.wait_ge(own_step, 2)
                nc.vector.tensor_copy(mean_tokens[:].rearrange("p c (b s) -> p (c b) s", s=SEQ),
                                      mean[:].rearrange("p c b -> p (c b)").unsqueeze(2).to_broadcast([P, CHUNKS * BATCH, SEQ])).then_inc(mean_ready, 1)
                nc.vector.memset(gates_by_token[:, :, 0], 1.0)
                dve.wait_ge(products_ready, 1)
                nc.vector.tensor_tensor(gates_wide[:], wide[:, 0, 0:TASKS * BATCH].rearrange("p (e b) -> p e b", b=BATCH),
                                        gb2[:].unsqueeze(2).to_broadcast([P, TASKS, BATCH]), ALU.add).then_inc(wide_ready, 1)
                dve.wait_ge(products_ready, 3)
                nc.vector.tensor_tensor(gates_by_token[:, :, 1:PARTS], by_token[:, 0, 0:TILES * TASKS].rearrange("p (t e) -> p t e", e=TASKS),
                                        gb2[:].unsqueeze(1).to_broadcast([P, TILES, TASKS]), ALU.add)
                nc.vector.tensor_scalar(gates_by_task[:].rearrange("p (b n) -> p b n", b=HALVES), by_task[0:TASKS],
                                        gb2_column[:], None, ALU.add)
                dve.wait_ge(wide_ready, 1)
                for e in range(DVE_TASKS):
                    scale_rows(nc.vector, e)

            @block.gpsimd
            def _(pool):
                pool.wait_ge(wide_ready, 1)
                for e in range(DVE_TASKS, TASKS):
                    scale_rows(nc.gpsimd, e)

            @block.tensor
            def _(pe):
                pe.wait_ge(mean_ready, 1)
                for e in range(TASKS):
                    for k in range(CHUNKS):
                        last = nc.tensor.matmul(wide[:, 0, e * BATCH:(e + 1) * BATCH], gw2_wide[:, k, e, :], mean[:, k, :],
                                                start=k == 0, stop=k == CHUNKS - 1)
                last.then_inc(products_ready, 1)
                for t in range(TILES):
                    for k in range(CHUNKS):
                        last = nc.tensor.matmul(by_token[:, 0, t * TASKS:(t + 1) * TASKS], mean_tokens[:, k, t * P:(t + 1) * P],
                                                gw2[:, k, :], start=k == 0, stop=k == CHUNKS - 1)
                last.then_inc(products_ready, 1)
                for h in range(HALVES):
                    for k in range(CHUNKS):
                        last = nc.tensor.matmul(by_task[0:TASKS, h, :], gw2[:, k, :], mean_tokens[:, k, h * BANK:(h + 1) * BANK],
                                                start=k == 0, stop=k == CHUNKS - 1)
                last.then_inc(products_ready, 1)


def merged_up_block(core, xn_t, scaled_t, gates_by_task, hidden_t):
    nc, dram = core.nc, core.dram
    with ExitStack() as stack:
        slab = [core.sbuf(stack, f"up_slab{i}", [P, PARTS, CHUNKS, P]) for i in range(2)]
        task_bias = [core.sbuf(stack, f"up_task_bias{i}", [TASKS, P]) for i in range(2)]
        b1 = core.sbuf(stack, "up_b1", [P, HIDDEN_TILES])
        psum = [core.banks(stack, f"up_psum{i}", HALVES) for i in range(2)]
        b1_loaded = core.sem(stack, "up_b1_loaded")
        slab_loaded = [core.sem(stack, f"up_slab_loaded{i}") for i in range(2)]
        product_ready = core.sem(stack, "up_product_ready")
        hidden_ready = core.sem(stack, "up_hidden_ready")
        with core.block() as block:
            @block.sync
            def _(sp):
                def load(m, parity):
                    sp.dma_start(slab[parity][:], dram["ffn_w1"][ds(m, 1)].rearrange("o p e c n -> (o p) e c n")).then_inc(slab_loaded[parity], 16)
                    sp.dma_start(task_bias[parity][:], dram["ffn_tb1"][ds(m, 1)].rearrange("o e n -> (o e) n")).then_inc(slab_loaded[parity], 16)

                sp.dma_start(b1[:], dram["ffn_b1"]).then_inc(b1_loaded, 16)
                load(0, 0)
                load(1, 1)
                with sp.Fori(0, HIDDEN_TILES // 2 - 1) as j:
                    for parity in range(2):
                        used = sp.snap(HALVES * (2 * j + parity + 1))
                        sp.wait_ge(product_ready, used)
                        load(2 * j + parity + 2, parity)

            @block.tensor
            def _(pe):
                def tile(m, parity, first):
                    pe.wait_ge(slab_loaded[parity], 16 * (m - parity) + 32)
                    for h in range(HALVES):
                        if not first:
                            pe.wait_ge(hidden_ready, HALVES * (m - 2) + h + 1)
                        cols = slice(h * BANK, (h + 1) * BANK)
                        nc.tensor.matmul(psum[parity][:, h, :], task_bias[parity][:], gates_by_task[:, cols],
                                         start=True, stop=False)
                        for e in range(PARTS):
                            for k in range(CHUNKS):
                                rows = xn_t[:, k, cols] if e == 0 else scaled_t[:, e - 1, k, cols]
                                last = nc.tensor.matmul(psum[parity][:, h, :], slab[parity][:, e, k, :], rows,
                                                        start=False, stop=e == PARTS - 1 and k == CHUNKS - 1)
                        last.then_inc(product_ready, 1)

                tile(0, 0, True)
                tile(1, 1, True)
                with pe.Fori(1, HIDDEN_TILES // 2) as j:
                    tile(2 * j, 0, False)
                    tile(2 * j + 1, 1, False)

            @block.scalar
            def _(act):
                act.wait_ge(b1_loaded, 16)
                with act.Fori(0, HIDDEN_TILES // 2) as j:
                    for parity in range(2):
                        m = 2 * j + parity
                        for h in range(HALVES):
                            act.wait_ge(product_ready, HALVES * m + h + 1)
                            nc.scalar.activation(hidden_t[:, ds(m, 1), h * BANK:(h + 1) * BANK].rearrange("p o n -> p (o n)"),
                                                 psum[parity][:, h, :], ACT.Gelu_apprx_tanh,
                                                 bias=b1[:, ds(m, 1)]).then_inc(hidden_ready, 1)


def merged_down_block(core, hidden_t, gates_by_token, gates_by_task):
    nc, dram, x = core.nc, core.dram, core.x
    with ExitStack() as stack:
        slab = [core.sbuf(stack, f"down_slab{i}", [P, HIDDEN_TILES, DIM]) for i in range(2)]
        tb2 = core.sbuf(stack, "down_tb2", [TASKS, DIM])
        psum = core.banks(stack, "down_psum", TILES)
        tb2_loaded = core.sem(stack, "down_tb2_loaded")
        slab_loaded = [core.sem(stack, f"down_slab_loaded{i}") for i in range(2)]
        product_ready = core.sem(stack, "down_product_ready")
        added = core.sem(stack, "down_added")
        with core.block() as block:
            @block.sync
            def _(sp):
                def load(e, parity):
                    sp.dma_start(slab[parity][:], dram["ffn_w2"][ds(e, 1)].rearrange("o p k n -> (o p) k n")).then_inc(slab_loaded[parity], 16)

                sp.dma_start(tb2[:], dram["ffn_tb2"]).then_inc(tb2_loaded, 16)
                load(0, 0)
                load(1, 1)
                with sp.Fori(0, PARTS // 2 - 1) as j:
                    for parity in range(2):
                        used = sp.snap(TILES * (2 * j + parity + 1))
                        sp.wait_ge(product_ready, used)
                        load(2 * j + parity + 2, parity)
                sp.wait_ge(product_ready, TILES * (PARTS - 2))
                load(PARTS - 1, 0)

            @block.tensor
            def _(pe):
                def part(e, parity, first):
                    pe.wait_ge(slab_loaded[parity], 8 * (e - parity) + 16)
                    for t in range(TILES):
                        if not first:
                            pe.wait_ge(added, TILES * (e - 1) + t + 1)
                        for k in range(HIDDEN_TILES):
                            last = nc.tensor.matmul(psum[:, t, 0:DIM], hidden_t[:, k, t * P:(t + 1) * P], slab[parity][:, k, :],
                                                    start=k == 0, stop=k == HIDDEN_TILES - 1 and not first)
                        if first:
                            last = nc.tensor.matmul(psum[:, t, 0:DIM], gates_by_task[:, t * P:(t + 1) * P], tb2[:],
                                                    start=False, stop=True)
                        last.then_inc(product_ready, 1)

                pe.wait_ge(tb2_loaded, 16)
                part(0, 0, True)
                with pe.Fori(0, PARTS // 2) as j:
                    part(2 * j + 1, 1, False)
                    part(2 * j + 2, 0, False)

            @block.vector
            def _(dve):
                def part(e, first):
                    for t in range(TILES):
                        dve.wait_ge(product_ready, TILES * e + t + 1)
                        if not first:
                            dve.wait_ge(added, TILES * (e - 1) + t + 1)
                        nc.vector.scalar_tensor_tensor(x[:, t, :], psum[:, t, 0:DIM], gates_by_token[:, t, ds(e, 1)],
                                                       x[:, t, :], ALU.mult, ALU.add).then_inc(added, 1)

                part(0, True)
                with dve.Fori(1, PARTS) as e:
                    part(e, False)



def value_tasks(nc, xn_t, wv, v_rows, cols=DIM):
    tasks = []
    per_unit = 4
    for b0 in range(0, BATCH, per_unit):
        products = [(lambda u, i=i: u[0:SEQ, i // 2, (i % 2) * cols:(i % 2 + 1) * cols],
                     xn_t[:, k, (b0 + i) * SEQ:(b0 + i + 1) * SEQ], wv[:, k, :], k == 0, k == CHUNKS - 1)
                    for i in range(per_unit) for k in range(CHUNKS)]

        def move(unit, step, b0=b0):
            return nc.scalar.activation(v_rows[:, b0:b0 + per_unit, :].rearrange("s (h b) c -> s h (b c)", h=2),
                                        unit[0:SEQ], ACT.Copy)

        tasks.append((products, move, "act"))
    return tasks


def self_attention_block(core, name, q_t, k_t, v_rows, bias, bv, heads_t):
    nc = core.nc
    SCALE = float(HEAD_DIM) ** -0.5
    with ExitStack() as stack:
        def sb(n, shape):
            return core.sbuf(stack, f"{name}_{n}", shape)

        def sem(n):
            return core.sem(stack, f"{name}_{n}")

        q_blocks = [sb(f"q_blocks{i}", [P, GROUPS, GROUP_HEADS, SEQ]) for i in range(2)]
        v = [sb(f"v{i}", [SEQ, DIM]) for i in range(2)]
        logits = [sb(f"logits{i}", [P, PAIRS, SEQ]) for i in range(2)]
        probs = [sb(f"probs{i}", [P, PAIRS, SEQ]) for i in range(2)]
        probs_t = sb("probs_t", [SEQ, PAIRS, P])
        maxima, sums = sb("maxima", [P, PAIRS]), sb("sums", [P, PAIRS])
        mixed = sb("mixed", [P, GROUPS, SEQ])
        scores = [core.banks(stack, f"{name}_scores{i}", 1) for i in range(2)]
        turned = core.banks(stack, f"{name}_turned", 1)
        weighed = core.banks(stack, f"{name}_weighed", 1)

        blocks_ready = sem("blocks_ready")
        values_ready = sem("values_ready")
        scored = sem("scored")
        logits_ready = sem("logits_ready")
        maxima_ready = sem("maxima_ready")
        shifted = sem("shifted")
        exp_done = sem("exp_done")
        sums_ready = sem("sums_ready")
        inverses_ready = sem("inverses_ready")
        probs_ready = sem("probs_ready")
        turned_ready = sem("turned_ready")
        turned_moved = sem("turned_moved")
        weighed_ready = sem("weighed_ready")
        mixed_ready = sem("mixed_ready")
        heads_ready = sem("heads_ready")

        with core.block() as block:
            @block.gpsimd
            def _(pool):
                def blocks(b, parity, wait):
                    if wait:
                        pool.wait_ge(scored, b - 1)
                    for g in range(GROUPS):
                        last = nc.gpsimd.tensor_tensor(
                            q_blocks[parity][:, g],
                            q_t[:, g, ds(b * SEQ, SEQ)].unsqueeze(1).to_broadcast([P, GROUP_HEADS, SEQ]),
                            core.head_mask[:].unsqueeze(2).to_broadcast([P, GROUP_HEADS, SEQ]), ALU.mult)
                    last.then_inc(blocks_ready, 1)

                def values(b, parity, wait):
                    if wait:
                        pool.wait_ge(weighed_ready, b - 1)
                    nc.gpsimd.tensor_copy(v[parity][:], v_rows[:, ds(b, 1), :].rearrange("s o c -> s (o c)")).then_inc(values_ready, 1)

                for b in range(2):
                    blocks(b, b, False)
                    values(b, b, False)
                with pool.Fori(1, BATCH // 2) as j:
                    for parity in range(2):
                        blocks(2 * j + parity, parity, True)
                        values(2 * j + parity, parity, True)

            @block.tensor
            def _(pe):
                def score(b, parity, pairs):
                    for n in pairs:
                        g, p = divmod(n, GROUP_PAIRS)
                        last = nc.tensor.matmul(scores[parity][:, 0, n * SEQ:(n + 1) * SEQ],
                                                q_blocks[parity][:, g, 2 * p:2 * p + 2, :].rearrange("p h q -> p (h q)"),
                                                k_t[:, g, ds(b * SEQ, SEQ)], start=True, stop=True)
                    if pairs[-1] == PAIRS - 1:
                        last.then_inc(scored, 1)

                def turn_and_weigh(b, parity, first, score_next):
                    pe.wait_ge(values_ready, b + 1)
                    pe.wait_ge(probs_ready, b + 1)
                    if not first:
                        pe.wait_ge(turned_moved, b)
                        pe.wait_ge(heads_ready, b)
                    for n in range(0, PAIRS, 2):
                        last = nc.tensor.transpose(turned[:, 0, n // 2 * P:(n // 2 + 1) * P],
                                                   probs[parity][:, n:n + 2, :].rearrange("p n k -> p (n k)"), core.ident[:])
                    last.then_inc(turned_ready, 1)
                    if score_next:
                        pe.wait_ge(blocks_ready, b + 3)
                        pe.wait_ge(logits_ready, b + 1)
                        score(b + 2, parity, range(0, PAIRS // 2))
                    pe.wait_ge(turned_moved, b + 1)
                    if score_next:
                        score(b + 2, parity, range(PAIRS // 2, PAIRS))
                    for n in range(PAIRS):
                        g, p = divmod(n, GROUP_PAIRS)
                        last = nc.tensor.matmul(weighed[32 * p:32 * (p + 1), 0, g * P:(g + 1) * P],
                                                v[parity][:, 32 * n:32 * (n + 1)], probs_t[:, n, :],
                                                start=True, stop=True, skip_group_check=True)
                    last.then_inc(weighed_ready, 1)

                for b in range(2):
                    pe.wait_ge(blocks_ready, b + 1)
                    score(b, b, range(PAIRS))
                turn_and_weigh(0, 0, True, True)
                turn_and_weigh(1, 1, False, True)
                with pe.Fori(1, BATCH // 2 - 1) as j:
                    turn_and_weigh(2 * j, 0, False, True)
                    turn_and_weigh(2 * j + 1, 1, False, True)
                turn_and_weigh(BATCH - 2, 0, False, False)
                turn_and_weigh(BATCH - 1, 1, False, False)

            @block.vector
            def _(dve):
                def shift(b, parity, first):
                    dve.wait_ge(scored, b + 1)
                    if not first:
                        dve.wait_ge(exp_done, b - 1)
                    nc.vector.scalar_tensor_tensor(
                        logits[parity][:].rearrange("p n k -> p (n k)"), scores[parity][:, 0, :], SCALE,
                        bias[:].rearrange("p n k -> p (n k)"), ALU.mult, ALU.add).then_inc(logits_ready, 1)
                    dve.wait_ge(logits_ready, b + 1)
                    nc.vector.reduce_max(maxima[:], logits[parity][:], axis=AX).then_inc(maxima_ready, 1)
                    dve.wait_ge(maxima_ready, b + 1)
                    nc.vector.tensor_tensor(logits[parity][:], logits[parity][:],
                                            maxima[:].unsqueeze(2).to_broadcast([P, PAIRS, SEQ]), ALU.subtract).then_inc(shifted, 1)

                def normalise(b, parity, first):
                    dve.wait_ge(exp_done, b + 1)
                    nc.vector.reduce_sum(sums[:], probs[parity][:], axis=AX).then_inc(sums_ready, 1)
                    dve.wait_ge(sums_ready, b + 1)
                    nc.vector.reciprocal(sums[:], sums[:]).then_inc(inverses_ready, 1)
                    dve.wait_ge(inverses_ready, b + 1)
                    nc.vector.tensor_tensor(probs[parity][:], probs[parity][:],
                                            sums[:].unsqueeze(2).to_broadcast([P, PAIRS, SEQ]), ALU.mult).then_inc(probs_ready, 1)

                def keep_heads(b):
                    dve.wait_ge(weighed_ready, b + 1)
                    psum = weighed[:, 0, 0:GROUPS * P].rearrange("p (g n) -> p g n", g=GROUPS)
                    if bv is None:
                        last = nc.vector.tensor_scalar(mixed[:], psum[:, :, 0:SEQ], core.even_head[:], None, ALU.mult)
                    else:
                        for g in range(GROUPS):
                            last = nc.vector.tensor_scalar(mixed[:, g], psum[:, g, 0:SEQ], core.even_head[:], bv[:, g:g + 1],
                                                           ALU.mult, ALU.add)
                    last.then_inc(mixed_ready, 1)
                    dve.wait_ge(mixed_ready, b + 1)
                    nc.vector.scalar_tensor_tensor(heads_t[:, :, ds(b * SEQ, SEQ)], psum[:, :, SEQ:2 * SEQ],
                                                   core.odd_head[:], mixed[:], ALU.mult, ALU.add).then_inc(heads_ready, 1)

                shift(0, 0, True)
                shift(1, 1, True)
                normalise(0, 0, True)
                with dve.Fori(1, BATCH // 2) as j:
                    shift(2 * j, 0, False)
                    normalise(2 * j - 1, 1, False)
                    keep_heads(2 * j - 2)
                    shift(2 * j + 1, 1, False)
                    normalise(2 * j, 0, False)
                    keep_heads(2 * j - 1)
                normalise(BATCH - 1, 1, False)
                keep_heads(BATCH - 2)
                keep_heads(BATCH - 1)

            @block.scalar
            def _(act):
                def exp(b, parity, first):
                    act.wait_ge(shifted, b + 1)
                    if not first:
                        act.wait_ge(turned_ready, b - 1)
                    nc.scalar.activation(probs[parity][:], logits[parity][:], ACT.Exp).then_inc(exp_done, 1)

                def move_turned(b, first):
                    act.wait_ge(turned_ready, b + 1)
                    if not first:
                        act.wait_ge(weighed_ready, b)
                    halves = probs_t[:].rearrange("s (n two) q -> s n two q", two=2)
                    for i in range(2):
                        last = nc.scalar.activation(halves[:, :, i, :],
                                                    turned[i * SEQ:(i + 1) * SEQ, 0, :].rearrange("s (n q) -> s n q", q=P), ACT.Copy)
                    last.then_inc(turned_moved, 1)

                exp(0, 0, True)
                exp(1, 1, True)
                move_turned(0, True)
                with act.Fori(1, BATCH // 2) as j:
                    exp(2 * j, 0, False)
                    move_turned(2 * j - 1, False)
                    exp(2 * j + 1, 1, False)
                    move_turned(2 * j, False)
                move_turned(BATCH - 1, False)


def alibi_attention(core):
    nc, dram, x = core.nc, core.dram, core.x
    with ExitStack() as stack:
        def sb(name, shape):
            return core.sbuf(stack, f"alibi_{name}", shape)

        wq, wk, wv, wo = (sb(n, [P, CHUNKS, DIM]) for n in ("wq", "wk", "wv", "wo"))
        bq, bk, bv = (sb(n, [P, CHUNKS]) for n in ("bq", "bk", "bv"))
        bo = sb("bo", [P, DIM])
        distance, slopes = sb("distance", [P, SEQ]), sb("slopes", [P, PAIRS])
        bias = sb("bias", [P, PAIRS, SEQ])
        xn, xn_t = sb("xn", [P, TILES, DIM]), sb("xn_t", [P, CHUNKS, TOKENS])
        q_t, k_t = sb("q_t", [P, CHUNKS, TOKENS]), sb("k_t", [P, CHUNKS, TOKENS])
        v_rows, heads_t = sb("v_rows", [SEQ, BATCH, DIM]), sb("heads_t", [P, CHUNKS, TOKENS])
        load_block(core, "alibi_weights",
                   [(t[:], dram[f"L1_attn_{n}"]) for t, n in ((wq, "wq"), (wk, "wk"), (wv, "wv"), (wo, "wo"), (bq, "bq"),
                                                              (bk, "bk"), (bv, "bv"), (slopes, "slopes"))]
                   + [(distance[:], dram["distance"]), (bo[:], dram["L1_attn_bo"].partition_broadcast(P))])
        with core.block() as block:
            @block.gpsimd
            def _(pool):
                nc.gpsimd.tensor_tensor(bias[:], distance[:].unsqueeze(1).to_broadcast([P, PAIRS, SEQ]),
                                        slopes[:].unsqueeze(2).to_broadcast([P, PAIRS, SEQ]), ALU.mult)
        norm_block(core, "alibi_norm", x, xn, xn_t, True)
        add_bias_block(core, "alibi_out_bias", bo)
        project_feature_major(core, "alibi_qk", [(wq, CHUNKS, xn_t, q_t, bq, False), (wk, CHUNKS, xn_t, k_t, bk, False)])
        dense_block(core, "alibi_v", value_tasks(nc, xn_t, wv, v_rows))
        self_attention_block(core, "alibi", q_t, k_t, v_rows, bias, bv, heads_t)
        add_projection(core, "alibi_out", heads_t, CHUNKS, wo, x)



EXPERTS = 8
EXPERT_HIDDEN = 512
EXPERT_TILES = EXPERT_HIDDEN // P
LIMIT = 100.0


def rotary_tasks(core, name, stack, xn_t, weights, swapped, cos, sin, dst):
    nc = core.nc
    parts = [[core.sbuf(stack, f"{name}_part_{n}{i}", [P, BANK // SEQ, SEQ]) for n in ("cos", "sin")] for i in range(2)]
    tasks = []
    for m in range(CHUNKS):
        for h in range(HALVES):
            products = [(lambda u, i=i: u[:, i, :], w[:, k, m * P:(m + 1) * P], xn_t[:, k, h * BANK:(h + 1) * BANK],
                         k == 0, k == CHUNKS - 1) for i, w in enumerate((weights, swapped)) for k in range(CHUNKS)]

            def move(unit, step, m=m, h=h):
                views = [unit[:, i, :].rearrange("p (b s) -> p b s", s=SEQ) for i in range(2)]
                shape = [P, BANK // SEQ, SEQ]
                part_cos, part_sin = parts[h % 2]
                nc.vector.tensor_tensor(part_cos[:], views[0], cos[:].unsqueeze(1).to_broadcast(shape), ALU.mult)
                step(nc.vector.tensor_tensor(part_sin[:], views[1], sin[:].unsqueeze(1).to_broadcast(shape), ALU.mult))
                last = nc.vector.tensor_tensor(dst[:, m, h * BANK:(h + 1) * BANK].rearrange("p (b s) -> p b s", s=SEQ),
                                               part_cos[:], part_sin[:], ALU.add)
                return last

            tasks.append((products, move, "dve"))
    return tasks


def moe_layer(core):
    nc, dram, x = core.nc, core.dram, core.x
    with ExitStack() as outer:
        def sb(stack, name, shape):
            return core.sbuf(stack, f"moe_{name}", shape)

        h = sb(outer, "h", [P, TILES, DIM])
        hn_t = sb(outer, "hn_t", [P, CHUNKS, TOKENS])
        hn = sb(outer, "hn", [P, TILES, DIM])
        ln2 = sb(outer, "ln2", [P, CHUNKS])
        router = sb(outer, "router", [P, CHUNKS, EXPERTS])
        order = sb(outer, "order", [P, EXPERTS])
        with ExitStack() as inner:
            wq, wq_swapped, wk, wk_swapped, wv, wo = (
                sb(inner, n, [P, CHUNKS, DIM]) for n in ("wq", "wq_swapped", "wk", "wk_swapped", "wv", "wo"))
            ln1 = sb(inner, "ln1", [P, CHUNKS])
            cos, sin = sb(inner, "cos", [P, SEQ]), sb(inner, "sin", [P, SEQ])
            causal = sb(inner, "causal", [P, PAIRS, SEQ])
            q_t, k_t = sb(inner, "q_t", [P, CHUNKS, TOKENS]), sb(inner, "k_t", [P, CHUNKS, TOKENS])
            v_rows, heads_t = sb(inner, "v_rows", [SEQ, BATCH, DIM]), sb(inner, "heads_t", [P, CHUNKS, TOKENS])
            load_block(core, "moe_weights",
                       [(t[:], dram[f"L1_ffn_{n}"]) for t, n in (
                           (wq, "wq"), (wq_swapped, "wq_swapped"), (wk, "wk"), (wk_swapped, "wk_swapped"), (wv, "wv"),
                           (wo, "wo"), (ln1, "ln1"), (ln2, "ln2"), (router, "router"))]
                       + [(t[:], dram[n]) for t, n in ((cos, "cos"), (sin, "sin"), (causal, "causal"), (order, "order"))])
            norm_block(core, "moe_norm0", x, h, None, True)
            norm_block(core, "moe_norm1", h, hn, hn_t, False, ln1)
            dense_block(core, "moe_qk",
                        rotary_tasks(core, "moe_q", inner, hn_t, wq, wq_swapped, cos, sin, q_t)
                        + rotary_tasks(core, "moe_k", inner, hn_t, wk, wk_swapped, cos, sin, k_t))
            dense_block(core, "moe_v", value_tasks(nc, hn_t, wv, v_rows))
            self_attention_block(core, "moe_attn", q_t, k_t, v_rows, causal, None, heads_t)
            add_projection(core, "moe_out", heads_t, CHUNKS, wo, h)
        clip_block(core, h)
        norm_block(core, "moe_norm2", h, hn, hn_t, False, ln2)
        weights = sb(outer, "weights", [P, TILES, EXPERTS])
        router_block(core, hn_t, router, order, weights)
        experts_block(core, hn_t, weights, h)
        finish_block(core, h)


def clip_block(core, h):
    nc = core.nc
    with core.block() as block:
        @block.vector
        def _(dve):
            nc.vector.tensor_scalar(h[:], h[:], -LIMIT, LIMIT, ALU.max, ALU.min)


def finish_block(core, h):
    nc, x = core.nc, core.x
    with ExitStack() as stack:
        clipped = core.sem(stack, "finish_clipped")
        with core.block() as block:
            @block.vector
            def _(dve):
                nc.vector.tensor_scalar(h[:], h[:], -LIMIT, LIMIT, ALU.max, ALU.min).then_inc(clipped, 1)
                dve.wait_ge(clipped, 1)
                nc.vector.tensor_tensor(x[:], x[:], h[:], ALU.add)


def router_block(core, hn_t, router, order, weights):
    nc = core.nc
    shape = [P, TILES, EXPERTS]
    with ExitStack() as stack:
        def sb(name, s):
            return core.sbuf(stack, f"router_{name}", s)

        prob, rest, pick, key = sb("prob", shape), sb("rest", shape), sb("pick", shape), sb("key", shape)
        best = sb("best", [P, TILES])
        psum = core.banks(stack, "router_psum", 1)
        logits = psum[:, 0, 0:TILES * EXPERTS].rearrange("p (t e) -> p t e", e=EXPERTS)
        logits_ready = core.sem(stack, "router_logits_ready")
        shifted = core.sem(stack, "router_shifted")
        exp_done = core.sem(stack, "router_exp_done")
        own_step = core.sem(stack, "router_own_step")
        with core.block() as block:
            @block.tensor
            def _(pe):
                for t in range(TILES):
                    for k in range(CHUNKS):
                        last = nc.tensor.matmul(logits[:, t, :], hn_t[:, k, t * P:(t + 1) * P], router[:, k, :],
                                                start=k == 0, stop=k == CHUNKS - 1)
                last.then_inc(logits_ready, 1)

            @block.scalar
            def _(act):
                act.wait_ge(shifted, 1)
                nc.scalar.activation(prob[:], rest[:], ACT.Exp).then_inc(exp_done, 1)

            @block.vector
            def _(dve):
                steps = [0]

                def step(ins):
                    steps[0] += 1
                    ins.then_inc(own_step, 1)
                    dve.wait_ge(own_step, steps[0])

                wide = best[:].unsqueeze(2).to_broadcast(shape)
                orders = order[:].unsqueeze(1).to_broadcast(shape)
                dve.wait_ge(logits_ready, 1)
                step(nc.vector.reduce_max(best[:], logits, axis=AX))
                nc.vector.tensor_tensor(rest[:], logits, wide, ALU.subtract).then_inc(shifted, 1)
                dve.wait_ge(exp_done, 1)
                remaining = prob
                for choice in range(2):
                    step(nc.vector.reduce_max(best[:], remaining[:], axis=AX))
                    step(nc.vector.tensor_tensor(key[:], remaining[:], wide, ALU.is_equal))
                    step(nc.vector.tensor_tensor(key[:], key[:], orders, ALU.mult))
                    step(nc.vector.reduce_max(best[:], key[:], axis=AX))
                    step(nc.vector.tensor_tensor(pick[:], key[:], wide, ALU.is_equal))
                    if choice == 0:
                        step(nc.vector.scalar_tensor_tensor(
                            rest[:].rearrange("p t e -> p (t e)"), pick[:].rearrange("p t e -> p (t e)"), -2.0,
                            prob[:].rearrange("p t e -> p (t e)"), ALU.mult, ALU.add))
                        step(nc.vector.tensor_tensor(weights[:], pick[:], prob[:], ALU.mult))
                        remaining = rest
                    else:
                        step(nc.vector.tensor_tensor(key[:], pick[:], prob[:], ALU.mult))
                        step(nc.vector.tensor_tensor(weights[:], weights[:], key[:], ALU.add))
                step(nc.vector.reduce_sum(best[:], weights[:], axis=AX))
                step(nc.vector.reciprocal(best[:], best[:]))
                nc.vector.tensor_tensor(weights[:], weights[:], wide, ALU.mult)


def experts_block(core, hn_t, weights, h):
    nc, dram = core.nc, core.dram
    STEPS = EXPERT_TILES * HALVES
    assert STEPS == TILES
    with ExitStack() as stack:
        w_in = [core.sbuf(stack, f"experts_w_in{i}", [P, 2, CHUNKS, EXPERT_HIDDEN]) for i in range(2)]
        w_out = [core.sbuf(stack, f"experts_w_out{i}", [P, EXPERT_TILES, DIM]) for i in range(2)]
        hidden_t = [core.sbuf(stack, f"experts_hidden_t{i}", [P, EXPERT_TILES, TOKENS]) for i in range(2)]
        gate = [core.sbuf(stack, f"experts_gate{i}", [P, BANK]) for i in range(2)]
        ups = [core.banks(stack, f"experts_ups{i}", 2) for i in range(2)]
        downs = [core.banks(stack, f"experts_downs{i}", 1) for i in range(4)]
        in_loaded = [core.sem(stack, f"experts_in_loaded{i}") for i in range(2)]
        out_loaded = [core.sem(stack, f"experts_out_loaded{i}") for i in range(2)]
        ups_ready = core.sem(stack, "experts_ups_ready")
        gate_ready = core.sem(stack, "experts_gate_ready")
        hidden_ready = core.sem(stack, "experts_hidden_ready")
        downs_ready = core.sem(stack, "experts_downs_ready")
        added = core.sem(stack, "experts_added")

        def over_experts(eng, body):
            body(0, 0, True)
            body(1, 1, False)
            with eng.Fori(1, EXPERTS // 2) as j:
                body(2 * j, 0, False)
                body(2 * j + 1, 1, False)

        with core.block() as block:
            @block.sync
            def _(sp):
                def load_in(e, parity):
                    sp.dma_start(w_in[parity][:], dram["expert_in"][ds(e, 1)].rearrange("o p w c n -> (o p) w c n")).then_inc(in_loaded[parity], 16)

                def load_out(e, parity):
                    sp.dma_start(w_out[parity][:], dram["expert_out"][ds(e, 1)].rearrange("o p k n -> (o p) k n")).then_inc(out_loaded[parity], 16)

                for e in range(2):
                    load_in(e, e)
                    load_out(e, e)
                with sp.Fori(0, EXPERTS // 2 - 1) as j:
                    for parity in range(2):
                        used = sp.snap(STEPS * (2 * j + parity + 1))
                        sp.wait_ge(ups_ready, used)
                        load_in(2 * j + parity + 2, parity)
                        sp.wait_ge(downs_ready, used)
                        load_out(2 * j + parity + 2, parity)

            @block.tensor
            def _(pe):
                def up(e, parity, i):
                    m, half = divmod(i, HALVES)
                    n = STEPS * e + i
                    if i == 0:
                        pe.wait_ge(in_loaded[parity], 8 * (e - parity) + 16)
                    if not (isinstance(e, int) and n < 2):
                        pe.wait_ge(hidden_ready, n - 1)
                    for w in range(2):
                        for k in range(CHUNKS):
                            last = nc.tensor.matmul(ups[i % 2][:, w, :], w_in[parity][:, w, k, m * P:(m + 1) * P],
                                                    hn_t[:, k, half * BANK:(half + 1) * BANK], start=k == 0, stop=k == CHUNKS - 1)
                    last.then_inc(ups_ready, 1)

                def down(e, parity, t):
                    n = STEPS * e + t
                    if t == 0:
                        pe.wait_ge(out_loaded[parity], 8 * (e - parity) + 16)
                        pe.wait_ge(hidden_ready, STEPS * e + STEPS)
                    if not (isinstance(e, int) and n < 4):
                        pe.wait_ge(added, n - 3)
                    for k in range(EXPERT_TILES):
                        last = nc.tensor.matmul(downs[t % 4][:, 0, 0:DIM], hidden_t[parity][:, k, t * P:(t + 1) * P],
                                                w_out[parity][:, k, :], start=k == 0, stop=k == EXPERT_TILES - 1)
                    last.then_inc(downs_ready, 1)

                def expert(e, parity, first):
                    for i in range(STEPS):
                        up(e, parity, i)
                        if not first:
                            down(e - 1, 1 - parity, i)

                over_experts(pe, expert)
                for t in range(TILES):
                    down(EXPERTS - 1, 1, t)

            @block.scalar
            def _(act):
                def expert(e, parity, first):
                    for i in range(STEPS):
                        n = STEPS * e + i
                        act.wait_ge(ups_ready, n + 1)
                        if not (isinstance(e, int) and n < 2):
                            act.wait_ge(hidden_ready, n - 1)
                        nc.scalar.activation(gate[i % 2][:], ups[i % 2][:, 0, :], ACT.Silu).then_inc(gate_ready, 1)

                over_experts(act, expert)

            @block.vector
            def _(dve):
                def add(e, t):
                    dve.wait_ge(downs_ready, STEPS * e + t + 1)
                    if not isinstance(e, int) or e > 0:
                        dve.wait_ge(added, STEPS * e + t)
                    nc.vector.scalar_tensor_tensor(h[:, t, :], downs[t % 4][:, 0, 0:DIM], weights[:, t, ds(e, 1)],
                                                   h[:, t, :], ALU.mult, ALU.add).then_inc(added, 1)

                def expert(e, parity, first):
                    for i in range(STEPS):
                        m, half = divmod(i, HALVES)
                        n = STEPS * e + i
                        dve.wait_ge(gate_ready, n + 1)
                        if i == 0 and not (isinstance(e, int) and e < 2):
                            dve.wait_ge(downs_ready, STEPS * (e - 1))
                        nc.vector.tensor_tensor(hidden_t[parity][:, m, half * BANK:(half + 1) * BANK], gate[i % 2][:],
                                                ups[i % 2][:, 1, :], ALU.mult).then_inc(hidden_ready, 1)
                        if not first:
                            add(e - 1, i)

                over_experts(dve, expert)
                for t in range(TILES):
                    add(EXPERTS - 1, t)



def perceiver(nc, dram, out, first=0, last=6):
    core = Core(nc, dram)
    with ExitStack() as stack:
        core.x = core.sbuf(stack, "x", [P, TILES, DIM])
        core.ident = core.sbuf(stack, "ident", [P, P])
        core.head_mask = core.sbuf(stack, "head_mask", [P, GROUP_HEADS])
        core.even_head = core.sbuf(stack, "even_head", [P, 1])
        core.odd_head = core.sbuf(stack, "odd_head", [P, 1])
        load_block(core, "start", [(core.x[:], dram["x"]), (core.ident[:], dram["ident"]),
                                   (core.head_mask[:], dram["head_mask"]), (core.even_head[:], dram["even_head"]),
                                   (core.odd_head[:], dram["odd_head"])])
        stages = [
            lambda: cross_attention(core, "L0_xattn", 2, DIM),
            lambda: wide_attention(core),
            lambda: merged_ffn(core),
            lambda: cross_attention(core, "L1_xattn", 1, 2 * HEAD_DIM),
            lambda: alibi_attention(core),
            lambda: moe_layer(core),
        ]
        for stage in stages[first:last]:
            stage()
        store(core, out)


def store(core, out):
    nc = core.nc
    with ExitStack() as stack:
        stored = core.sem(stack, "stored")
        with core.block() as block:
            @block.sync
            def _(sp):
                sp.dma_start(out, core.x[:]).then_inc(stored, 16)
                sp.wait_ge(stored, 16)


def chunked(w, rows=P):
    k = w.shape[0]
    return w.reshape(k // rows, rows, w.shape[1]).transpose(1, 0, 2)


def column(b):
    return b.reshape(-1, P).T


def per_head(w, rows):
    return np.stack([chunked(w[:, h * WIDE_DIM:(h + 1) * WIDE_DIM], rows) for h in range(WIDE_HEADS)])


def layouts(i):
    rows = np.arange(P)
    lanes, query = rows // SEQ, rows % SEQ
    key = np.arange(SEQ)
    half_dim = HEAD_DIM // 2
    inverse = (1.0 / np.float32(10000.0) ** (np.arange(0, HEAD_DIM, 2, dtype=np.float32) / np.float32(HEAD_DIM))).astype(np.float32)
    angles = key.astype(np.float32)[None, :] * inverse[rows % half_dim][:, None]
    sign = np.where(rows % HEAD_DIM < half_dim, -1.0, 1.0).astype(np.float32)[:, None]
    swap = np.arange(DIM).reshape(HEADS, 2, half_dim)[:, ::-1].reshape(-1)
    d = {
        "x": i["x"].reshape(TILES, P, DIM).transpose(1, 0, 2),
        "ctx_t": i["ctx_1024"].transpose(0, 2, 1).reshape(BATCH, CHUNKS, P, KEYS).transpose(0, 2, 1, 3),
        "ident": np.eye(P, dtype=np.float32),
        "head_mask": (rows[:, None] // HEAD_DIM == np.arange(GROUP_HEADS)).astype(np.float32),
        "even_head": (rows[:, None] // HEAD_DIM % 2 == 0).astype(np.float32),
        "odd_head": (rows[:, None] // HEAD_DIM % 2 == 1).astype(np.float32),
        "distance": (key[None, :] - query[:, None]).astype(np.float32),
        "causal": np.broadcast_to(np.where(key[None, :] <= query[:, None], 0.0, -3.0e38).astype(np.float32)[:, None, :],
                                  (P, PAIRS, SEQ)),
        "cos": np.cos(angles).astype(np.float32),
        "sin": (np.sin(angles) * sign).astype(np.float32),
        "order": np.broadcast_to((EXPERTS - np.arange(EXPERTS)).astype(np.float32), (P, EXPERTS)),
    }
    for n in ("wq", "wk", "wv", "wo"):
        d[f"L0_xattn_{n}"] = chunked(i[f"L0_xattn_{n}"])
    for n in ("bq", "bk", "bv"):
        d[f"L0_xattn_{n}"] = column(i[f"L0_xattn_{n}"])
    d["L0_xattn_bo"] = i["L0_xattn_bo"]

    d["L0_attn_ctx_t"] = chunked(i["L0_attn_context"].reshape(WIDE_KEYS, 2 * CTX_ROWS).T, CTX_ROWS)
    d["L0_attn_wq"] = per_head(i["L0_attn_Wq"], P)
    d["L0_attn_wk"] = per_head(i["L0_attn_Wk"], CTX_ROWS)
    d["L0_attn_wv"] = per_head(i["L0_attn_Wv"], CTX_ROWS)
    d["L0_attn_wout"] = chunked(i["L0_attn_Wout"])
    d["L0_attn_bout"] = i["L0_attn_bout"]

    d["gate_w1"] = chunked(i["L0_ffn_gate_w1"].T)
    d["gate_b1"] = column(i["L0_ffn_gate_b1"])
    d["gate_w2"] = chunked(i["L0_ffn_gate_w2"].T)
    d["gate_w2_wide"] = np.broadcast_to(d["gate_w2"][:, :, :, None], (P, CHUNKS, TASKS, P))
    d["gate_b2"] = i["L0_ffn_gate_b2"]
    w1 = np.concatenate([i["L0_ffn_W1"][None], i["L0_ffn_TW1"]])
    d["ffn_w1"] = w1.reshape(PARTS, HIDDEN_TILES, P, CHUNKS, P).transpose(1, 4, 0, 3, 2)
    d["ffn_b1"] = column(i["L0_ffn_b1"])
    d["ffn_tb1"] = i["L0_ffn_Tb1"].reshape(TASKS, HIDDEN_TILES, P).transpose(1, 0, 2)
    w2 = np.concatenate([i["L0_ffn_W2"][None], i["L0_ffn_TW2"]])
    d["ffn_w2"] = w2.reshape(PARTS, DIM, HIDDEN_TILES, P).transpose(0, 3, 2, 1)
    d["ffn_b2"] = i["L0_ffn_b2"]
    d["ffn_tb2"] = i["L0_ffn_Tb2"]

    d["L1_xattn_wq"] = chunked(i["L1_xattn_Wq"].T)
    d["L1_xattn_wk"] = chunked(np.tile(i["L1_xattn_Wk"].T, (1, GROUP_HEADS)))
    d["L1_xattn_wv"] = chunked(np.tile(i["L1_xattn_Wv"].T, (1, 2)))
    d["L1_xattn_wo"] = chunked(i["L1_xattn_Wo"].T)
    d["L1_xattn_bq"] = column(i["L1_xattn_bq"])
    d["L1_xattn_bk"] = column(np.tile(i["L1_xattn_bk"], GROUP_HEADS))
    d["L1_xattn_bv"] = column(np.tile(i["L1_xattn_bv"], HEADS))
    d["L1_xattn_bo"] = i["L1_xattn_bo"]

    for n in ("q", "k", "v", "o"):
        d[f"L1_attn_w{n}"] = chunked(i[f"L1_attn_W{n}"].T)
    for n in ("q", "k", "v"):
        d[f"L1_attn_b{n}"] = column(i[f"L1_attn_b{n}"])
    d["L1_attn_bo"] = i["L1_attn_bo"]
    d["L1_attn_slopes"] = i["L1_attn_slopes"].reshape(PAIRS, 2).T[lanes]

    repeat = np.repeat(np.arange(4), HEADS // 4)
    def spread(w):
        return w.reshape(DIM, 4, HEAD_DIM)[:, repeat].reshape(DIM, DIM)
    wq, wk, wv = i["L1_ffn_Wq"], spread(i["L1_ffn_Wk"]), spread(i["L1_ffn_Wv"])
    d["L1_ffn_wq"], d["L1_ffn_wq_swapped"] = chunked(wq), chunked(wq[:, swap])
    d["L1_ffn_wk"], d["L1_ffn_wk_swapped"] = chunked(wk), chunked(wk[:, swap])
    d["L1_ffn_wv"], d["L1_ffn_wo"] = chunked(wv), chunked(i["L1_ffn_Wo"])
    d["L1_ffn_ln1"], d["L1_ffn_ln2"] = column(i["L1_ffn_ln1_w"]), column(i["L1_ffn_ln2_w"])
    d["L1_ffn_router"] = chunked(i["L1_ffn_Wr"])
    d["expert_in"] = np.stack([i["L1_ffn_Wg"], i["L1_ffn_Wu"]], 1).reshape(
        EXPERTS, 2, CHUNKS, P, EXPERT_HIDDEN).transpose(0, 3, 1, 2, 4)
    d["expert_out"] = i["L1_ffn_Wd"].reshape(EXPERTS, EXPERT_TILES, P, DIM).transpose(0, 2, 1, 3)
    return {k: np.ascontiguousarray(v) for k, v in d.items()}


def kernel(**inputs):
    import concourse.bacc as _bacc
    from concourse.bass_utils import run_bass_kernel_spmd as _run

    arrays = {f"in_{k}": v for k, v in layouts({k: np.asarray(v) for k, v in inputs.items()}).items()}
    nc = _bacc.Bacc("TRN2", target_bir_lowering=False, num_devices=1)
    dram = {k[3:]: nc.dram_tensor(k, v.shape, mybir.dt.from_np(v.dtype), kind="ExternalInput").ap()
            for k, v in arrays.items()}
    out = nc.dram_tensor("out", [P, TILES, DIM], F32, kind="ExternalOutput").ap()
    perceiver(nc, dram, out)
    r = _run(nc, [arrays], core_ids=[0])
    got = np.asarray(r.results[0]["out"])
    return np.ascontiguousarray(got.transpose(1, 0, 2)).reshape(BATCH, SEQ, DIM)
```

```python
from contextlib import ExitStack, contextmanager

import numpy as np
import concourse.bass as bass
from concourse import mybir

F32 = mybir.dt.float32
ALU = mybir.AluOpType
ACT = mybir.ActivationFunctionType
AX = mybir.AxisListType.X

P = 128
BATCH, SEQ, DIM = 16, 64, 256
TOKENS = BATCH * SEQ
TILES = TOKENS // P
CHUNKS = DIM // P
BANK = 512
HALVES = TOKENS // BANK
HEADS, HEAD_DIM = 16, 16
PAIRS = HEADS // 2
GROUP_PAIRS = 4
GROUPS = 2
GROUP_HEADS = 8
KEYS = 1601
KEY_TILES = -(-KEYS // P)
KEYS_PADDED = KEY_TILES * P
LAST_KEYS = KEYS - (KEY_TILES - 1) * P
LN_EPS = 1e-5
ds = bass.ds


class Core:

    def __init__(self, nc, dram):
        self.nc, self.dram = nc, dram
        self.counted = []

    @contextmanager
    def block(self):
        with self.nc.Block() as block:
            yield block
        numbers, self.counted = sorted(self.counted), []
        while numbers:
            n = 1
            while n < len(numbers) and numbers[n] == numbers[0] + n:
                n += 1
            self.nc.gpsimd.sem_clear(range(numbers[0], numbers[0] + n))
            numbers = numbers[n:]

    def sbuf(self, stack, name, shape, dtype=F32):
        return stack.enter_context(self.nc.sbuf_tensor(name, shape, dtype))

    def banks(self, stack, name, n):
        return stack.enter_context(self.nc.psum_tensor(name, [P, n, BANK], F32))

    def sem(self, stack, name):
        semaphore = stack.enter_context(self.nc.semaphore(name))
        self.counted.append(semaphore.num)
        return semaphore


def load_block(core, name, pairs):
    nc = core.nc
    with ExitStack() as stack:
        loaded = core.sem(stack, f"{name}_loaded")
        with core.block() as block:
            @block.sync
            def _(sp):
                for tile, view in pairs:
                    sp.dma_start(tile, view).then_inc(loaded, 16)
                sp.wait_ge(loaded, 16 * len(pairs))


def norm_block(core, name, src, dst, dst_t, centered, feature_scale=None):
    nc = core.nc
    with ExitStack() as stack:
        stats = core.sbuf(stack, f"{name}_stats", [P, TILES, 6])
        moments = core.sbuf(stack, f"{name}_moments", [P, TILES, 2])
        spread = core.sbuf(stack, f"{name}_spread", [P, 3, TILES])
        rstd = core.sbuf(stack, f"{name}_rstd", [P, TILES])
        turned = core.banks(stack, f"{name}_turned", 4)
        sums_done = core.sem(stack, f"{name}_sums_done")
        moments_ready = core.sem(stack, f"{name}_moments_ready")
        own_step = core.sem(stack, f"{name}_own_step")
        spread_ready = core.sem(stack, f"{name}_spread_ready")
        root_ready = core.sem(stack, f"{name}_root_ready")
        rows_ready = core.sem(stack, f"{name}_rows_ready")
        turned_ready = core.sem(stack, f"{name}_turned_ready")

        with core.block() as block:
            @block.vector
            def _(dve):
                steps = [0]

                def step(ins):
                    steps[0] += 1
                    ins.then_inc(own_step, 1)
                    dve.wait_ge(own_step, steps[0])

                for t in range(TILES):
                    nc.vector.bn_stats(stats[:, t, :], src[:, t, :]).then_inc(sums_done, 1)
                for t in range(TILES):
                    dve.wait_ge(sums_done, t + 1)
                    nc.vector.bn_aggr(moments[:, t, :], stats[:, t, :]).then_inc(moments_ready, 1)
                dve.wait_ge(moments_ready, TILES)
                step(nc.vector.tensor_scalar(spread[:, 0], moments[:, :, 1], LN_EPS, None, ALU.add))
                if not centered:
                    step(nc.vector.tensor_tensor(spread[:, 1], moments[:, :, 0], moments[:, :, 0], ALU.mult))
                    step(nc.vector.tensor_tensor(spread[:, 0], spread[:, 0], spread[:, 1], ALU.add))
                dve.sem_inc(spread_ready, 1)
                dve.wait_ge(root_ready, 1)
                step(nc.vector.reciprocal(spread[:, 2], spread[:, 1]))
                step(nc.vector.tensor_tensor(spread[:, 2], spread[:, 2], spread[:, 0], ALU.mult))
                step(nc.vector.tensor_tensor(spread[:, 2], spread[:, 2], spread[:, 1], ALU.add))
                step(nc.vector.tensor_scalar(spread[:, 2], spread[:, 2], 0.5, None, ALU.mult))
                step(nc.vector.reciprocal(rstd[:], spread[:, 2]))
                for t in range(TILES):
                    if centered:
                        ins = nc.vector.tensor_scalar(dst[:, t, :], src[:, t, :], moments[:, t, 0:1],
                                                      rstd[:, t:t + 1], ALU.subtract, ALU.mult)
                    else:
                        ins = nc.vector.tensor_scalar(dst[:, t, :], src[:, t, :], rstd[:, t:t + 1],
                                                      None, ALU.mult)
                    ins.then_inc(rows_ready, 1)

            @block.tensor
            def _(pe):
                for t in range(TILES if dst_t is not None else 0):
                    pe.wait_ge(rows_ready, t + 1)
                    for c in range(CHUNKS):
                        last = nc.tensor.transpose(
                            turned[:, HALVES * c + t // 4, (t % 4) * P:(t % 4 + 1) * P],
                            dst[:, t, c * P:(c + 1) * P], core.ident[:])
                    if t % 4 == 3:
                        last.then_inc(turned_ready, 1)

            @block.scalar
            def _(act):
                act.wait_ge(spread_ready, 1)
                nc.scalar.activation(spread[:, 1], spread[:, 0], ACT.Sqrt).then_inc(root_ready, 1)
                for half in range(HALVES if dst_t is not None else 0):
                    act.wait_ge(turned_ready, half + 1)
                    for c in range(CHUNKS):
                        scale = 1.0 if feature_scale is None else feature_scale[:, c:c + 1]
                        nc.scalar.activation(dst_t[:, c, half * BANK:(half + 1) * BANK],
                                             turned[:, HALVES * c + half, :], ACT.Copy if feature_scale is None else ACT.Identity,
                                             scale=scale)


def dense_block(core, name, tasks):
    nc = core.nc
    units = 4
    with ExitStack() as stack:
        psum = core.banks(stack, f"{name}_psum", 2 * units)
        products_ready = core.sem(stack, f"{name}_products_ready")
        moved = {on: core.sem(stack, f"{name}_moved_{on}") for on in ("dve", "act")}
        own_step = core.sem(stack, f"{name}_own_step")

        def moved_count(i):
            return sum(tasks[k][2] == tasks[i][2] for k in range(i + 1))

        with core.block() as block:
            @block.tensor
            def _(pe):
                for i, (products, _, on) in enumerate(tasks):
                    if i >= units:
                        pe.wait_ge(moved[tasks[i - units][2]], moved_count(i - units))
                    u = 2 * (i % units)
                    for part, lhs_t, rhs, start, stop in products:
                        last = nc.tensor.matmul(part(psum[:, u:u + 2, :]), lhs_t, rhs, start=start, stop=stop)
                    last.then_inc(products_ready, 1)

            @block.vector
            def _(dve):
                steps = [0]

                def step(ins):
                    steps[0] += 1
                    ins.then_inc(own_step, 1)
                    dve.wait_ge(own_step, steps[0])

                for i, (_, move, on) in enumerate(tasks):
                    if on == "dve":
                        dve.wait_ge(products_ready, i + 1)
                        move(psum[:, 2 * (i % units):2 * (i % units) + 2, :], step).then_inc(moved["dve"], 1)

            @block.scalar
            def _(act):
                for i, (_, move, on) in enumerate(tasks):
                    if on == "act":
                        act.wait_ge(products_ready, i + 1)
                        move(psum[:, 2 * (i % units):2 * (i % units) + 2, :], None).then_inc(moved["act"], 1)


def feature_products(weights, m, src_t, chunks=CHUNKS, rows=P, cols=P):
    return [(lambda u, h=h: u[0:cols, h, :], weights[:, k, m * cols:(m + 1) * cols],
             src_t[:, k, h * BANK:(h + 1) * BANK], k == 0, k == chunks - 1)
            for h in range(HALVES) for k in range(chunks)]


def project_feature_major(core, name, jobs):
    nc = core.nc
    tasks = []
    for weights, m_tiles, src_t, dst, bias, relu in jobs:
        for m in range(m_tiles):
            def move_dve(unit, step, m=m, dst=dst, bias=bias, relu=relu):
                out = dst[:, m, :].rearrange("p (h n) -> p h n", h=HALVES)
                if bias is None:
                    return nc.vector.tensor_copy(out, unit)
                if relu:
                    return nc.vector.tensor_scalar(out, unit, bias[:, m:m + 1], 0.0, ALU.add, ALU.max)
                return nc.vector.tensor_scalar(out, unit, bias[:, m:m + 1], None, ALU.add)

            def move_act(unit, step, m=m, dst=dst, bias=bias, relu=relu):
                out = dst[:, m, :].rearrange("p (h n) -> p h n", h=HALVES)
                func = ACT.Relu if relu else (ACT.Copy if bias is None else ACT.Identity)
                return nc.scalar.activation(out, unit, func, bias=0.0 if bias is None else bias[:, m:m + 1])

            on = ("dve", "act")[len(tasks) % 2]
            tasks.append((feature_products(weights, m, src_t), move_dve if on == "dve" else move_act, on))
    dense_block(core, name, tasks)


def add_projection(core, name, heads_t, chunks, weights, x):
    nc = core.nc
    tasks = []
    for t in range(TILES):
        products = [(lambda u: u[:, 0, 0:DIM], heads_t[:, k, t * P:(t + 1) * P], weights[:, k, :],
                     k == 0, k == chunks - 1) for k in range(chunks)]

        def move(unit, step, t=t):
            return nc.vector.tensor_tensor(x[:, t, :], unit[:, 0, 0:DIM], x[:, t, :], ALU.add)

        tasks.append((products, move, "dve"))
    dense_block(core, name, tasks)



A_COLS = 2 * BANK
B_COLS = KEYS - A_COLS
K_STARTS = list(range(0, KEYS, BANK))
EVEN_KEYS = KEYS + KEYS % 2


def cross_attention(core, layer, key_groups, value_cols):
    nc, dram, x = core.nc, core.dram, core.x
    v_rows_cols = value_cols
    with ExitStack() as outer:
        def sb(name, shape):
            return core.sbuf(outer, f"{layer}_{name}", shape)

        wq, wo = sb("wq", [P, CHUNKS, DIM]), sb("wo", [P, CHUNKS, DIM])
        wk, wv = sb("wk", [P, CHUNKS, key_groups * P]), sb("wv", [P, CHUNKS, value_cols])
        bq, bk, bv = sb("bq", [P, GROUPS]), sb("bk", [P, key_groups]), sb("bv", [P, GROUPS])
        bo = sb("bo", [P, DIM])
        q_t, heads_t = sb("q_t", [P, GROUPS, TOKENS]), sb("heads_t", [P, GROUPS, TOKENS])
        load_block(core, f"{layer}_weights", [
            (wq[:], dram[f"{layer}_wq"]), (wo[:], dram[f"{layer}_wo"]), (wk[:], dram[f"{layer}_wk"]),
            (wv[:], dram[f"{layer}_wv"]), (bq[:], dram[f"{layer}_bq"]), (bk[:], dram[f"{layer}_bk"]),
            (bv[:], dram[f"{layer}_bv"]), (bo[:], dram[f"{layer}_bo"].partition_broadcast(P))])
        with ExitStack() as inner:
            xn = core.sbuf(inner, f"{layer}_xn", [P, TILES, DIM])
            xn_t = core.sbuf(inner, f"{layer}_xn_t", [P, CHUNKS, TOKENS])
            norm_block(core, f"{layer}_norm", x, xn, xn_t, True)
            project_feature_major(core, f"{layer}_q", [(wq, GROUPS, xn_t, q_t, bq, False)])
        cross_attention_block(core, layer, key_groups, value_cols, wk, bk, wv, bv, bo, q_t, heads_t)
        add_projection(core, f"{layer}_out", heads_t, CHUNKS, wo, x)


def cross_attention_block(core, layer, key_groups, value_cols, wk, bk, wv, bv, bo, q_t, heads_t):
    nc, dram, x = core.nc, core.dram, core.x
    SCALE = float(HEAD_DIM) ** -0.5
    v_per_unit = min(KEY_TILES, BANK // value_cols)
    k_units = [(g, s) for s in K_STARTS for g in range(key_groups)]
    v_units = [list(range(t, min(t + v_per_unit, KEY_TILES))) for t in range(0, KEY_TILES, v_per_unit)]
    units = k_units + v_units
    U = len(units)
    slots = [[] for _ in range(2 * PAIRS)]
    if key_groups == 2:
        for i in range(U):
            slots[i].append(i)
    else:
        for i in range(len(k_units)):
            slots[2 * i].append(i)
        slots[8].append(len(k_units))
    assert all(u < len(k_units) for s in slots[:4] for u in s)
    units_before = [sum(len(s) for s in slots[:i]) for i in range(2 * PAIRS)]

    with ExitStack() as stack:
        def sb(name, shape):
            return core.sbuf(stack, f"{layer}_{name}", shape)

        def sem(name):
            return core.sem(stack, f"{layer}_{name}")

        ctx = [sb(f"ctx{i}", [P, CHUNKS, EVEN_KEYS]) for i in range(2)]
        k_t = [sb(f"k_t{i}", [P, key_groups, KEYS]) for i in range(2)]
        v = [sb(f"v{i}", [P, KEY_TILES, value_cols]) for i in range(2)]
        q_blocks = [sb(f"q_blocks{i}", [P, GROUPS, GROUP_HEADS, SEQ]) for i in range(2)]
        probs = [sb(f"probs{i}", [P, KEYS_PADDED]) for i in range(2)]
        probs_t = sb("probs_t", [P, KEY_TILES, GROUP_PAIRS * P])
        maxima = [sb(f"maxima{i}", [P, 4]) for i in range(2)]
        sums = [sb(f"sums{i}", [P, 4]) for i in range(2)]
        mixed = sb("mixed", [P, SEQ])
        scores = core.banks(stack, f"{layer}_scores", 4)
        turned = core.banks(stack, f"{layer}_turned", 2)
        projected = core.banks(stack, f"{layer}_projected", 1)
        weighed = core.banks(stack, f"{layer}_weighed", 1)
        scores_flat = scores[:].rearrange("p b n -> p (b n)")
        turned_tiles = turned[:].rearrange("p b (t n) -> p (b t) n", n=P)

        ctx_loaded = [sem(f"ctx_loaded{i}") for i in range(2)]
        pads_zeroed = sem("pads_zeroed")
        blocks_ready = sem("blocks_ready")
        projection_done = sem("projection_done")
        projection_moved = sem("projection_moved")
        scored = sem("scored")
        halves_maxed = sem("halves_maxed")
        bias_ready = sem("bias_ready")
        exps_done = sem("exps_done")
        sum_steps = sem("sum_steps")
        probs_ready = sem("probs_ready")
        turned_ready = sem("turned_ready")
        turned_moved = sem("turned_moved")
        weighed_ready = sem("weighed_ready")
        mixed_ready = sem("mixed_ready")
        heads_ready = sem("heads_ready")

        def over_batches(eng, body):
            body(0, 0, True, False)
            body(1, 1, False, False)
            with eng.Fori(1, BATCH // 2 - 1) as j:
                body(2 * j, 0, False, False)
                body(2 * j + 1, 1, False, False)
            body(BATCH - 2, 0, False, False)
            body(BATCH - 1, 1, False, True)

        with core.block() as block:
            @block.sync
            def _(sp):
                sp.dma_start(ctx[0][:], dram["ctx_t"][0]).then_inc(ctx_loaded[0], 16)
                sp.dma_start(ctx[1][:], dram["ctx_t"][1]).then_inc(ctx_loaded[1], 16)
                with sp.Fori(0, BATCH // 2 - 1) as j:
                    for parity in range(2):
                        used = sp.snap(U * (2 * j + parity + 1))
                        sp.wait_ge(projection_done, used)
                        sp.dma_start(ctx[parity][:], dram["ctx_t"][ds(2 * j + parity + 2, 1)].rearrange("o p c n -> (o p) c n")).then_inc(ctx_loaded[parity], 16)

            @block.gpsimd
            def _(pool):
                for i in range(2):
                    nc.gpsimd.memset(probs[i][:, KEYS:KEYS_PADDED], 0.0).then_inc(pads_zeroed, 1)
                nc.gpsimd.tensor_tensor(x[:], x[:], bo[:].unsqueeze(1).to_broadcast([P, TILES, DIM]), ALU.add)

                def blocks(b, parity, wait):
                    if wait:
                        pool.wait_ge(scored, 2 * PAIRS * (b - 1))
                    for g in range(GROUPS):
                        last = nc.gpsimd.tensor_tensor(
                            q_blocks[parity][:, g],
                            q_t[:, g, ds(b * SEQ, SEQ)].unsqueeze(1).to_broadcast([P, GROUP_HEADS, SEQ]),
                            core.head_mask[:].unsqueeze(2).to_broadcast([P, GROUP_HEADS, SEQ]), ALU.mult)
                    last.then_inc(blocks_ready, 1)

                blocks(0, 0, False)
                blocks(1, 1, False)
                with pool.Fori(1, BATCH // 2) as j:
                    blocks(2 * j, 0, True)
                    blocks(2 * j + 1, 1, True)

            @block.tensor
            def _(pe):
                def project(b, parity, u):
                    n = U * b + u
                    if u == 0:
                        pe.wait_ge(ctx_loaded[parity], 8 * (b - parity) + 16)
                    if not (isinstance(b, int) and n == 0):
                        pe.wait_ge(projection_moved, n)
                    if u < len(k_units):
                        g, s = k_units[u]
                        w = min(BANK, KEYS - s)
                        for k in range(CHUNKS):
                            last = nc.tensor.matmul(projected[:, 0, 0:w], wk[:, k, g * P:(g + 1) * P],
                                                    ctx[parity][:, k, s:s + w], start=k == 0, stop=k == CHUNKS - 1)
                    else:
                        for i, t in enumerate(v_units[u - len(k_units)]):
                            rows = P if t < KEY_TILES - 1 else LAST_KEYS
                            for k in range(CHUNKS):
                                last = nc.tensor.matmul(
                                    projected[0:rows, 0, i * value_cols:(i + 1) * value_cols],
                                    ctx[parity][:, k, t * P:t * P + rows], wv[:, k, :],
                                    start=k == 0, stop=k == CHUNKS - 1)
                    last.then_inc(projection_done, 1)

                def score(b, parity, n, half):
                    pair = PAIRS * b + n
                    g = n // GROUP_PAIRS
                    if not (isinstance(b, int) and pair == 0):
                        pe.wait_ge(exps_done, 2 * pair - 1 + half)
                    heads = q_blocks[parity][:, g, 2 * (n % GROUP_PAIRS):2 * (n % GROUP_PAIRS) + 2, :]
                    for s in K_STARTS[2 * half:2 * half + 2]:
                        w = min(BANK, KEYS - s)
                        last = nc.tensor.matmul(scores[:, s // BANK, 0:w], heads.rearrange("p h q -> p (h q)"),
                                                k_t[parity][:, g % key_groups, s:s + w], start=True, stop=True)
                    last.then_inc(scored, 1)

                def turn(b, n, part):
                    pair = PAIRS * b + n
                    if part == 0:
                        pe.wait_ge(probs_ready, pair + 1)
                    if not (isinstance(b, int) and pair == 0 and part == 0):
                        pe.wait_ge(turned_moved, 2 * pair + part)
                    tiles = range(0, 8) if part == 0 else range(8, KEY_TILES)
                    for i, t in enumerate(tiles):
                        last = nc.tensor.transpose(turned_tiles[:, i, :], probs[n % 2][:, t * P:(t + 1) * P], core.ident[:])
                    last.then_inc(turned_ready, 1)

                def weigh(b, parity, g):
                    group = GROUPS * b + g
                    pe.wait_ge(turned_moved, 2 * GROUP_PAIRS * (group + 1))
                    if not (isinstance(b, int) and group == 0):
                        pe.wait_ge(heads_ready, group)
                    for t in range(KEY_TILES):
                        rows = P if t < KEY_TILES - 1 else LAST_KEYS
                        for p in range(GROUP_PAIRS):
                            c = (2 * HEAD_DIM * (GROUP_PAIRS * g + p)) % value_cols
                            last = nc.tensor.matmul(
                                weighed[32 * p:32 * (p + 1), 0, 0:P], v[parity][0:rows, t, c:c + 32],
                                probs_t[0:rows, t, p * P:(p + 1) * P],
                                start=t == 0, stop=t == KEY_TILES - 1, skip_group_check=True)
                    last.then_inc(weighed_ready, 1)

                def batch(b, parity, first, last):
                    for n in range(PAIRS):
                        if n == 0:
                            pe.wait_ge(blocks_ready, b + 1)
                            pe.wait_ge(projection_moved, U * b + U)
                        score(b, parity, n, 0)
                        if n == 1 and not first:
                            weigh(b - 1, 1 - parity, 1)
                        if n == GROUP_PAIRS + 1:
                            weigh(b, parity, 0)
                        if not last:
                            for u in slots[2 * n]:
                                project(b + 1, 1 - parity, u)
                        if n > 0:
                            turn(b, n - 1, 0)
                        elif not first:
                            turn(b - 1, PAIRS - 1, 0)
                        score(b, parity, n, 1)
                        if not last:
                            for u in slots[2 * n + 1]:
                                project(b + 1, 1 - parity, u)
                        if n > 0:
                            turn(b, n - 1, 1)
                        elif not first:
                            turn(b - 1, PAIRS - 1, 1)

                for u in range(U):
                    project(0, 0, u)
                over_batches(pe, batch)
                turn(BATCH - 1, PAIRS - 1, 0)
                turn(BATCH - 1, PAIRS - 1, 1)
                weigh(BATCH - 1, 1, 1)

            @block.vector
            def _(dve):
                def move_projection(b, parity, u):
                    dve.wait_ge(projection_done, U * b + u + 1)
                    if u < len(k_units):
                        g, s = k_units[u]
                        w = min(BANK, KEYS - s)
                        ins = nc.vector.tensor_scalar(k_t[parity][:, g, s:s + w], projected[:, 0, 0:w],
                                                      bk[:, g:g + 1], None, ALU.add)
                    else:
                        tiles = v_units[u - len(k_units)]
                        full = [t for t in tiles if t < KEY_TILES - 1]
                        if full:
                            n = len(full)
                            ins = nc.vector.tensor_copy(
                                v[parity][:, full[0]:full[0] + n, :],
                                projected[:, 0, 0:n * value_cols].rearrange("p (t c) -> p t c", c=value_cols))
                        if tiles[-1] == KEY_TILES - 1:
                            n = len(full)
                            ins = nc.vector.tensor_copy(v[parity][0:LAST_KEYS, KEY_TILES - 1, :],
                                                        projected[0:LAST_KEYS, 0, n * value_cols:(n + 1) * value_cols])
                    ins.then_inc(projection_moved, 1)

                def maximum(b, n, half):
                    pair = PAIRS * b + n
                    dve.wait_ge(scored, 2 * pair + half + 1)
                    cols = scores_flat[:, 0:A_COLS] if half == 0 else scores_flat[:, A_COLS:KEYS]
                    if half == 0 and not (isinstance(b, int) and pair < 2):
                        dve.wait_ge(exps_done, 2 * (pair - 1))
                    nc.vector.reduce_max(maxima[n % 2][:, half:half + 1], cols, axis=AX).then_inc(halves_maxed, 1)
                    if half == 1:
                        dve.wait_ge(halves_maxed, 2 * pair + 2)
                        nc.vector.tensor_scalar(maxima[n % 2][:, 2:3], maxima[n % 2][:, 0:1], maxima[n % 2][:, 1:2],
                                                -SCALE, ALU.max, ALU.mult).then_inc(bias_ready, 1)

                def normalise(b, n):
                    pair = PAIRS * b + n
                    s = sums[n % 2]
                    dve.wait_ge(exps_done, 2 * pair + 2)
                    nc.vector.tensor_tensor(s[:, 2:3], s[:, 0:1], s[:, 1:2], ALU.add).then_inc(sum_steps, 1)
                    dve.wait_ge(sum_steps, 2 * pair + 1)
                    nc.vector.reciprocal(s[:, 3:4], s[:, 2:3]).then_inc(sum_steps, 1)
                    dve.wait_ge(sum_steps, 2 * pair + 2)
                    nc.vector.tensor_scalar(probs[n % 2][:, 0:KEYS], probs[n % 2][:, 0:KEYS], s[:, 3:4], None,
                                            ALU.mult).then_inc(probs_ready, 1)

                def keep_heads(b, g):
                    group = GROUPS * b + g
                    dve.wait_ge(weighed_ready, group + 1)
                    nc.vector.tensor_scalar(mixed[:], weighed[:, 0, 0:SEQ], core.even_head[:], bv[:, g:g + 1],
                                            ALU.mult, ALU.add).then_inc(mixed_ready, 1)
                    dve.wait_ge(mixed_ready, group + 1)
                    nc.vector.scalar_tensor_tensor(heads_t[:, g, ds(b * SEQ, SEQ)], weighed[:, 0, SEQ:2 * SEQ],
                                                   core.odd_head[:], mixed[:], ALU.mult, ALU.add).then_inc(heads_ready, 1)

                def batch(b, parity, first, last):
                    for n in range(PAIRS):
                        maximum(b, n, 0)
                        if n == 1 and not first:
                            keep_heads(b - 1, 1)
                        if n == GROUP_PAIRS + 1:
                            keep_heads(b, 0)
                        if not last:
                            for u in slots[2 * n]:
                                move_projection(b + 1, 1 - parity, u)
                        maximum(b, n, 1)
                        if not last:
                            for u in slots[2 * n + 1]:
                                move_projection(b + 1, 1 - parity, u)
                        normalise(b, n)

                for u in range(U):
                    move_projection(0, 0, u)
                over_batches(dve, batch)
                keep_heads(BATCH - 1, 1)

            @block.scalar
            def _(act):
                def move_turned(b, n, part):
                    pair = PAIRS * b + n
                    act.wait_ge(turned_ready, 2 * pair + part + 1)
                    if n % GROUP_PAIRS == 0 and part == 0 and not (isinstance(b, int) and pair == 0):
                        act.wait_ge(weighed_ready, pair // GROUP_PAIRS if isinstance(pair, int) else GROUPS * b + n // GROUP_PAIRS)
                    t, m = (0, 8) if part == 0 else (8, KEY_TILES - 8)
                    p = n % GROUP_PAIRS
                    nc.scalar.activation(probs_t[:, t:t + m, p * P:(p + 1) * P], turned_tiles[:, 0:m, :],
                                         ACT.Copy).then_inc(turned_moved, 1)

                def exps(b, n, half):
                    pair = PAIRS * b + n
                    if half == 0:
                        act.wait_ge(bias_ready, pair + 1)
                        if not (isinstance(b, int) and pair < 2):
                            act.wait_ge(turned_ready, 2 * pair - 2)
                    lo, hi = (0, A_COLS) if half == 0 else (A_COLS, KEYS)
                    nc.scalar.activation(probs[n % 2][:, lo:hi], scores_flat[:, lo:hi], ACT.Exp,
                                         bias=maxima[n % 2][:, 2:3], scale=SCALE,
                                         accum_out=sums[n % 2][:, half:half + 1]).then_inc(exps_done, 1)

                def batch(b, parity, first, last):
                    for n in range(PAIRS):
                        if n > 0:
                            move_turned(b, n - 1, 0)
                        elif not first:
                            move_turned(b - 1, PAIRS - 1, 0)
                        exps(b, n, 0)
                        exps(b, n, 1)
                        if n > 0:
                            move_turned(b, n - 1, 1)
                        elif not first:
                            move_turned(b - 1, PAIRS - 1, 1)

                act.wait_ge(pads_zeroed, 2)
                over_batches(act, batch)
                move_turned(BATCH - 1, PAIRS - 1, 0)
                move_turned(BATCH - 1, PAIRS - 1, 1)



WIDE_HEADS, WIDE_DIM = 8, 128
WIDE_KEYS = 1024
CTX_ROWS = 96
WIDE_KEY_TILES = WIDE_KEYS // P
QUERY_TILES = 4


def wide_attention(core):
    nc, dram, x = core.nc, core.dram, core.x
    with ExitStack() as outer:
        heads_t = core.sbuf(outer, "wide_heads_t", [P, WIDE_HEADS, TOKENS])
        with ExitStack() as inner:
            xn_t = core.sbuf(inner, "wide_xn_t", [P, CHUNKS, TOKENS])
            with ExitStack() as norm:
                xn = core.sbuf(norm, "wide_xn", [P, TILES, DIM])
                norm_block(core, "wide_norm", x, xn, xn_t, True)
            wide_attention_block(core, xn_t, heads_t)
        wout = core.sbuf(outer, "wide_wout", [P, WIDE_HEADS, DIM])
        bout = core.sbuf(outer, "wide_bout", [P, DIM])
        load_block(core, "wide_out_weights", [(wout[:], dram["L0_attn_wout"]),
                                              (bout[:], dram["L0_attn_bout"].partition_broadcast(P))])
        add_bias_block(core, "wide_bias", bout)
        add_projection(core, "wide_out", heads_t, WIDE_HEADS, wout, x)


def add_bias_block(core, name, bias):
    nc, x = core.nc, core.x
    with core.block() as block:
        @block.gpsimd
        def _(pool):
            nc.gpsimd.tensor_tensor(x[:, 0:3], x[:, 0:3], bias[:].unsqueeze(1).to_broadcast([P, 3, DIM]), ALU.add)

        @block.vector
        def _(dve):
            nc.vector.tensor_tensor(x[:, 3:TILES], x[:, 3:TILES],
                                    bias[:].unsqueeze(1).to_broadcast([P, TILES - 3, DIM]), ALU.add)


def wide_attention_block(core, xn_t, heads_t):
    nc, dram = core.nc, core.dram
    SCALE = 1.5 * float(WIDE_DIM) ** -0.5
    U = 6
    WIDE_GROUPS = TILES // QUERY_TILES
    with ExitStack() as stack:
        def sb(name, shape):
            return core.sbuf(stack, f"wide_{name}", shape)

        def sem(name):
            return core.sem(stack, f"wide_{name}")

        ctx = sb("ctx", [CTX_ROWS, CHUNKS, WIDE_KEYS])
        w_q = [sb(f"w_q{i}", [P, CHUNKS, WIDE_DIM]) for i in range(2)]
        w_k = [sb(f"w_k{i}", [CTX_ROWS, CHUNKS, WIDE_DIM]) for i in range(2)]
        w_v = [sb(f"w_v{i}", [CTX_ROWS, CHUNKS, WIDE_DIM]) for i in range(2)]
        q_t = [sb(f"q_t{i}", [P, TOKENS]) for i in range(2)]
        k_t = [sb(f"k_t{i}", [P, WIDE_KEYS]) for i in range(2)]
        v = [sb(f"v{i}", [P, WIDE_KEY_TILES, WIDE_DIM]) for i in range(2)]
        probs = [sb(f"probs{i}", [P, WIDE_KEYS]) for i in range(2)]
        probs_t = [sb(f"probs_t{i}", [P, WIDE_KEY_TILES, BANK]) for i in range(2)]
        stats = [sb(f"stats{i}", [P, 4]) for i in range(2)]
        scores = [core.banks(stack, f"wide_scores{i}", 2) for i in range(2)]
        turned = core.banks(stack, "wide_turned", 2)
        projected = core.banks(stack, "wide_projected", 1)
        weighed = core.banks(stack, "wide_weighed", 1)

        ctx_loaded = sem("ctx_loaded")
        weights_loaded = [sem(f"weights_loaded{i}") for i in range(2)]
        projection_done = sem("projection_done")
        projection_moved = sem("projection_moved")
        scored = sem("scored")
        maximum_ready = sem("maximum_ready")
        bias_ready = sem("bias_ready")
        exp_done = sem("exp_done")
        inverse_ready = sem("inverse_ready")
        probs_ready = sem("probs_ready")
        turned_ready = sem("turned_ready")
        turned_moved = sem("turned_moved")
        weighed_ready = sem("weighed_ready")
        heads_ready = sem("heads_ready")

        def over_heads(eng, body):
            body(0, 0, True, False)
            body(1, 1, False, False)
            with eng.Fori(1, WIDE_HEADS // 2 - 1) as j:
                body(2 * j, 0, False, False)
                body(2 * j + 1, 1, False, False)
            body(WIDE_HEADS - 2, 0, False, False)
            body(WIDE_HEADS - 1, 1, False, True)

        with core.block() as block:
            @block.sync
            def _(sp):
                def load(h, parity):
                    for tile, name in ((w_q, "L0_attn_wq"), (w_k, "L0_attn_wk"), (w_v, "L0_attn_wv")):
                        sp.dma_start(tile[parity][:], dram[name][ds(h, 1)].rearrange("o p c n -> (o p) c n")).then_inc(weights_loaded[parity], 16)

                load(0, 0)
                sp.dma_start(ctx[:], dram["L0_attn_ctx_t"]).then_inc(ctx_loaded, 16)
                load(1, 1)
                with sp.Fori(0, WIDE_HEADS // 2 - 1) as j:
                    for parity in range(2):
                        used = sp.snap(U * (2 * j + parity + 1))
                        sp.wait_ge(projection_done, used)
                        load(2 * j + parity + 2, parity)

            @block.tensor
            def _(pe):
                def project(h, parity, u):
                    if u == 0:
                        pe.wait_ge(weights_loaded[parity], 24 * (h - parity) + 48)
                    if not (isinstance(h, int) and U * h + u == 0):
                        pe.wait_ge(projection_moved, U * h + u)
                    for k in range(CHUNKS):
                        if u < 2:
                            last = nc.tensor.matmul(projected[:, 0, :], w_q[parity][:, k, :],
                                                    xn_t[:, k, u * BANK:(u + 1) * BANK], start=k == 0, stop=k == 1)
                        elif u < 4:
                            last = nc.tensor.matmul(projected[:, 0, :], w_k[parity][:, k, :],
                                                    ctx[:, k, (u - 2) * BANK:(u - 1) * BANK], start=k == 0, stop=k == 1)
                    if u >= 4:
                        for i in range(4):
                            t = 4 * (u - 4) + i
                            for k in range(CHUNKS):
                                last = nc.tensor.matmul(projected[:, 0, i * P:(i + 1) * P], ctx[:, k, t * P:(t + 1) * P],
                                                        w_v[parity][:, k, :], start=k == 0, stop=k == 1)
                    last.then_inc(projection_done, 1)

                def score(h, parity, t):
                    n = TILES * h + t
                    if not (isinstance(h, int) and n < 2):
                        pe.wait_ge(exp_done, n - 1)
                    for s in range(HALVES):
                        last = nc.tensor.matmul(scores[t % 2][:, s, :], q_t[parity][:, t * P:(t + 1) * P],
                                                k_t[parity][:, s * BANK:(s + 1) * BANK], start=True, stop=True)
                    last.then_inc(scored, 1)

                def turn(h, t):
                    n = TILES * h + t
                    pe.wait_ge(probs_ready, n + 1)
                    if not (isinstance(h, int) and n == 0):
                        pe.wait_ge(turned_moved, n)
                    for i in range(WIDE_KEY_TILES):
                        last = nc.tensor.transpose(turned[:, i // 4, (i % 4) * P:(i % 4 + 1) * P],
                                                   probs[t % 2][:, i * P:(i + 1) * P], core.ident[:])
                    last.then_inc(turned_ready, 1)

                def weigh(h, parity, g):
                    group = WIDE_GROUPS * h + g
                    pe.wait_ge(turned_moved, QUERY_TILES * (group + 1))
                    if not (isinstance(h, int) and group == 0):
                        pe.wait_ge(heads_ready, group)
                    for i in range(WIDE_KEY_TILES):
                        last = nc.tensor.matmul(weighed[:, 0, :], v[parity][:, i, :], probs_t[g][:, i, :],
                                                start=i == 0, stop=i == WIDE_KEY_TILES - 1)
                    last.then_inc(weighed_ready, 1)

                def head(h, parity, first, last):
                    pe.wait_ge(projection_moved, U * h + U)
                    for t in range(TILES):
                        score(h, parity, t)
                        if t == 1 and not first:
                            weigh(h - 1, 1 - parity, 1)
                        if t == QUERY_TILES + 1:
                            weigh(h, parity, 0)
                        if not last and 2 <= t:
                            project(h + 1, 1 - parity, t - 2)
                        if t > 0:
                            turn(h, t - 1)
                        elif not first:
                            turn(h - 1, TILES - 1)

                pe.wait_ge(ctx_loaded, 16)
                for u in range(U):
                    project(0, 0, u)
                over_heads(pe, head)
                turn(WIDE_HEADS - 1, TILES - 1)
                weigh(WIDE_HEADS - 1, 1, 1)

            @block.vector
            def _(dve):
                def move_projection(h, parity, u):
                    dve.wait_ge(projection_done, U * h + u + 1)
                    if u < 2:
                        out = q_t[parity][:, u * BANK:(u + 1) * BANK]
                    elif u < 4:
                        out = k_t[parity][:, (u - 2) * BANK:(u - 1) * BANK]
                    else:
                        out = v[parity][:, 4 * (u - 4):4 * (u - 3), :].rearrange("p t d -> p (t d)")
                    nc.vector.tensor_copy(out, projected[:, 0, :]).then_inc(projection_moved, 1)

                def maximum(h, t):
                    n = TILES * h + t
                    dve.wait_ge(scored, n + 1)
                    nc.vector.reduce_max(stats[t % 2][:, 0:1], scores[t % 2][:].rearrange("p b n -> p (b n)"),
                                         axis=AX).then_inc(maximum_ready, 1)
                    if not (isinstance(h, int) and n < 2):
                        dve.wait_ge(exp_done, n - 1)
                    dve.wait_ge(maximum_ready, n + 1)
                    nc.vector.tensor_scalar(stats[t % 2][:, 1:2], stats[t % 2][:, 0:1], -SCALE, None,
                                            ALU.mult).then_inc(bias_ready, 1)

                def normalise(h, t):
                    n = TILES * h + t
                    dve.wait_ge(exp_done, n + 1)
                    nc.vector.reciprocal(stats[t % 2][:, 3:4], stats[t % 2][:, 2:3]).then_inc(inverse_ready, 1)
                    dve.wait_ge(inverse_ready, n + 1)
                    nc.vector.tensor_scalar(probs[t % 2][:], probs[t % 2][:], stats[t % 2][:, 3:4], None,
                                            ALU.mult).then_inc(probs_ready, 1)

                def keep_heads(h, g):
                    dve.wait_ge(weighed_ready, WIDE_GROUPS * h + g + 1)
                    nc.vector.tensor_copy(heads_t[:, ds(h, 1), g * BANK:(g + 1) * BANK].rearrange("p o n -> p (o n)"),
                                          weighed[:, 0, :]).then_inc(heads_ready, 1)

                def head(h, parity, first, last):
                    for t in range(TILES):
                        maximum(h, t)
                        if t == 1 and not first:
                            keep_heads(h - 1, 1)
                        if t == QUERY_TILES + 1:
                            keep_heads(h, 0)
                        normalise(h, t)
                        if not last and 2 <= t:
                            move_projection(h + 1, 1 - parity, t - 2)

                for u in range(U):
                    move_projection(0, 0, u)
                over_heads(dve, head)
                keep_heads(WIDE_HEADS - 1, 1)

            @block.scalar
            def _(act):
                def move_turned(h, t):
                    n = TILES * h + t
                    act.wait_ge(turned_ready, n + 1)
                    group = WIDE_GROUPS * h + t // QUERY_TILES
                    if t % QUERY_TILES == 0 and not (isinstance(h, int) and group < 2):
                        act.wait_ge(weighed_ready, group - 1)
                    q = t % QUERY_TILES
                    nc.scalar.activation(probs_t[t // QUERY_TILES][:, :, q * P:(q + 1) * P],
                                         turned[:].rearrange("p b (t n) -> p (b t) n", n=P), ACT.Copy).then_inc(turned_moved, 1)

                def head(h, parity, first, last):
                    for t in range(TILES):
                        n = TILES * h + t
                        act.wait_ge(bias_ready, n + 1)
                        if not (isinstance(h, int) and n < 2):
                            act.wait_ge(turned_ready, n - 1)
                        nc.scalar.activation(probs[t % 2][:], scores[t % 2][:].rearrange("p b n -> p (b n)"), ACT.Exp,
                                             bias=stats[t % 2][:, 1:2], scale=SCALE,
                                             accum_out=stats[t % 2][:, 2:3]).then_inc(exp_done, 1)
                        if t > 0:
                            move_turned(h, t - 1)
                        elif not first:
                            move_turned(h - 1, TILES - 1)

                over_heads(act, head)
                move_turned(WIDE_HEADS - 1, TILES - 1)



TASKS = 8
PARTS = TASKS + 1
HIDDEN = 1024
HIDDEN_TILES = HIDDEN // P


def merged_ffn(core):
    nc, dram, x = core.nc, core.dram, core.x
    with ExitStack() as outer:
        def sb(stack, name, shape):
            return core.sbuf(stack, f"ffn_{name}", shape)

        gates_by_token = sb(outer, "gates_by_token", [P, TILES, PARTS])
        gates_by_task = sb(outer, "gates_by_task", [TASKS, TOKENS])
        hidden_t = sb(outer, "hidden_t", [P, HIDDEN_TILES, TOKENS])
        with ExitStack() as inner:
            xn_t = sb(inner, "xn_t", [P, CHUNKS, TOKENS])
            scaled_t = sb(inner, "scaled_t", [P, TASKS, CHUNKS, TOKENS])
            with ExitStack() as norm:
                xn = sb(norm, "xn", [P, TILES, DIM])
                gw1, gb1 = sb(norm, "gw1", [P, CHUNKS, DIM]), sb(norm, "gb1", [P, CHUNKS])
                gw2, gw2_wide = sb(norm, "gw2", [P, CHUNKS, TASKS]), sb(norm, "gw2_wide", [P, CHUNKS, TASKS, P])
                gb2, gb2_column = sb(norm, "gb2", [P, TASKS]), sb(norm, "gb2_column", [TASKS, 1])
                b2 = sb(norm, "b2", [P, DIM])
                gate_t = sb(norm, "gate_t", [P, CHUNKS, TOKENS])
                load_block(core, "ffn_gate_weights", [
                    (gw1[:], dram["gate_w1"]), (gb1[:], dram["gate_b1"]), (gw2[:], dram["gate_w2"]),
                    (gw2_wide[:], dram["gate_w2_wide"]), (gb2[:], dram["gate_b2"].partition_broadcast(P)),
                    (gb2_column[:], dram["gate_b2"].unsqueeze(1)), (b2[:], dram["ffn_b2"].partition_broadcast(P))])
                norm_block(core, "ffn_norm", x, xn, xn_t, True)
                add_bias_block(core, "ffn_bias", b2)
                project_feature_major(core, "ffn_gate", [(gw1, CHUNKS, xn_t, gate_t, gb1, True)])
                gates_block(core, gate_t, gw2, gw2_wide, gb2, gb2_column, xn_t, gates_by_token, gates_by_task, scaled_t)
            merged_up_block(core, xn_t, scaled_t, gates_by_task, hidden_t)
        merged_down_block(core, hidden_t, gates_by_token, gates_by_task)


def gates_block(core, gate_t, gw2, gw2_wide, gb2, gb2_column, xn_t, gates_by_token, gates_by_task, scaled_t):
    nc = core.nc
    with ExitStack() as stack:
        mean = core.sbuf(stack, "gates_mean", [P, CHUNKS, BATCH])
        mean_tokens = core.sbuf(stack, "gates_mean_tokens", [P, CHUNKS, TOKENS])
        gates_wide = core.sbuf(stack, "gates_wide", [P, TASKS, BATCH])
        by_token = core.banks(stack, "gates_by_token_psum", 1)
        by_task = core.banks(stack, "gates_by_task_psum", 2)
        wide = core.banks(stack, "gates_wide_psum", 1)
        own_step = core.sem(stack, "gates_own_step")
        mean_ready = core.sem(stack, "gates_mean_ready")
        products_ready = core.sem(stack, "gates_products_ready")
        wide_ready = core.sem(stack, "gates_wide_ready")
        DVE_TASKS = 5
        with core.block() as block:
            def scale_rows(eng, e):
                return eng.tensor_tensor(
                    scaled_t[:, e].rearrange("p c (b s) -> p c b s", s=SEQ),
                    xn_t[:].rearrange("p c (b s) -> p c b s", s=SEQ),
                    gates_wide[:, e].unsqueeze(1).unsqueeze(3).to_broadcast([P, CHUNKS, BATCH, SEQ]), ALU.mult)

            @block.vector
            def _(dve):
                nc.vector.reduce_sum(mean[:].rearrange("p c b -> p (c b)"),
                                     gate_t[:].rearrange("p c (b s) -> p (c b) s", s=SEQ), axis=AX).then_inc(own_step, 1)
                dve.wait_ge(own_step, 1)
                nc.vector.tensor_scalar(mean[:], mean[:], 1.0 / SEQ, None, ALU.mult).then_inc(own_step, 1)
                dve.wait_ge(own_step, 2)
                nc.vector.tensor_copy(mean_tokens[:].rearrange("p c (b s) -> p (c b) s", s=SEQ),
                                      mean[:].rearrange("p c b -> p (c b)").unsqueeze(2).to_broadcast([P, CHUNKS * BATCH, SEQ])).then_inc(mean_ready, 1)
                nc.vector.memset(gates_by_token[:, :, 0], 1.0)
                dve.wait_ge(products_ready, 1)
                nc.vector.tensor_tensor(gates_wide[:], wide[:, 0, 0:TASKS * BATCH].rearrange("p (e b) -> p e b", b=BATCH),
                                        gb2[:].unsqueeze(2).to_broadcast([P, TASKS, BATCH]), ALU.add).then_inc(wide_ready, 1)
                dve.wait_ge(products_ready, 3)
                nc.vector.tensor_tensor(gates_by_token[:, :, 1:PARTS], by_token[:, 0, 0:TILES * TASKS].rearrange("p (t e) -> p t e", e=TASKS),
                                        gb2[:].unsqueeze(1).to_broadcast([P, TILES, TASKS]), ALU.add)
                nc.vector.tensor_scalar(gates_by_task[:].rearrange("p (b n) -> p b n", b=HALVES), by_task[0:TASKS],
                                        gb2_column[:], None, ALU.add)
                dve.wait_ge(wide_ready, 1)
                for e in range(DVE_TASKS):
                    scale_rows(nc.vector, e)

            @block.gpsimd
            def _(pool):
                pool.wait_ge(wide_ready, 1)
                for e in range(DVE_TASKS, TASKS):
                    scale_rows(nc.gpsimd, e)

            @block.tensor
            def _(pe):
                pe.wait_ge(mean_ready, 1)
                for e in range(TASKS):
                    for k in range(CHUNKS):
                        last = nc.tensor.matmul(wide[:, 0, e * BATCH:(e + 1) * BATCH], gw2_wide[:, k, e, :], mean[:, k, :],
                                                start=k == 0, stop=k == CHUNKS - 1)
                last.then_inc(products_ready, 1)
                for t in range(TILES):
                    for k in range(CHUNKS):
                        last = nc.tensor.matmul(by_token[:, 0, t * TASKS:(t + 1) * TASKS], mean_tokens[:, k, t * P:(t + 1) * P],
                                                gw2[:, k, :], start=k == 0, stop=k == CHUNKS - 1)
                last.then_inc(products_ready, 1)
                for h in range(HALVES):
                    for k in range(CHUNKS):
                        last = nc.tensor.matmul(by_task[0:TASKS, h, :], gw2[:, k, :], mean_tokens[:, k, h * BANK:(h + 1) * BANK],
                                                start=k == 0, stop=k == CHUNKS - 1)
                last.then_inc(products_ready, 1)


def merged_up_block(core, xn_t, scaled_t, gates_by_task, hidden_t):
    nc, dram = core.nc, core.dram
    with ExitStack() as stack:
        slab = [core.sbuf(stack, f"up_slab{i}", [P, PARTS, CHUNKS, P]) for i in range(2)]
        task_bias = [core.sbuf(stack, f"up_task_bias{i}", [TASKS, P]) for i in range(2)]
        b1 = core.sbuf(stack, "up_b1", [P, HIDDEN_TILES])
        psum = [core.banks(stack, f"up_psum{i}", HALVES) for i in range(2)]
        b1_loaded = core.sem(stack, "up_b1_loaded")
        slab_loaded = [core.sem(stack, f"up_slab_loaded{i}") for i in range(2)]
        product_ready = core.sem(stack, "up_product_ready")
        hidden_ready = core.sem(stack, "up_hidden_ready")
        with core.block() as block:
            @block.sync
            def _(sp):
                def load(m, parity):
                    sp.dma_start(slab[parity][:], dram["ffn_w1"][ds(m, 1)].rearrange("o p e c n -> (o p) e c n")).then_inc(slab_loaded[parity], 16)
                    sp.dma_start(task_bias[parity][:], dram["ffn_tb1"][ds(m, 1)].rearrange("o e n -> (o e) n")).then_inc(slab_loaded[parity], 16)

                sp.dma_start(b1[:], dram["ffn_b1"]).then_inc(b1_loaded, 16)
                load(0, 0)
                load(1, 1)
                with sp.Fori(0, HIDDEN_TILES // 2 - 1) as j:
                    for parity in range(2):
                        used = sp.snap(HALVES * (2 * j + parity + 1))
                        sp.wait_ge(product_ready, used)
                        load(2 * j + parity + 2, parity)

            @block.tensor
            def _(pe):
                def tile(m, parity, first):
                    pe.wait_ge(slab_loaded[parity], 16 * (m - parity) + 32)
                    for h in range(HALVES):
                        if not first:
                            pe.wait_ge(hidden_ready, HALVES * (m - 2) + h + 1)
                        cols = slice(h * BANK, (h + 1) * BANK)
                        nc.tensor.matmul(psum[parity][:, h, :], task_bias[parity][:], gates_by_task[:, cols],
                                         start=True, stop=False)
                        for e in range(PARTS):
                            for k in range(CHUNKS):
                                rows = xn_t[:, k, cols] if e == 0 else scaled_t[:, e - 1, k, cols]
                                last = nc.tensor.matmul(psum[parity][:, h, :], slab[parity][:, e, k, :], rows,
                                                        start=False, stop=e == PARTS - 1 and k == CHUNKS - 1)
                        last.then_inc(product_ready, 1)

                tile(0, 0, True)
                tile(1, 1, True)
                with pe.Fori(1, HIDDEN_TILES // 2) as j:
                    tile(2 * j, 0, False)
                    tile(2 * j + 1, 1, False)

            @block.scalar
            def _(act):
                act.wait_ge(b1_loaded, 16)
                with act.Fori(0, HIDDEN_TILES // 2) as j:
                    for parity in range(2):
                        m = 2 * j + parity
                        for h in range(HALVES):
                            act.wait_ge(product_ready, HALVES * m + h + 1)
                            nc.scalar.activation(hidden_t[:, ds(m, 1), h * BANK:(h + 1) * BANK].rearrange("p o n -> p (o n)"),
                                                 psum[parity][:, h, :], ACT.Gelu_apprx_tanh,
                                                 bias=b1[:, ds(m, 1)]).then_inc(hidden_ready, 1)


def merged_down_block(core, hidden_t, gates_by_token, gates_by_task):
    nc, dram, x = core.nc, core.dram, core.x
    with ExitStack() as stack:
        slab = [core.sbuf(stack, f"down_slab{i}", [P, HIDDEN_TILES, DIM]) for i in range(2)]
        tb2 = core.sbuf(stack, "down_tb2", [TASKS, DIM])
        psum = core.banks(stack, "down_psum", TILES)
        tb2_loaded = core.sem(stack, "down_tb2_loaded")
        slab_loaded = [core.sem(stack, f"down_slab_loaded{i}") for i in range(2)]
        product_ready = core.sem(stack, "down_product_ready")
        added = core.sem(stack, "down_added")
        with core.block() as block:
            @block.sync
            def _(sp):
                def load(e, parity):
                    sp.dma_start(slab[parity][:], dram["ffn_w2"][ds(e, 1)].rearrange("o p k n -> (o p) k n")).then_inc(slab_loaded[parity], 16)

                sp.dma_start(tb2[:], dram["ffn_tb2"]).then_inc(tb2_loaded, 16)
                load(0, 0)
                load(1, 1)
                with sp.Fori(0, PARTS // 2 - 1) as j:
                    for parity in range(2):
                        used = sp.snap(TILES * (2 * j + parity + 1))
                        sp.wait_ge(product_ready, used)
                        load(2 * j + parity + 2, parity)
                sp.wait_ge(product_ready, TILES * (PARTS - 2))
                load(PARTS - 1, 0)

            @block.tensor
            def _(pe):
                def part(e, parity, first):
                    pe.wait_ge(slab_loaded[parity], 8 * (e - parity) + 16)
                    for t in range(TILES):
                        if not first:
                            pe.wait_ge(added, TILES * (e - 1) + t + 1)
                        for k in range(HIDDEN_TILES):
                            last = nc.tensor.matmul(psum[:, t, 0:DIM], hidden_t[:, k, t * P:(t + 1) * P], slab[parity][:, k, :],
                                                    start=k == 0, stop=k == HIDDEN_TILES - 1 and not first)
                        if first:
                            last = nc.tensor.matmul(psum[:, t, 0:DIM], gates_by_task[:, t * P:(t + 1) * P], tb2[:],
                                                    start=False, stop=True)
                        last.then_inc(product_ready, 1)

                pe.wait_ge(tb2_loaded, 16)
                part(0, 0, True)
                with pe.Fori(0, PARTS // 2) as j:
                    part(2 * j + 1, 1, False)
                    part(2 * j + 2, 0, False)

            @block.vector
            def _(dve):
                def part(e, first):
                    for t in range(TILES):
                        dve.wait_ge(product_ready, TILES * e + t + 1)
                        if not first:
                            dve.wait_ge(added, TILES * (e - 1) + t + 1)
                        nc.vector.scalar_tensor_tensor(x[:, t, :], psum[:, t, 0:DIM], gates_by_token[:, t, ds(e, 1)],
                                                       x[:, t, :], ALU.mult, ALU.add).then_inc(added, 1)

                part(0, True)
                with dve.Fori(1, PARTS) as e:
                    part(e, False)



F32R = mybir.dt.float32r
SPLIT_ROWS = 4 * HEAD_DIM
CHUNKS_OF_KEYS = len(K_STARTS)


def shared_attention(core):
    nc, dram, x = core.nc, core.dram, core.x
    scratch = nc.dram_tensor("q_scratch", [2, CHUNKS, P, TOKENS], F32, kind="Internal").ap()
    with ExitStack() as outer:
        def sb(stack, name, shape, dtype=F32):
            return core.sbuf(stack, f"shared_{name}", shape, dtype)

        wo, heads_t = sb(outer, "wo", [P, CHUNKS, DIM]), sb(outer, "heads_t", [P, CHUNKS, TOKENS])
        wk, wv = sb(outer, "wk", [P, CHUNKS, SPLIT_ROWS]), sb(outer, "wv", [P, CHUNKS, HEAD_DIM])
        bk, bv = sb(outer, "bk", [SPLIT_ROWS, 1]), sb(outer, "bv", [P, 1])
        with ExitStack() as inner:
            wq, bq, bo = sb(inner, "wq", [P, CHUNKS, DIM]), sb(inner, "bq", [P, CHUNKS]), sb(inner, "bo", [P, DIM])
            xn, xn_t = sb(inner, "xn", [P, TILES, DIM]), sb(inner, "xn_t", [P, CHUNKS, TOKENS])
            q_t = sb(inner, "q_t", [P, CHUNKS, TOKENS])
            parts = [sb(inner, f"q_part{i}", [P, CHUNKS, TOKENS], F32R) for i in range(2)]
            load_block(core, "shared_weights", [
                (t[:], dram[f"L1_xattn_{n}"]) for t, n in (
                    (wq, "wq"), (wo, "wo"), (wk, "wk"), (wv, "wv"), (bq, "bq"), (bk, "bk"), (bv, "bv"))]
                + [(bo[:], dram["L1_xattn_bo"].partition_broadcast(P))])
            norm_block(core, "shared_norm", x, xn, xn_t, True)
            project_feature_major(core, "shared_q", [(wq, CHUNKS, xn_t, q_t, bq, False)])
            high_done = core.sem(inner, "shared_high_done")
            low_done = core.sem(inner, "shared_low_done")
            scratch_stored = core.sem(inner, "shared_scratch_stored")
            with core.block() as block:
                @block.vector
                def _(dve):
                    nc.vector.tensor_copy(parts[0][:], q_t[:]).then_inc(high_done, 1)
                    dve.wait_ge(high_done, 1)
                    nc.vector.tensor_tensor(parts[1][:], q_t[:], parts[0][:].bitcast(F32), ALU.subtract).then_inc(low_done, 1)

                @block.gpsimd
                def _(pool):
                    nc.gpsimd.tensor_tensor(x[:], x[:], bo[:].unsqueeze(1).to_broadcast([P, TILES, DIM]), ALU.add)

                @block.sync
                def _(sp):
                    for i, done in enumerate((high_done, low_done)):
                        sp.wait_ge(done, 1)
                        sp.dma_start(scratch[i].rearrange("c p n -> p c n"), parts[i][:].bitcast(F32)).then_inc(scratch_stored, 16)
                    sp.wait_ge(scratch_stored, 32)
        shared_attention_block(core, wk, bk, wv, bv, scratch, heads_t)
        add_projection(core, "shared_out", heads_t, CHUNKS, wo, x)


def shared_attention_block(core, wk, bk, wv, bv, scratch, heads_t):
    nc, dram = core.nc, core.dram
    SCALE = float(HEAD_DIM) ** -0.5
    RING = 4
    SCORES = PAIRS * CHUNKS_OF_KEYS
    COLUMN_TILES = 4
    TILE_COLS = HEADS * SEQ // COLUMN_TILES
    KEY_STEPS, FIRST_TURN_STEP, SECOND_TURN_STEP, VALUE_STEP = (0, 1, 3, 5), 2, 4, 6
    STEP_UNITS = {s: ("keys", c) for c, s in enumerate(KEY_STEPS)}
    STEP_UNITS.update({FIRST_TURN_STEP: ("turn", 0), SECOND_TURN_STEP: ("turn", 1), VALUE_STEP: ("values", 0)})
    SCORE_STEPS = {t: n for t, n in zip(range(1, 11), (3, 3, 3, 3, 4, 4, 3, 3, 3, 3))}
    assert sum(SCORE_STEPS.values()) == SCORES
    scores_before = {t: sum(n for s, n in SCORE_STEPS.items() if s < t) for t in SCORE_STEPS}

    with ExitStack() as stack:
        def sb(name, shape, dtype=F32):
            return core.sbuf(stack, f"shared_{name}", shape, dtype)

        def sem(name):
            return core.sem(stack, f"shared_{name}")

        ctx = [sb(f"ctx{i}", [P, CHUNKS, EVEN_KEYS]) for i in range(2)]
        k = [sb(f"k{i}", [SPLIT_ROWS + 1, EVEN_KEYS], F32R) for i in range(2)]
        q = [sb(f"q{i}", [SPLIT_ROWS + 1, HEADS, SEQ], F32R) for i in range(2)]
        v = [sb(f"v{i}", [P, KEY_TILES, 2 * HEAD_DIM]) for i in range(2)]
        exps = [sb(f"exps{i}", [P, HEADS * SEQ]) for i in range(2)]
        chunk_maxima = sb("chunk_maxima", [P, PAIRS, CHUNKS_OF_KEYS])
        maxima = sb("maxima", [P, PAIRS])
        heads = sb("heads", [P, TILE_COLS])
        inverse = sb("inverse", [P, 2, COLUMN_TILES])
        rows = sb("rows", [P, 2, COLUMN_TILES, HEAD_DIM])
        ring = core.banks(stack, "shared_ring", RING)
        scores = core.banks(stack, "shared_scores", 2)
        weighed = core.banks(stack, "shared_weighed", 1)
        common = core.banks(stack, "shared_common", 1)

        constants_ready = sem("constants_ready")
        ctx_loaded = [sem(f"ctx_loaded{i}") for i in range(2)]
        q_loaded = [sem(f"q_loaded{i}") for i in range(2)]
        keys_done = sem("keys_done")
        keys_moved = sem("keys_moved")
        keys_rounded = sem("keys_rounded")
        values_done = sem("values_done")
        values_moved = sem("values_moved")
        ring_filled = sem("ring_filled")
        ring_maxed = sem("ring_maxed")
        largest_ready = sem("largest_ready")
        maxima_ready = sem("maxima_ready")
        maxima_turned = sem("maxima_turned")
        maxima_moved = sem("maxima_moved")
        scored = sem("scored")
        exps_done = sem("exps_done")
        tile_weighed = sem("tile_weighed")
        heads_moved = sem("heads_moved")
        first_turned = sem("first_turned")
        inverse_ready = sem("inverse_ready")
        rows_ready = sem("rows_ready")
        second_turned = sem("second_turned")
        heads_ready = sem("heads_ready")

        def over_batches(eng, body):
            body(0, 0, True, False)
            body(1, 1, False, False)
            with eng.Fori(1, BATCH // 2 - 1) as j:
                body(2 * j, 0, False, False)
                body(2 * j + 1, 1, False, False)
            body(BATCH - 2, 0, False, False)
            body(BATCH - 1, 1, False, True)

        with core.block() as block:
            @block.sync
            def _(sp):
                def load_ctx(b, parity):
                    sp.dma_start(ctx[parity][:], dram["ctx_t"][ds(b, 1)].rearrange("o p c n -> (o p) c n")).then_inc(ctx_loaded[parity], 16)

                def load_q(b, parity):
                    for r in range(4):
                        sp.dma_start(q[parity][r * HEAD_DIM:(r + 1) * HEAD_DIM].bitcast(F32),
                                     scratch[r % 2].rearrange("c (h d) n -> d (c h) n", d=HEAD_DIM)[:, :, ds(b * SEQ, SEQ)]
                                     ).then_inc(q_loaded[parity], 16)

                for b in range(2):
                    load_ctx(b, b)
                    load_q(b, b)
                with sp.Fori(0, BATCH // 2 - 1) as j:
                    for parity in range(2):
                        b = 2 * j + parity
                        projected, attended = sp.snap(b + 1), sp.snap(2 * KEY_TILES * (b + 1))
                        sp.wait_ge(values_done, projected)
                        load_ctx(b + 2, parity)
                        sp.wait_ge(scored, attended)
                        load_q(b + 2, parity)

            @block.tensor
            def _(pe):
                def keys(b, parity, c):
                    if c == 0:
                        pe.wait_ge(ctx_loaded[parity], 8 * (b - parity) + 16)
                    if not (isinstance(b, int) and b == 0 and c == 0):
                        if c == 0:
                            pe.wait_ge(values_moved, b)
                        else:
                            pe.wait_ge(keys_moved, CHUNKS_OF_KEYS * b + c)
                    s = K_STARTS[c]
                    w = min(BANK, EVEN_KEYS - s)
                    for i in range(CHUNKS):
                        last = nc.tensor.matmul(common[0:SPLIT_ROWS, 0, 0:w], wk[:, i, :], ctx[parity][:, i, s:s + w],
                                                start=i == 0, stop=i == CHUNKS - 1)
                    last.then_inc(keys_done, 1)

                def values(b, parity):
                    pe.wait_ge(keys_moved, CHUNKS_OF_KEYS * (b + 1))
                    for t in range(KEY_TILES):
                        m = P if t < KEY_TILES - 1 else LAST_KEYS
                        for i in range(CHUNKS):
                            last = nc.tensor.matmul(common[0:m, 0, t * HEAD_DIM:(t + 1) * HEAD_DIM], ctx[parity][:, i, t * P:t * P + m],
                                                    wv[:, i, :], start=i == 0, stop=i == CHUNKS - 1)
                    last.then_inc(values_done, 1)

                def fill_ring(b, parity, i):
                    c, n = divmod(i, PAIRS)
                    u = SCORES * b + i
                    if n == 0:
                        pe.wait_ge(keys_moved, CHUNKS_OF_KEYS * b + c + 1)
                        if c == 0:
                            pe.wait_ge(q_loaded[parity], 32 * (b - parity) + 64)
                    if not (isinstance(b, int) and u < RING):
                        pe.wait_ge(ring_maxed, u - RING + 1)
                        if i < 2:
                            pe.wait_ge(maxima_moved, b)
                    s = K_STARTS[c]
                    w = min(BANK, EVEN_KEYS - s)
                    nc.tensor.matmul(ring[:, i % RING, 0:w],
                                     q[parity][0:SPLIT_ROWS, 2 * n:2 * n + 2, :].rearrange("r h q -> r (h q)"),
                                     k[parity][0:SPLIT_ROWS, s:s + w], start=True, stop=True).then_inc(ring_filled, 1)

                def turn_maxima(b):
                    pe.wait_ge(maxima_ready, b + 1)
                    for n in range(PAIRS):
                        last = nc.tensor.transpose(ring[0:1, n // 4, (n % 4) * P:(n % 4 + 1) * P], maxima[:, n:n + 1], core.ident[:])
                    last.then_inc(maxima_turned, 1)

                def score(b, parity, t):
                    m = P if t < KEY_TILES - 1 else LAST_KEYS
                    for h in range(2):
                        n = 2 * (KEY_TILES * b + t) + h
                        if t == 0 and h == 0:
                            pe.wait_ge(maxima_moved, b + 1)
                        if not (isinstance(b, int) and n < 2):
                            pe.wait_ge(exps_done, n - 1)
                        nc.tensor.matmul(scores[0:m, h, :], k[parity][:, t * P:t * P + m],
                                         q[parity][:, h * 8:(h + 1) * 8, :].rearrange("r h q -> r (h q)"),
                                         start=True, stop=True).then_inc(scored, 1)

                def weigh(b, parity, t):
                    m = P if t < KEY_TILES - 1 else LAST_KEYS
                    n = KEY_TILES * b + t
                    pe.wait_ge(exps_done, 2 * n + 2)
                    if t == 0:
                        pe.wait_ge(values_moved, b + 1)
                        if not (isinstance(b, int) and b == 0):
                            pe.wait_ge(heads_moved, b)
                    for c in range(COLUMN_TILES):
                        last = nc.tensor.matmul(weighed[32 * c:32 * (c + 1), 0, 0:TILE_COLS], v[parity][0:m, t, :],
                                                exps[(parity + t) % 2][0:m, c * TILE_COLS:(c + 1) * TILE_COLS],
                                                start=t == 0, stop=t == KEY_TILES - 1, skip_group_check=True)
                    last.then_inc(tile_weighed, 1)

                def first_turn(b, keys_before):
                    pe.wait_ge(heads_moved, b + 1)
                    if keys_before is not None:
                        pe.wait_ge(keys_moved, keys_before)
                    for i in range(2):
                        last = nc.tensor.transpose(common[:, 0, i * P:(i + 1) * P], heads[:, i * P:(i + 1) * P], core.ident[:])
                    last.then_inc(first_turned, 1)

                def second_turn(b, keys_before):
                    pe.wait_ge(rows_ready, b + 1)
                    if keys_before is not None:
                        pe.wait_ge(keys_moved, keys_before)
                    nc.tensor.transpose(common[:, 0, 0:P], rows[:].rearrange("p i c d -> p (i c d)"), core.ident[:]).then_inc(second_turned, 1)

                def batch(b, parity, first, last):
                    for t in range(KEY_TILES):
                        score(b, parity, t)
                        if t > 0:
                            weigh(b, parity, t - 1)
                        elif not first:
                            weigh(b - 1, 1 - parity, KEY_TILES - 1)
                        if t in SCORE_STEPS and not last:
                            for i in range(SCORE_STEPS[t]):
                                fill_ring(b + 1, 1 - parity, scores_before[t] + i)
                        what, c = STEP_UNITS.get(t, (None, None))
                        if what == "keys" and not last:
                            if c == 2 and not first:
                                pe.wait_ge(rows_ready, b)
                            if c == 3 and not first:
                                pe.wait_ge(heads_ready, b)
                            keys(b + 1, 1 - parity, c)
                        if what == "turn" and not first:
                            turned = first_turn if c == 0 else second_turn
                            turned(b - 1, None if last else CHUNKS_OF_KEYS * (b + 1) + 2 + c)
                        if what == "values" and not last:
                            values(b + 1, 1 - parity)
                        if t == KEY_TILES - 1 and not last:
                            turn_maxima(b + 1)

                pe.wait_ge(constants_ready, 6)
                for c in range(CHUNKS_OF_KEYS):
                    keys(0, 0, c)
                values(0, 0)
                for i in range(SCORES):
                    fill_ring(0, 0, i)
                turn_maxima(0)
                over_batches(pe, batch)
                weigh(BATCH - 1, 1, KEY_TILES - 1)
                first_turn(BATCH - 1, None)
                second_turn(BATCH - 1, None)

            @block.vector
            def _(dve):
                def move_keys(b, parity, c):
                    n = CHUNKS_OF_KEYS * b + c
                    s = K_STARTS[c]
                    w = min(BANK, EVEN_KEYS - s)
                    dve.wait_ge(keys_done, n + 1)
                    nc.vector.tensor_scalar(k[parity][0:SPLIT_ROWS, s:s + w], common[0:SPLIT_ROWS, 0, 0:w], bk[:], None,
                                            ALU.add).then_inc(keys_rounded, 1)
                    dve.wait_ge(keys_rounded, n + 1)
                    low = k[parity][SPLIT_ROWS // 2:SPLIT_ROWS, s:s + w]
                    nc.vector.scalar_tensor_tensor(low, common[SPLIT_ROWS // 2:SPLIT_ROWS, 0, 0:w], bk[SPLIT_ROWS // 2:, :],
                                                   low.bitcast(F32), ALU.add, ALU.subtract).then_inc(keys_moved, 1)

                def move_values(b, parity):
                    dve.wait_ge(values_done, b + 1)
                    full = KEY_TILES - 1
                    nc.vector.tensor_copy(v[parity][:, 0:full, 0:HEAD_DIM],
                                          common[:, 0, 0:full * HEAD_DIM].rearrange("p (t d) -> p t d", d=HEAD_DIM))
                    nc.vector.tensor_copy(v[parity][0:LAST_KEYS, full, 0:HEAD_DIM],
                                          common[0:LAST_KEYS, 0, full * HEAD_DIM:(full + 1) * HEAD_DIM]).then_inc(values_moved, 1)

                def take_maximum(b, i):
                    c, n = divmod(i, PAIRS)
                    dve.wait_ge(ring_filled, SCORES * b + i + 1)
                    w = min(BANK, EVEN_KEYS - K_STARTS[c])
                    nc.vector.reduce_max(chunk_maxima[:, n, c:c + 1], ring[:, i % RING, 0:w], axis=AX).then_inc(ring_maxed, 1)

                def combine_maxima(b):
                    dve.wait_ge(ring_maxed, SCORES * (b + 1))
                    if not (isinstance(b, int) and b == 0):
                        dve.wait_ge(maxima_turned, b)
                    nc.vector.reduce_max(maxima[:], chunk_maxima[:], axis=AX).then_inc(largest_ready, 1)
                    dve.wait_ge(largest_ready, b + 1)
                    nc.vector.tensor_scalar(maxima[:], maxima[:], -1.0, None, ALU.mult).then_inc(maxima_ready, 1)

                def move_heads(b):
                    dve.wait_ge(tile_weighed, KEY_TILES * (b + 1))
                    nc.vector.tensor_copy(heads[:], weighed[:, 0, 0:TILE_COLS]).then_inc(heads_moved, 1)

                def divide(b):
                    dve.wait_ge(first_turned, b + 1)
                    turned = common[:, 0, 0:2 * P].rearrange("p (i c d) -> p i c d", i=2, c=COLUMN_TILES)
                    if not (isinstance(b, int) and b == 0):
                        dve.wait_ge(second_turned, b)
                    nc.vector.reciprocal(inverse[:], turned[:, :, :, HEAD_DIM]).then_inc(inverse_ready, 1)
                    dve.wait_ge(inverse_ready, b + 1)
                    nc.vector.tensor_tensor(rows[:], turned[:, :, :, 0:HEAD_DIM],
                                            inverse[:].unsqueeze(3).to_broadcast([P, 2, COLUMN_TILES, HEAD_DIM]), ALU.mult).then_inc(rows_ready, 1)

                def keep_heads(b):
                    dve.wait_ge(second_turned, b + 1)
                    nc.vector.tensor_scalar(heads_t[:, :, ds(b * SEQ, SEQ)], common[:, 0, 0:P].rearrange("p (h q) -> p h q", h=2),
                                            bv[:], None, ALU.add).then_inc(heads_ready, 1)

                def batch(b, parity, first, last):
                    for t in range(KEY_TILES):
                        if t == 0 and not first:
                            move_heads(b - 1)
                        what, c = STEP_UNITS.get(t, (None, None))
                        if t in SCORE_STEPS and not last:
                            for i in range(SCORE_STEPS[t]):
                                take_maximum(b + 1, scores_before[t] + i)
                        if what == "keys" and not last:
                            move_keys(b + 1, 1 - parity, c)
                        if what == "turn" and not first:
                            (divide if c == 0 else keep_heads)(b - 1)
                        if what == "values" and not last:
                            move_values(b + 1, 1 - parity)
                    if not last:
                        combine_maxima(b + 1)

                for i in range(2):
                    nc.vector.memset(k[i][SPLIT_ROWS:SPLIT_ROWS + 1, :].bitcast(F32), 1.0).then_inc(constants_ready, 1)
                    nc.vector.memset(v[i][:, :, HEAD_DIM:HEAD_DIM + 1], 1.0).then_inc(constants_ready, 1)
                    nc.vector.memset(v[i][:, :, HEAD_DIM + 1:], 0.0).then_inc(constants_ready, 1)
                for c in range(CHUNKS_OF_KEYS):
                    move_keys(0, 0, c)
                move_values(0, 0)
                for i in range(SCORES):
                    take_maximum(0, i)
                combine_maxima(0)
                over_batches(dve, batch)
                move_heads(BATCH - 1)
                divide(BATCH - 1)
                keep_heads(BATCH - 1)

            @block.scalar
            def _(act):
                def move_maxima(b, parity):
                    act.wait_ge(maxima_turned, b + 1)
                    nc.scalar.activation(q[parity][SPLIT_ROWS:SPLIT_ROWS + 1].rearrange("r (o h) q -> r o (h q)", o=2),
                                         ring[0:1, 0:2, :], ACT.Copy).then_inc(maxima_moved, 1)

                def batch(b, parity, first, last):
                    for t in range(KEY_TILES):
                        m = P if t < KEY_TILES - 1 else LAST_KEYS
                        n = KEY_TILES * b + t
                        if not (isinstance(b, int) and n < 2):
                            act.wait_ge(tile_weighed, n - 1)
                        for h in range(2):
                            act.wait_ge(scored, 2 * n + h + 1)
                            nc.scalar.activation(exps[(parity + t) % 2][0:m, h * BANK:(h + 1) * BANK], scores[0:m, h, :],
                                                 ACT.Exp, scale=SCALE).then_inc(exps_done, 1)
                    if not last:
                        move_maxima(b + 1, 1 - parity)

                move_maxima(0, 0)
                over_batches(act, batch)



def value_tasks(nc, xn_t, wv, v_rows, cols=DIM):
    tasks = []
    per_unit = 4
    for b0 in range(0, BATCH, per_unit):
        products = [(lambda u, i=i: u[0:SEQ, i // 2, (i % 2) * cols:(i % 2 + 1) * cols],
                     xn_t[:, k, (b0 + i) * SEQ:(b0 + i + 1) * SEQ], wv[:, k, :], k == 0, k == CHUNKS - 1)
                    for i in range(per_unit) for k in range(CHUNKS)]

        def move(unit, step, b0=b0):
            return nc.scalar.activation(v_rows[:, b0:b0 + per_unit, :].rearrange("s (h b) c -> s h (b c)", h=2),
                                        unit[0:SEQ], ACT.Copy)

        tasks.append((products, move, "act"))
    return tasks


def self_attention_block(core, name, q_t, k_t, v_rows, bias, bv, heads_t):
    nc = core.nc
    SCALE = float(HEAD_DIM) ** -0.5
    with ExitStack() as stack:
        def sb(n, shape):
            return core.sbuf(stack, f"{name}_{n}", shape)

        def sem(n):
            return core.sem(stack, f"{name}_{n}")

        q_blocks = [sb(f"q_blocks{i}", [P, GROUPS, GROUP_HEADS, SEQ]) for i in range(2)]
        v = [sb(f"v{i}", [SEQ, DIM]) for i in range(2)]
        logits = [sb(f"logits{i}", [P, PAIRS, SEQ]) for i in range(2)]
        probs = [sb(f"probs{i}", [P, PAIRS, SEQ]) for i in range(2)]
        probs_t = sb("probs_t", [SEQ, PAIRS, P])
        maxima, sums = sb("maxima", [P, PAIRS]), sb("sums", [P, PAIRS])
        mixed = sb("mixed", [P, GROUPS, SEQ])
        scores = [core.banks(stack, f"{name}_scores{i}", 1) for i in range(2)]
        turned = core.banks(stack, f"{name}_turned", 1)
        weighed = core.banks(stack, f"{name}_weighed", 1)

        blocks_ready = sem("blocks_ready")
        values_ready = sem("values_ready")
        scored = sem("scored")
        logits_ready = sem("logits_ready")
        maxima_ready = sem("maxima_ready")
        shifted = sem("shifted")
        exp_done = sem("exp_done")
        sums_ready = sem("sums_ready")
        inverses_ready = sem("inverses_ready")
        probs_ready = sem("probs_ready")
        turned_ready = sem("turned_ready")
        turned_moved = sem("turned_moved")
        weighed_ready = sem("weighed_ready")
        mixed_ready = sem("mixed_ready")
        heads_ready = sem("heads_ready")

        with core.block() as block:
            @block.gpsimd
            def _(pool):
                def blocks(b, parity, wait):
                    if wait:
                        pool.wait_ge(scored, b - 1)
                    for g in range(GROUPS):
                        last = nc.gpsimd.tensor_tensor(
                            q_blocks[parity][:, g],
                            q_t[:, g, ds(b * SEQ, SEQ)].unsqueeze(1).to_broadcast([P, GROUP_HEADS, SEQ]),
                            core.head_mask[:].unsqueeze(2).to_broadcast([P, GROUP_HEADS, SEQ]), ALU.mult)
                    last.then_inc(blocks_ready, 1)

                def values(b, parity, wait):
                    if wait:
                        pool.wait_ge(weighed_ready, b - 1)
                    nc.gpsimd.tensor_copy(v[parity][:], v_rows[:, ds(b, 1), :].rearrange("s o c -> s (o c)")).then_inc(values_ready, 1)

                for b in range(2):
                    blocks(b, b, False)
                    values(b, b, False)
                with pool.Fori(1, BATCH // 2) as j:
                    for parity in range(2):
                        blocks(2 * j + parity, parity, True)
                        values(2 * j + parity, parity, True)

            @block.tensor
            def _(pe):
                def score(b, parity, pairs):
                    for n in pairs:
                        g, p = divmod(n, GROUP_PAIRS)
                        last = nc.tensor.matmul(scores[parity][:, 0, n * SEQ:(n + 1) * SEQ],
                                                q_blocks[parity][:, g, 2 * p:2 * p + 2, :].rearrange("p h q -> p (h q)"),
                                                k_t[:, g, ds(b * SEQ, SEQ)], start=True, stop=True)
                    if pairs[-1] == PAIRS - 1:
                        last.then_inc(scored, 1)

                def turn_and_weigh(b, parity, first, score_next):
                    pe.wait_ge(values_ready, b + 1)
                    pe.wait_ge(probs_ready, b + 1)
                    if not first:
                        pe.wait_ge(turned_moved, b)
                        pe.wait_ge(heads_ready, b)
                    for n in range(0, PAIRS, 2):
                        last = nc.tensor.transpose(turned[:, 0, n // 2 * P:(n // 2 + 1) * P],
                                                   probs[parity][:, n:n + 2, :].rearrange("p n k -> p (n k)"), core.ident[:])
                    last.then_inc(turned_ready, 1)
                    if score_next:
                        pe.wait_ge(blocks_ready, b + 3)
                        pe.wait_ge(logits_ready, b + 1)
                        score(b + 2, parity, range(0, PAIRS // 2))
                    pe.wait_ge(turned_moved, b + 1)
                    if score_next:
                        score(b + 2, parity, range(PAIRS // 2, PAIRS))
                    for n in range(PAIRS):
                        g, p = divmod(n, GROUP_PAIRS)
                        last = nc.tensor.matmul(weighed[32 * p:32 * (p + 1), 0, g * P:(g + 1) * P],
                                                v[parity][:, 32 * n:32 * (n + 1)], probs_t[:, n, :],
                                                start=True, stop=True, skip_group_check=True)
                    last.then_inc(weighed_ready, 1)

                for b in range(2):
                    pe.wait_ge(blocks_ready, b + 1)
                    score(b, b, range(PAIRS))
                turn_and_weigh(0, 0, True, True)
                turn_and_weigh(1, 1, False, True)
                with pe.Fori(1, BATCH // 2 - 1) as j:
                    turn_and_weigh(2 * j, 0, False, True)
                    turn_and_weigh(2 * j + 1, 1, False, True)
                turn_and_weigh(BATCH - 2, 0, False, False)
                turn_and_weigh(BATCH - 1, 1, False, False)

            @block.vector
            def _(dve):
                def shift(b, parity, first):
                    dve.wait_ge(scored, b + 1)
                    if not first:
                        dve.wait_ge(exp_done, b - 1)
                    nc.vector.scalar_tensor_tensor(
                        logits[parity][:].rearrange("p n k -> p (n k)"), scores[parity][:, 0, :], SCALE,
                        bias[:].rearrange("p n k -> p (n k)"), ALU.mult, ALU.add).then_inc(logits_ready, 1)
                    dve.wait_ge(logits_ready, b + 1)
                    nc.vector.reduce_max(maxima[:], logits[parity][:], axis=AX).then_inc(maxima_ready, 1)
                    dve.wait_ge(maxima_ready, b + 1)
                    nc.vector.tensor_tensor(logits[parity][:], logits[parity][:],
                                            maxima[:].unsqueeze(2).to_broadcast([P, PAIRS, SEQ]), ALU.subtract).then_inc(shifted, 1)

                def normalise(b, parity, first):
                    dve.wait_ge(exp_done, b + 1)
                    nc.vector.reduce_sum(sums[:], probs[parity][:], axis=AX).then_inc(sums_ready, 1)
                    dve.wait_ge(sums_ready, b + 1)
                    nc.vector.reciprocal(sums[:], sums[:]).then_inc(inverses_ready, 1)
                    dve.wait_ge(inverses_ready, b + 1)
                    nc.vector.tensor_tensor(probs[parity][:], probs[parity][:],
                                            sums[:].unsqueeze(2).to_broadcast([P, PAIRS, SEQ]), ALU.mult).then_inc(probs_ready, 1)

                def keep_heads(b):
                    dve.wait_ge(weighed_ready, b + 1)
                    psum = weighed[:, 0, 0:GROUPS * P].rearrange("p (g n) -> p g n", g=GROUPS)
                    if bv is None:
                        last = nc.vector.tensor_scalar(mixed[:], psum[:, :, 0:SEQ], core.even_head[:], None, ALU.mult)
                    else:
                        for g in range(GROUPS):
                            last = nc.vector.tensor_scalar(mixed[:, g], psum[:, g, 0:SEQ], core.even_head[:], bv[:, g:g + 1],
                                                           ALU.mult, ALU.add)
                    last.then_inc(mixed_ready, 1)
                    dve.wait_ge(mixed_ready, b + 1)
                    nc.vector.scalar_tensor_tensor(heads_t[:, :, ds(b * SEQ, SEQ)], psum[:, :, SEQ:2 * SEQ],
                                                   core.odd_head[:], mixed[:], ALU.mult, ALU.add).then_inc(heads_ready, 1)

                shift(0, 0, True)
                shift(1, 1, True)
                normalise(0, 0, True)
                with dve.Fori(1, BATCH // 2) as j:
                    shift(2 * j, 0, False)
                    normalise(2 * j - 1, 1, False)
                    keep_heads(2 * j - 2)
                    shift(2 * j + 1, 1, False)
                    normalise(2 * j, 0, False)
                    keep_heads(2 * j - 1)
                normalise(BATCH - 1, 1, False)
                keep_heads(BATCH - 2)
                keep_heads(BATCH - 1)

            @block.scalar
            def _(act):
                def exp(b, parity, first):
                    act.wait_ge(shifted, b + 1)
                    if not first:
                        act.wait_ge(turned_ready, b - 1)
                    nc.scalar.activation(probs[parity][:], logits[parity][:], ACT.Exp).then_inc(exp_done, 1)

                def move_turned(b, first):
                    act.wait_ge(turned_ready, b + 1)
                    if not first:
                        act.wait_ge(weighed_ready, b)
                    halves = probs_t[:].rearrange("s (n two) q -> s n two q", two=2)
                    for i in range(2):
                        last = nc.scalar.activation(halves[:, :, i, :],
                                                    turned[i * SEQ:(i + 1) * SEQ, 0, :].rearrange("s (n q) -> s n q", q=P), ACT.Copy)
                    last.then_inc(turned_moved, 1)

                exp(0, 0, True)
                exp(1, 1, True)
                move_turned(0, True)
                with act.Fori(1, BATCH // 2) as j:
                    exp(2 * j, 0, False)
                    move_turned(2 * j - 1, False)
                    exp(2 * j + 1, 1, False)
                    move_turned(2 * j, False)
                move_turned(BATCH - 1, False)


def alibi_attention(core):
    nc, dram, x = core.nc, core.dram, core.x
    with ExitStack() as stack:
        def sb(name, shape):
            return core.sbuf(stack, f"alibi_{name}", shape)

        wq, wk, wv, wo = (sb(n, [P, CHUNKS, DIM]) for n in ("wq", "wk", "wv", "wo"))
        bq, bk, bv = (sb(n, [P, CHUNKS]) for n in ("bq", "bk", "bv"))
        bo = sb("bo", [P, DIM])
        distance, slopes = sb("distance", [P, SEQ]), sb("slopes", [P, PAIRS])
        bias = sb("bias", [P, PAIRS, SEQ])
        xn, xn_t = sb("xn", [P, TILES, DIM]), sb("xn_t", [P, CHUNKS, TOKENS])
        q_t, k_t = sb("q_t", [P, CHUNKS, TOKENS]), sb("k_t", [P, CHUNKS, TOKENS])
        v_rows, heads_t = sb("v_rows", [SEQ, BATCH, DIM]), sb("heads_t", [P, CHUNKS, TOKENS])
        load_block(core, "alibi_weights",
                   [(t[:], dram[f"L1_attn_{n}"]) for t, n in ((wq, "wq"), (wk, "wk"), (wv, "wv"), (wo, "wo"), (bq, "bq"),
                                                              (bk, "bk"), (bv, "bv"), (slopes, "slopes"))]
                   + [(distance[:], dram["distance"]), (bo[:], dram["L1_attn_bo"].partition_broadcast(P))])
        with core.block() as block:
            @block.gpsimd
            def _(pool):
                nc.gpsimd.tensor_tensor(bias[:], distance[:].unsqueeze(1).to_broadcast([P, PAIRS, SEQ]),
                                        slopes[:].unsqueeze(2).to_broadcast([P, PAIRS, SEQ]), ALU.mult)
        norm_block(core, "alibi_norm", x, xn, xn_t, True)
        add_bias_block(core, "alibi_out_bias", bo)
        project_feature_major(core, "alibi_qk", [(wq, CHUNKS, xn_t, q_t, bq, False), (wk, CHUNKS, xn_t, k_t, bk, False)])
        dense_block(core, "alibi_v", value_tasks(nc, xn_t, wv, v_rows))
        self_attention_block(core, "alibi", q_t, k_t, v_rows, bias, bv, heads_t)
        add_projection(core, "alibi_out", heads_t, CHUNKS, wo, x)



EXPERTS = 8
EXPERT_HIDDEN = 512
EXPERT_TILES = EXPERT_HIDDEN // P
LIMIT = 100.0


def rotary_tasks(core, name, stack, xn_t, weights, swapped, cos, sin, dst):
    nc = core.nc
    parts = [[core.sbuf(stack, f"{name}_part_{n}{i}", [P, BANK // SEQ, SEQ]) for n in ("cos", "sin")] for i in range(2)]
    tasks = []
    for m in range(CHUNKS):
        for h in range(HALVES):
            products = [(lambda u, i=i: u[:, i, :], w[:, k, m * P:(m + 1) * P], xn_t[:, k, h * BANK:(h + 1) * BANK],
                         k == 0, k == CHUNKS - 1) for i, w in enumerate((weights, swapped)) for k in range(CHUNKS)]

            def move(unit, step, m=m, h=h):
                views = [unit[:, i, :].rearrange("p (b s) -> p b s", s=SEQ) for i in range(2)]
                shape = [P, BANK // SEQ, SEQ]
                part_cos, part_sin = parts[h % 2]
                nc.vector.tensor_tensor(part_cos[:], views[0], cos[:].unsqueeze(1).to_broadcast(shape), ALU.mult)
                step(nc.vector.tensor_tensor(part_sin[:], views[1], sin[:].unsqueeze(1).to_broadcast(shape), ALU.mult))
                last = nc.vector.tensor_tensor(dst[:, m, h * BANK:(h + 1) * BANK].rearrange("p (b s) -> p b s", s=SEQ),
                                               part_cos[:], part_sin[:], ALU.add)
                return last

            tasks.append((products, move, "dve"))
    return tasks


def moe_layer(core):
    nc, dram, x = core.nc, core.dram, core.x
    with ExitStack() as outer:
        def sb(stack, name, shape):
            return core.sbuf(stack, f"moe_{name}", shape)

        h = sb(outer, "h", [P, TILES, DIM])
        hn_t = sb(outer, "hn_t", [P, CHUNKS, TOKENS])
        hn = sb(outer, "hn", [P, TILES, DIM])
        ln2 = sb(outer, "ln2", [P, CHUNKS])
        router = sb(outer, "router", [P, CHUNKS, EXPERTS])
        order = sb(outer, "order", [P, EXPERTS])
        with ExitStack() as inner:
            wq, wq_swapped, wk, wk_swapped, wv, wo = (
                sb(inner, n, [P, CHUNKS, DIM]) for n in ("wq", "wq_swapped", "wk", "wk_swapped", "wv", "wo"))
            ln1 = sb(inner, "ln1", [P, CHUNKS])
            cos, sin = sb(inner, "cos", [P, SEQ]), sb(inner, "sin", [P, SEQ])
            causal = sb(inner, "causal", [P, PAIRS, SEQ])
            q_t, k_t = sb(inner, "q_t", [P, CHUNKS, TOKENS]), sb(inner, "k_t", [P, CHUNKS, TOKENS])
            v_rows, heads_t = sb(inner, "v_rows", [SEQ, BATCH, DIM]), sb(inner, "heads_t", [P, CHUNKS, TOKENS])
            load_block(core, "moe_weights",
                       [(t[:], dram[f"L1_ffn_{n}"]) for t, n in (
                           (wq, "wq"), (wq_swapped, "wq_swapped"), (wk, "wk"), (wk_swapped, "wk_swapped"), (wv, "wv"),
                           (wo, "wo"), (ln1, "ln1"), (ln2, "ln2"), (router, "router"))]
                       + [(t[:], dram[n]) for t, n in ((cos, "cos"), (sin, "sin"), (causal, "causal"), (order, "order"))])
            norm_block(core, "moe_norm0", x, h, None, True)
            norm_block(core, "moe_norm1", h, hn, hn_t, False, ln1)
            dense_block(core, "moe_qk",
                        rotary_tasks(core, "moe_q", inner, hn_t, wq, wq_swapped, cos, sin, q_t)
                        + rotary_tasks(core, "moe_k", inner, hn_t, wk, wk_swapped, cos, sin, k_t))
            dense_block(core, "moe_v", value_tasks(nc, hn_t, wv, v_rows))
            self_attention_block(core, "moe_attn", q_t, k_t, v_rows, causal, None, heads_t)
            add_projection(core, "moe_out", heads_t, CHUNKS, wo, h)
        clip_block(core, h)
        norm_block(core, "moe_norm2", h, hn, hn_t, False, ln2)
        weights = sb(outer, "weights", [P, TILES, EXPERTS])
        router_block(core, hn_t, router, order, weights)
        experts_block(core, hn_t, weights, h)
        finish_block(core, h)


def clip_block(core, h):
    nc = core.nc
    with core.block() as block:
        @block.vector
        def _(dve):
            nc.vector.tensor_scalar(h[:], h[:], -LIMIT, LIMIT, ALU.max, ALU.min)


def finish_block(core, h):
    nc, x = core.nc, core.x
    with ExitStack() as stack:
        clipped = core.sem(stack, "finish_clipped")
        with core.block() as block:
            @block.vector
            def _(dve):
                nc.vector.tensor_scalar(h[:], h[:], -LIMIT, LIMIT, ALU.max, ALU.min).then_inc(clipped, 1)
                dve.wait_ge(clipped, 1)
                nc.vector.tensor_tensor(x[:], x[:], h[:], ALU.add)


def router_block(core, hn_t, router, order, weights):
    nc = core.nc
    shape = [P, TILES, EXPERTS]
    with ExitStack() as stack:
        def sb(name, s):
            return core.sbuf(stack, f"router_{name}", s)

        prob, rest, pick, key = sb("prob", shape), sb("rest", shape), sb("pick", shape), sb("key", shape)
        best = sb("best", [P, TILES])
        psum = core.banks(stack, "router_psum", 1)
        logits = psum[:, 0, 0:TILES * EXPERTS].rearrange("p (t e) -> p t e", e=EXPERTS)
        logits_ready = core.sem(stack, "router_logits_ready")
        shifted = core.sem(stack, "router_shifted")
        exp_done = core.sem(stack, "router_exp_done")
        own_step = core.sem(stack, "router_own_step")
        with core.block() as block:
            @block.tensor
            def _(pe):
                for t in range(TILES):
                    for k in range(CHUNKS):
                        last = nc.tensor.matmul(logits[:, t, :], hn_t[:, k, t * P:(t + 1) * P], router[:, k, :],
                                                start=k == 0, stop=k == CHUNKS - 1)
                last.then_inc(logits_ready, 1)

            @block.scalar
            def _(act):
                act.wait_ge(shifted, 1)
                nc.scalar.activation(prob[:], rest[:], ACT.Exp).then_inc(exp_done, 1)

            @block.vector
            def _(dve):
                steps = [0]

                def step(ins):
                    steps[0] += 1
                    ins.then_inc(own_step, 1)
                    dve.wait_ge(own_step, steps[0])

                wide = best[:].unsqueeze(2).to_broadcast(shape)
                orders = order[:].unsqueeze(1).to_broadcast(shape)
                dve.wait_ge(logits_ready, 1)
                step(nc.vector.reduce_max(best[:], logits, axis=AX))
                nc.vector.tensor_tensor(rest[:], logits, wide, ALU.subtract).then_inc(shifted, 1)
                dve.wait_ge(exp_done, 1)
                remaining = prob
                for choice in range(2):
                    step(nc.vector.reduce_max(best[:], remaining[:], axis=AX))
                    step(nc.vector.tensor_tensor(key[:], remaining[:], wide, ALU.is_equal))
                    step(nc.vector.tensor_tensor(key[:], key[:], orders, ALU.mult))
                    step(nc.vector.reduce_max(best[:], key[:], axis=AX))
                    step(nc.vector.tensor_tensor(pick[:], key[:], wide, ALU.is_equal))
                    if choice == 0:
                        step(nc.vector.scalar_tensor_tensor(
                            rest[:].rearrange("p t e -> p (t e)"), pick[:].rearrange("p t e -> p (t e)"), -2.0,
                            prob[:].rearrange("p t e -> p (t e)"), ALU.mult, ALU.add))
                        step(nc.vector.tensor_tensor(weights[:], pick[:], prob[:], ALU.mult))
                        remaining = rest
                    else:
                        step(nc.vector.tensor_tensor(key[:], pick[:], prob[:], ALU.mult))
                        step(nc.vector.tensor_tensor(weights[:], weights[:], key[:], ALU.add))
                step(nc.vector.reduce_sum(best[:], weights[:], axis=AX))
                step(nc.vector.reciprocal(best[:], best[:]))
                nc.vector.tensor_tensor(weights[:], weights[:], wide, ALU.mult)


def experts_block(core, hn_t, weights, h):
    nc, dram = core.nc, core.dram
    STEPS = EXPERT_TILES * HALVES
    assert STEPS == TILES
    with ExitStack() as stack:
        w_in = [core.sbuf(stack, f"experts_w_in{i}", [P, 2, CHUNKS, EXPERT_HIDDEN]) for i in range(2)]
        w_out = [core.sbuf(stack, f"experts_w_out{i}", [P, EXPERT_TILES, DIM]) for i in range(2)]
        hidden_t = [core.sbuf(stack, f"experts_hidden_t{i}", [P, EXPERT_TILES, TOKENS]) for i in range(2)]
        gate = [core.sbuf(stack, f"experts_gate{i}", [P, BANK]) for i in range(2)]
        ups = [core.banks(stack, f"experts_ups{i}", 2) for i in range(2)]
        downs = [core.banks(stack, f"experts_downs{i}", 1) for i in range(4)]
        in_loaded = [core.sem(stack, f"experts_in_loaded{i}") for i in range(2)]
        out_loaded = [core.sem(stack, f"experts_out_loaded{i}") for i in range(2)]
        ups_ready = core.sem(stack, "experts_ups_ready")
        gate_ready = core.sem(stack, "experts_gate_ready")
        hidden_ready = core.sem(stack, "experts_hidden_ready")
        downs_ready = core.sem(stack, "experts_downs_ready")
        added = core.sem(stack, "experts_added")

        def over_experts(eng, body):
            body(0, 0, True)
            body(1, 1, False)
            with eng.Fori(1, EXPERTS // 2) as j:
                body(2 * j, 0, False)
                body(2 * j + 1, 1, False)

        with core.block() as block:
            @block.sync
            def _(sp):
                def load_in(e, parity):
                    sp.dma_start(w_in[parity][:], dram["expert_in"][ds(e, 1)].rearrange("o p w c n -> (o p) w c n")).then_inc(in_loaded[parity], 16)

                def load_out(e, parity):
                    sp.dma_start(w_out[parity][:], dram["expert_out"][ds(e, 1)].rearrange("o p k n -> (o p) k n")).then_inc(out_loaded[parity], 16)

                for e in range(2):
                    load_in(e, e)
                    load_out(e, e)
                with sp.Fori(0, EXPERTS // 2 - 1) as j:
                    for parity in range(2):
                        used = sp.snap(STEPS * (2 * j + parity + 1))
                        sp.wait_ge(ups_ready, used)
                        load_in(2 * j + parity + 2, parity)
                        sp.wait_ge(downs_ready, used)
                        load_out(2 * j + parity + 2, parity)

            @block.tensor
            def _(pe):
                def up(e, parity, i):
                    m, half = divmod(i, HALVES)
                    n = STEPS * e + i
                    if i == 0:
                        pe.wait_ge(in_loaded[parity], 8 * (e - parity) + 16)
                    if not (isinstance(e, int) and n < 2):
                        pe.wait_ge(hidden_ready, n - 1)
                    for w in range(2):
                        for k in range(CHUNKS):
                            last = nc.tensor.matmul(ups[i % 2][:, w, :], w_in[parity][:, w, k, m * P:(m + 1) * P],
                                                    hn_t[:, k, half * BANK:(half + 1) * BANK], start=k == 0, stop=k == CHUNKS - 1)
                    last.then_inc(ups_ready, 1)

                def down(e, parity, t):
                    n = STEPS * e + t
                    if t == 0:
                        pe.wait_ge(out_loaded[parity], 8 * (e - parity) + 16)
                        pe.wait_ge(hidden_ready, STEPS * e + STEPS)
                    if not (isinstance(e, int) and n < 4):
                        pe.wait_ge(added, n - 3)
                    for k in range(EXPERT_TILES):
                        last = nc.tensor.matmul(downs[t % 4][:, 0, 0:DIM], hidden_t[parity][:, k, t * P:(t + 1) * P],
                                                w_out[parity][:, k, :], start=k == 0, stop=k == EXPERT_TILES - 1)
                    last.then_inc(downs_ready, 1)

                def expert(e, parity, first):
                    for i in range(STEPS):
                        up(e, parity, i)
                        if not first:
                            down(e - 1, 1 - parity, i)

                over_experts(pe, expert)
                for t in range(TILES):
                    down(EXPERTS - 1, 1, t)

            @block.scalar
            def _(act):
                def expert(e, parity, first):
                    for i in range(STEPS):
                        n = STEPS * e + i
                        act.wait_ge(ups_ready, n + 1)
                        if not (isinstance(e, int) and n < 2):
                            act.wait_ge(hidden_ready, n - 1)
                        nc.scalar.activation(gate[i % 2][:], ups[i % 2][:, 0, :], ACT.Silu).then_inc(gate_ready, 1)

                over_experts(act, expert)

            @block.vector
            def _(dve):
                def add(e, t):
                    dve.wait_ge(downs_ready, STEPS * e + t + 1)
                    if not isinstance(e, int) or e > 0:
                        dve.wait_ge(added, STEPS * e + t)
                    nc.vector.scalar_tensor_tensor(h[:, t, :], downs[t % 4][:, 0, 0:DIM], weights[:, t, ds(e, 1)],
                                                   h[:, t, :], ALU.mult, ALU.add).then_inc(added, 1)

                def expert(e, parity, first):
                    for i in range(STEPS):
                        m, half = divmod(i, HALVES)
                        n = STEPS * e + i
                        dve.wait_ge(gate_ready, n + 1)
                        if i == 0 and not (isinstance(e, int) and e < 2):
                            dve.wait_ge(downs_ready, STEPS * (e - 1))
                        nc.vector.tensor_tensor(hidden_t[parity][:, m, half * BANK:(half + 1) * BANK], gate[i % 2][:],
                                                ups[i % 2][:, 1, :], ALU.mult).then_inc(hidden_ready, 1)
                        if not first:
                            add(e - 1, i)

                over_experts(dve, expert)
                for t in range(TILES):
                    add(EXPERTS - 1, t)



def perceiver(nc, dram, out, first=0, last=6):
    core = Core(nc, dram)
    with ExitStack() as stack:
        core.x = core.sbuf(stack, "x", [P, TILES, DIM])
        core.ident = core.sbuf(stack, "ident", [P, P])
        core.head_mask = core.sbuf(stack, "head_mask", [P, GROUP_HEADS])
        core.even_head = core.sbuf(stack, "even_head", [P, 1])
        core.odd_head = core.sbuf(stack, "odd_head", [P, 1])
        load_block(core, "start", [(core.x[:], dram["x"]), (core.ident[:], dram["ident"]),
                                   (core.head_mask[:], dram["head_mask"]), (core.even_head[:], dram["even_head"]),
                                   (core.odd_head[:], dram["odd_head"])])
        stages = [
            lambda: cross_attention(core, "L0_xattn", 2, DIM),
            lambda: wide_attention(core),
            lambda: merged_ffn(core),
            lambda: shared_attention(core),
            lambda: alibi_attention(core),
            lambda: moe_layer(core),
        ]
        for stage in stages[first:last]:
            stage()
        store(core, out)


def store(core, out):
    nc = core.nc
    with ExitStack() as stack:
        stored = core.sem(stack, "stored")
        with core.block() as block:
            @block.sync
            def _(sp):
                sp.dma_start(out, core.x[:]).then_inc(stored, 16)
                sp.wait_ge(stored, 16)


def chunked(w, rows=P):
    k = w.shape[0]
    return w.reshape(k // rows, rows, w.shape[1]).transpose(1, 0, 2)


def column(b):
    return b.reshape(-1, P).T


def per_head(w, rows):
    return np.stack([chunked(w[:, h * WIDE_DIM:(h + 1) * WIDE_DIM], rows) for h in range(WIDE_HEADS)])


def layouts(i):
    rows = np.arange(P)
    lanes, query = rows // SEQ, rows % SEQ
    key = np.arange(SEQ)
    half_dim = HEAD_DIM // 2
    inverse = (1.0 / np.float32(10000.0) ** (np.arange(0, HEAD_DIM, 2, dtype=np.float32) / np.float32(HEAD_DIM))).astype(np.float32)
    angles = key.astype(np.float32)[None, :] * inverse[rows % half_dim][:, None]
    sign = np.where(rows % HEAD_DIM < half_dim, -1.0, 1.0).astype(np.float32)[:, None]
    swap = np.arange(DIM).reshape(HEADS, 2, half_dim)[:, ::-1].reshape(-1)
    d = {
        "x": i["x"].reshape(TILES, P, DIM).transpose(1, 0, 2),
        "ctx_t": np.concatenate([i["ctx_1024"], i["ctx_1024"][:, -1:]], 1)[:, :EVEN_KEYS].transpose(0, 2, 1).reshape(
            BATCH, CHUNKS, P, EVEN_KEYS).transpose(0, 2, 1, 3),
        "ident": np.eye(P, dtype=np.float32),
        "head_mask": (rows[:, None] // HEAD_DIM == np.arange(GROUP_HEADS)).astype(np.float32),
        "even_head": (rows[:, None] // HEAD_DIM % 2 == 0).astype(np.float32),
        "odd_head": (rows[:, None] // HEAD_DIM % 2 == 1).astype(np.float32),
        "distance": (key[None, :] - query[:, None]).astype(np.float32),
        "causal": np.broadcast_to(np.where(key[None, :] <= query[:, None], 0.0, -3.0e38).astype(np.float32)[:, None, :],
                                  (P, PAIRS, SEQ)),
        "cos": np.cos(angles).astype(np.float32),
        "sin": (np.sin(angles) * sign).astype(np.float32),
        "order": np.broadcast_to((EXPERTS - np.arange(EXPERTS)).astype(np.float32), (P, EXPERTS)),
    }
    for n in ("wq", "wk", "wv", "wo"):
        d[f"L0_xattn_{n}"] = chunked(i[f"L0_xattn_{n}"])
    for n in ("bq", "bk", "bv"):
        d[f"L0_xattn_{n}"] = column(i[f"L0_xattn_{n}"])
    d["L0_xattn_bo"] = i["L0_xattn_bo"]

    d["L0_attn_ctx_t"] = chunked(i["L0_attn_context"].reshape(WIDE_KEYS, 2 * CTX_ROWS).T, CTX_ROWS)
    d["L0_attn_wq"] = per_head(i["L0_attn_Wq"], P)
    d["L0_attn_wk"] = per_head(i["L0_attn_Wk"], CTX_ROWS)
    d["L0_attn_wv"] = per_head(i["L0_attn_Wv"], CTX_ROWS)
    d["L0_attn_wout"] = chunked(i["L0_attn_Wout"])
    d["L0_attn_bout"] = i["L0_attn_bout"]

    d["gate_w1"] = chunked(i["L0_ffn_gate_w1"].T)
    d["gate_b1"] = column(i["L0_ffn_gate_b1"])
    d["gate_w2"] = chunked(i["L0_ffn_gate_w2"].T)
    d["gate_w2_wide"] = np.broadcast_to(d["gate_w2"][:, :, :, None], (P, CHUNKS, TASKS, P))
    d["gate_b2"] = i["L0_ffn_gate_b2"]
    w1 = np.concatenate([i["L0_ffn_W1"][None], i["L0_ffn_TW1"]])
    d["ffn_w1"] = w1.reshape(PARTS, HIDDEN_TILES, P, CHUNKS, P).transpose(1, 4, 0, 3, 2)
    d["ffn_b1"] = column(i["L0_ffn_b1"])
    d["ffn_tb1"] = i["L0_ffn_Tb1"].reshape(TASKS, HIDDEN_TILES, P).transpose(1, 0, 2)
    w2 = np.concatenate([i["L0_ffn_W2"][None], i["L0_ffn_TW2"]])
    d["ffn_w2"] = w2.reshape(PARTS, DIM, HIDDEN_TILES, P).transpose(0, 3, 2, 1)
    d["ffn_b2"] = i["L0_ffn_b2"]
    d["ffn_tb2"] = i["L0_ffn_Tb2"]

    slot = np.arange(HEADS).reshape(4, 2, 2).transpose(2, 1, 0).reshape(-1)
    d["L1_xattn_wq"] = chunked(i["L1_xattn_Wq"].T)
    d["L1_xattn_wk"] = chunked(np.tile(i["L1_xattn_Wk"].T, (1, 4)))
    d["L1_xattn_wv"] = chunked(i["L1_xattn_Wv"].T)
    d["L1_xattn_wo"] = chunked(i["L1_xattn_Wo"].T.reshape(HEADS, HEAD_DIM, DIM)[slot].reshape(DIM, DIM))
    d["L1_xattn_bq"] = column(i["L1_xattn_bq"])
    d["L1_xattn_bk"] = np.tile(i["L1_xattn_bk"], 4)[:, None]
    d["L1_xattn_bv"] = np.tile(i["L1_xattn_bv"], GROUP_HEADS)[:, None]
    d["L1_xattn_bo"] = i["L1_xattn_bo"]

    for n in ("q", "k", "v", "o"):
        d[f"L1_attn_w{n}"] = chunked(i[f"L1_attn_W{n}"].T)
    for n in ("q", "k", "v"):
        d[f"L1_attn_b{n}"] = column(i[f"L1_attn_b{n}"])
    d["L1_attn_bo"] = i["L1_attn_bo"]
    d["L1_attn_slopes"] = i["L1_attn_slopes"].reshape(PAIRS, 2).T[lanes]

    repeat = np.repeat(np.arange(4), HEADS // 4)
    def spread(w):
        return w.reshape(DIM, 4, HEAD_DIM)[:, repeat].reshape(DIM, DIM)
    wq, wk, wv = i["L1_ffn_Wq"], spread(i["L1_ffn_Wk"]), spread(i["L1_ffn_Wv"])
    d["L1_ffn_wq"], d["L1_ffn_wq_swapped"] = chunked(wq), chunked(wq[:, swap])
    d["L1_ffn_wk"], d["L1_ffn_wk_swapped"] = chunked(wk), chunked(wk[:, swap])
    d["L1_ffn_wv"], d["L1_ffn_wo"] = chunked(wv), chunked(i["L1_ffn_Wo"])
    d["L1_ffn_ln1"], d["L1_ffn_ln2"] = column(i["L1_ffn_ln1_w"]), column(i["L1_ffn_ln2_w"])
    d["L1_ffn_router"] = chunked(i["L1_ffn_Wr"])
    d["expert_in"] = np.stack([i["L1_ffn_Wg"], i["L1_ffn_Wu"]], 1).reshape(
        EXPERTS, 2, CHUNKS, P, EXPERT_HIDDEN).transpose(0, 3, 1, 2, 4)
    d["expert_out"] = i["L1_ffn_Wd"].reshape(EXPERTS, EXPERT_TILES, P, DIM).transpose(0, 2, 1, 3)
    return {k: np.ascontiguousarray(v) for k, v in d.items()}


def kernel(**inputs):
    import concourse.bacc as _bacc
    from concourse.bass_utils import run_bass_kernel_spmd as _run

    arrays = {f"in_{k}": v for k, v in layouts({k: np.asarray(v) for k, v in inputs.items()}).items()}
    nc = _bacc.Bacc("TRN2", target_bir_lowering=False, num_devices=1)
    dram = {k[3:]: nc.dram_tensor(k, v.shape, mybir.dt.from_np(v.dtype), kind="ExternalInput").ap()
            for k, v in arrays.items()}
    out = nc.dram_tensor("out", [P, TILES, DIM], F32, kind="ExternalOutput").ap()
    perceiver(nc, dram, out)
    r = _run(nc, [arrays], core_ids=[0])
    got = np.asarray(r.results[0]["out"])
    return np.ascontiguousarray(got.transpose(1, 0, 2)).reshape(BATCH, SEQ, DIM)
```
